# Optimizing a Trainium2 kernel written in Bass

```python
import numpy as np
import jax
import jax.numpy as jnp

def _softmax(x, axis=-1):
    return jax.nn.softmax(x, axis=axis)

def _gelu(x):
    return jax.nn.gelu(x, approximate=True)

def _silu(x):
    return jax.nn.silu(x)

def _sigmoid(x):
    return jax.nn.sigmoid(x)

def _layernorm(x, axis=-1, eps=1e-05):
    m = jnp.mean(x, axis=axis, keepdims=True)
    v = jnp.var(x, axis=axis, keepdims=True)
    return (x - m) / jnp.sqrt(v + eps)

def _scatter_add(tgt, idx, src, axis=0):
    return tgt.at[idx].add(src)

def _segment_sum(src, seg, n):
    return jax.ops.segment_sum(src, seg, n)
kernel_name = 'mk_cond_resid_d4_seqx_r8_839646'

def setup_inputs(seed: int=0):
    np.random.seed(seed)
    _w = jnp.asarray

    def _rec_inputs():
        import jax
        import jax.numpy as jnp
        _rk = jax.random.key(seed)
        x = 7.22e-05 + 1 * jax.random.normal(jax.random.fold_in(_rk, 1), (8, 128, 512), jnp.float32)
        _lenS = 128 - jax.random.randint(jax.random.fold_in(_rk, 7), (8,), 0, max(1, 128 // 4) + 1, jnp.int32)
        _lenS2 = 128 - jax.random.randint(jax.random.fold_in(_rk, 8), (8,), 0, max(1, 128 // 4) + 1, jnp.int32)
        itok_B_2_6 = jax.random.randint(jax.random.fold_in(_rk, 11), (8,), 2, 7, jnp.int32)
        itok_Bx16_0_63 = jax.random.randint(jax.random.fold_in(_rk, 12), (8, 16), 0, 64, jnp.int32)
        itok_B_207_1644 = jax.random.randint(jax.random.fold_in(_rk, 13), (8,), 207, 1645, jnp.int32)
        condB_codebook = -0.0625 + 0.715345 * jax.random.normal(jax.random.fold_in(_rk, 14), (8,), jnp.float32)
        itok_B_3_7 = jax.random.randint(jax.random.fold_in(_rk, 15), (8,), 3, 8, jnp.int32)
        return (x, itok_B_2_6, itok_Bx16_0_63, itok_B_207_1644, condB_codebook, itok_B_3_7)
    x, itok_B_2_6, itok_Bx16_0_63, itok_B_207_1644, condB_codebook, itok_B_3_7 = _rec_inputs()

    def _L0_cond_setup():
        import jax, jax.numpy as jnp
        import numpy as np
        B, N, H, F = (4, 64, 512, 1376)
        L, R, RANK = (1, 16, 16)
        SCALE = 0.5
        key = jax.random.key(seed)
        ks = jax.random.split(key, 12)
        nrm = lambda k, shape, fan: jax.random.normal(k, shape, jnp.float32) * fan ** (-0.5)
        inp = {'x': jax.random.normal(ks[0], (B, N, H), jnp.float32), 'W_gate': nrm(ks[1], (F, H), H), 'W_up': nrm(ks[2], (F, H), H), 'W_down': nrm(ks[3], (H, F), F), 'A_gate': nrm(ks[4], (L, R, RANK, H), H), 'B_gate': nrm(ks[5], (L, R, F, RANK), RANK), 'A_up': nrm(ks[6], (L, R, RANK, H), H), 'B_up': nrm(ks[7], (L, R, F, RANK), RANK), 'A_down': nrm(ks[8], (L, R, RANK, F), F), 'B_down': nrm(ks[9], (L, R, H, RANK), RANK), 'lora_indices': jax.random.randint(ks[10], (B,), 0, R), 'layer_idx': 0}
        return inp
    _L0_cond_all = _L0_cond_setup()
    _L0_cond_in = {k: v for k, v in _L0_cond_all.items() if k in ('W_gate', 'W_up', 'W_down', 'A_gate', 'B_gate', 'A_up', 'B_up', 'A_down', 'B_down')}
    del _L0_cond_all

    def _L1_cond_setup():
        import jax, jax.numpy as jnp
        import numpy as np
        B, S, HID = (4, 128, 512)
        D, HQ, HK = (128, 32, 8)
        PAGES, PSIZE, NPP = (64, 32, 16)
        THETA = 10000.0
        EPS = 1e-06
        SCALE = 1.0 / float(np.sqrt(D))

        def _rmsnorm(t, w):
            var = jnp.mean(t * t, axis=-1, keepdims=True)
            return t * jax.lax.rsqrt(var + EPS) * w

        def _rope(t, pos):
            inv_freq = 1.0 / THETA ** (jnp.arange(0, D, 2, dtype=jnp.float32) / D)
            freqs = pos[..., None].astype(jnp.float32) * inv_freq
            cos = jnp.cos(freqs)[:, :, None, :]
            sin = jnp.sin(freqs)[:, :, None, :]
            t1, t2 = (t[..., :D // 2], t[..., D // 2:])
            return jnp.concatenate([t1 * cos - t2 * sin, t2 * cos + t1 * sin], axis=-1)
        key = jax.random.key(seed)
        ks = jax.random.split(key, 10)
        x = jax.random.normal(ks[0], (B, S, HID), jnp.float32)
        Wq = jax.random.normal(ks[1], (HQ * D, HID), jnp.float32) * 0.02
        Wk = jax.random.normal(ks[2], (HK * D, HID), jnp.float32) * 0.02
        Wv = jax.random.normal(ks[3], (HK * D, HID), jnp.float32) * 0.02
        Wo = jax.random.normal(ks[4], (HID, HQ * D), jnp.float32) * 0.02
        q_norm_w = jax.random.uniform(ks[5], (D,), jnp.float32)
        k_norm_w = jax.random.uniform(ks[6], (D,), jnp.float32)
        k_cache = jax.random.normal(ks[7], (PAGES, PSIZE, HK, D), jnp.float32)
        v_cache = jax.random.normal(ks[8], (PAGES, PSIZE, HK, D), jnp.float32)
        block_table = jnp.arange(B * NPP, dtype=jnp.int32).reshape(B, NPP)
        cache_seqlens = jax.random.randint(ks[9], (B,), 0, 475).astype(jnp.int32)
        return dict(x=x, Wq=Wq, Wk=Wk, Wv=Wv, Wo=Wo, q_norm_w=q_norm_w, k_norm_w=k_norm_w, k_cache=k_cache, v_cache=v_cache, block_table=block_table, cache_seqlens=cache_seqlens)
    _L1_cond_all = _L1_cond_setup()
    _L1_cond_in = {k: v for k, v in _L1_cond_all.items() if k in ('Wq', 'Wk', 'Wv', 'Wo', 'q_norm_w', 'k_norm_w', 'k_cache', 'v_cache')}
    del _L1_cond_all

    def _L2_cond_setup():
        import jax, jax.numpy as jnp
        import numpy as np
        GROUP = 128
        LORA_ALPHA = 32.0
        LORA_RANK = 64
        key = jax.random.key(seed)
        k1, k2, k3, k4 = jax.random.split(key, 4)
        O, I = (512, 512)
        x = jax.random.normal(k1, (4, 256, I), dtype=jnp.float32)
        weight = jax.random.normal(k2, (O, I), dtype=jnp.float32) * 0.02
        wg = weight.reshape(O, I // GROUP, GROUP)
        scale_log = jnp.log(jnp.clip(jnp.max(jnp.abs(wg), axis=2, keepdims=True), 1e-05))
        codebook = jnp.array([-1.0, -0.25, 0.0, 1.0], dtype=jnp.float32)
        lora_A = jax.random.normal(k3, (LORA_RANK, I), dtype=jnp.float32) * 0.02
        lora_B = jax.random.normal(k4, (O, LORA_RANK), dtype=jnp.float32) * 0.02
        return {'x': x, 'weight': weight, 'scale_log': scale_log, 'codebook': codebook, 'lora_A': lora_A, 'lora_B': lora_B}
    _L2_cond_all = _L2_cond_setup()
    _L2_cond_in = {k: v for k, v in _L2_cond_all.items() if k in ('weight', 'scale_log', 'lora_A', 'lora_B')}
    del _L2_cond_all

    def _L3_cond_setup():
        import jax, jax.numpy as jnp
        import numpy as np
        MAX_LORAS, OUT, IN = (8, 512, 512)
        B, S = (4, 256)
        key = jax.random.key(seed)
        k1, k2, k3 = jax.random.split(key, 3)
        x = jax.random.normal(k1, (B, S, IN), dtype=jnp.float32)
        weight = jax.random.normal(k2, (MAX_LORAS, OUT, IN), dtype=jnp.float32) * 0.02
        adapter_ids = jax.random.randint(k3, (B,), 0, MAX_LORAS, dtype=jnp.int32)
        return {'x': x, 'weight': weight, 'adapter_ids': adapter_ids}
    _L3_cond_all = _L3_cond_setup()
    _L3_cond_in = {k: v for k, v in _L3_cond_all.items() if k in ('weight',)}
    del _L3_cond_all
    return {'x': x, 'itok_B_2_6': itok_B_2_6, 'itok_Bx16_0_63': itok_Bx16_0_63, 'itok_B_207_1644': itok_B_207_1644, 'condB_codebook': condB_codebook, 'itok_B_3_7': itok_B_3_7, 'L0_cond_W_gate': _L0_cond_in['W_gate'], 'L0_cond_W_up': _L0_cond_in['W_up'], 'L0_cond_W_down': _L0_cond_in['W_down'], 'L0_cond_A_gate': _L0_cond_in['A_gate'], 'L0_cond_B_gate': _L0_cond_in['B_gate'], 'L0_cond_A_up': _L0_cond_in['A_up'], 'L0_cond_B_up': _L0_cond_in['B_up'], 'L0_cond_A_down': _L0_cond_in['A_down'], 'L0_cond_B_down': _L0_cond_in['B_down'], 'L1_cond_Wq': _L1_cond_in['Wq'], 'L1_cond_Wk': _L1_cond_in['Wk'], 'L1_cond_Wv': _L1_cond_in['Wv'], 'L1_cond_Wo': _L1_cond_in['Wo'], 'L1_cond_q_norm_w': _L1_cond_in['q_norm_w'], 'L1_cond_k_norm_w': _L1_cond_in['k_norm_w'], 'L1_cond_k_cache': _L1_cond_in['k_cache'], 'L1_cond_v_cache': _L1_cond_in['v_cache'], 'L2_cond_weight': _L2_cond_in['weight'], 'L2_cond_scale_log': _L2_cond_in['scale_log'], 'L2_cond_lora_A': _L2_cond_in['lora_A'], 'L2_cond_lora_B': _L2_cond_in['lora_B'], 'L3_cond_weight': _L3_cond_in['weight']}

def reference(x, itok_B_2_6, itok_Bx16_0_63, itok_B_207_1644, condB_codebook, itok_B_3_7, L0_cond_W_gate, L0_cond_W_up, L0_cond_W_down, L0_cond_A_gate, L0_cond_B_gate, L0_cond_A_up, L0_cond_B_up, L0_cond_A_down, L0_cond_B_down, L1_cond_Wq, L1_cond_Wk, L1_cond_Wv, L1_cond_Wo, L1_cond_q_norm_w, L1_cond_k_norm_w, L1_cond_k_cache, L1_cond_v_cache, L2_cond_weight, L2_cond_scale_log, L2_cond_lora_A, L2_cond_lora_B, L3_cond_weight):
    import jax
    import jax.numpy as jnp

    def _L0_cond_ref(x, W_gate, W_up, W_down, A_gate, B_gate, A_up, B_up, A_down, B_down, lora_indices, layer_idx):
        import jax, jax.numpy as jnp
        import numpy as np
        B, N, H, F = (4, 64, 512, 1376)
        L, R, RANK = (1, 16, 16)
        SCALE = 0.5

        def lora_add(base, inp, A, B):
            Ab = A[layer_idx][lora_indices]
            Bb = B[layer_idx][lora_indices]
            t = jnp.einsum('bri,bni->bnr', Ab, inp)
            return base + jnp.einsum('bor,bnr->bno', Bb, t) * SCALE
        gate = lora_add(jnp.einsum('bnh,fh->bnf', x, W_gate), x, A_gate, B_gate)
        up = lora_add(jnp.einsum('bnh,fh->bnf', x, W_up), x, A_up, B_up)
        act = jax.nn.silu(gate) * up
        down = lora_add(jnp.einsum('bnf,hf->bnh', act, W_down), act, A_down, B_down)
        return down

    def _L1_cond_ref(x, Wq, Wk, Wv, Wo, q_norm_w, k_norm_w, k_cache, v_cache, block_table, cache_seqlens):
        import jax, jax.numpy as jnp
        import numpy as np
        B, S, HID = (4, 128, 512)
        D, HQ, HK = (128, 32, 8)
        PAGES, PSIZE, NPP = (64, 32, 16)
        THETA = 10000.0
        EPS = 1e-06
        SCALE = 1.0 / float(np.sqrt(D))

        def _rmsnorm(t, w):
            var = jnp.mean(t * t, axis=-1, keepdims=True)
            return t * jax.lax.rsqrt(var + EPS) * w

        def _rope(t, pos):
            inv_freq = 1.0 / THETA ** (jnp.arange(0, D, 2, dtype=jnp.float32) / D)
            freqs = pos[..., None].astype(jnp.float32) * inv_freq
            cos = jnp.cos(freqs)[:, :, None, :]
            sin = jnp.sin(freqs)[:, :, None, :]
            t1, t2 = (t[..., :D // 2], t[..., D // 2:])
            return jnp.concatenate([t1 * cos - t2 * sin, t2 * cos + t1 * sin], axis=-1)
        bsz, seqlen, _ = x.shape
        q = jnp.einsum('bsd,ed->bse', x, Wq).reshape(bsz, seqlen, HQ, D)
        k = jnp.einsum('bsd,ed->bse', x, Wk).reshape(bsz, seqlen, HK, D)
        v = jnp.einsum('bsd,ed->bse', x, Wv).reshape(bsz, seqlen, HK, D)
        q = _rmsnorm(q, q_norm_w)
        k = _rmsnorm(k, k_norm_w)
        pos = cache_seqlens[:, None] + jnp.arange(seqlen)[None, :]
        q = _rope(q, pos)
        k = _rope(k, pos)
        L = NPP * PSIZE
        kc = k_cache[block_table].reshape(bsz, L, HK, D)
        vc = v_cache[block_table].reshape(bsz, L, HK, D)
        k_all = jnp.concatenate([kc, k], axis=1)
        v_all = jnp.concatenate([vc, v], axis=1)
        valid_c = jnp.arange(L)[None, :] < cache_seqlens[:, None]
        valid = jnp.concatenate([valid_c, jnp.ones((bsz, seqlen), dtype=bool)], axis=1)
        rep = HQ // HK
        k_all = jnp.repeat(k_all, rep, axis=2)
        v_all = jnp.repeat(v_all, rep, axis=2)
        scores = jnp.einsum('bqhd,bkhd->bhqk', q, k_all) * SCALE
        scores = jnp.where(valid[:, None, None, :], scores, -1e+30)
        probs = jax.nn.softmax(scores, axis=-1)
        o = jnp.einsum('bhqk,bkhd->bqhd', probs, v_all)
        o = o.reshape(bsz, seqlen, HQ * D)
        return jnp.einsum('bse,de->bsd', o, Wo)

    def _L2_cond_ref(x, weight, scale_log, codebook, lora_A, lora_B):
        import jax, jax.numpy as jnp
        import numpy as np
        GROUP = 128
        LORA_ALPHA = 32.0
        LORA_RANK = 64
        O, I = weight.shape
        lora_delta = lora_B @ lora_A * (LORA_ALPHA / LORA_RANK)
        cb = codebook / jnp.clip(jnp.max(jnp.abs(codebook)), 1e-08)
        scale = jnp.exp(scale_log)
        wg = (weight + lora_delta).reshape(O, I // GROUP, GROUP)
        normalized = wg / scale
        thresholds = (cb[:-1] + cb[1:]) * 0.5
        idx = jnp.searchsorted(thresholds, normalized, side='left')
        quantized = cb[idx]
        w = jax.lax.stop_gradient(quantized - normalized) + normalized
        w_q = (w * scale).reshape(O, I)
        w_eff = w_q + lora_delta
        return x @ w_eff.T

    def _L3_cond_ref(x, weight, adapter_ids):
        import jax, jax.numpy as jnp
        import numpy as np
        MAX_LORAS, OUT, IN = (8, 512, 512)
        B, S = (4, 256)
        w = weight[adapter_ids]
        return jnp.einsum('bsi,boi->bso', x, w)
    x = x + _L0_cond_ref(x, L0_cond_W_gate, L0_cond_W_up, L0_cond_W_down, L0_cond_A_gate, L0_cond_B_gate, L0_cond_A_up, L0_cond_B_up, L0_cond_A_down, L0_cond_B_down, itok_B_2_6, 0)
    x = x + _L1_cond_ref(x, L1_cond_Wq, L1_cond_Wk, L1_cond_Wv, L1_cond_Wo, L1_cond_q_norm_w, L1_cond_k_norm_w, L1_cond_k_cache, L1_cond_v_cache, itok_Bx16_0_63, itok_B_207_1644)
    x = x + _L2_cond_ref(x, L2_cond_weight, L2_cond_scale_log, condB_codebook, L2_cond_lora_A, L2_cond_lora_B)
    x = x + _L3_cond_ref(x, L3_cond_weight, itok_B_3_7)
    return x

_drawn_inputs = setup_inputs


def setup_inputs(seed=0):
    import zlib

    import numpy as np

    out = dict(_drawn_inputs(seed))
    spreads = {}
    factors = {'L1_cond_Wk': 24.235,
     'L1_cond_Wv': 29.748,
     'L1_cond_q_norm_w': 4.391,
     'L1_cond_k_norm_w': 25.164,
     'L1_cond_k_cache': 8.0,
     'L1_cond_v_cache': 8.0}
    for name, (base, spread) in spreads.items():
        noise = np.random.default_rng([zlib.crc32(name.encode()), seed]).standard_normal(out[name].shape)
        drawn = base * np.exp(spread * noise) if base else spread * noise
        out[name] = jnp.asarray(drawn.astype(out[name].dtype))
    for name, factor in factors.items():
        out[name] = (out[name] * factor).astype(out[name].dtype)
    return out
```

```python
from contextlib import ExitStack

import numpy as np

import concourse.bass as bass
from concourse import mybir

F32 = mybir.dt.float32
F32R = mybir.dt.float32r
BF16 = mybir.dt.bfloat16
I32 = mybir.dt.int32
ALU = mybir.AluOpType
ACT = mybir.ActivationFunctionType
AX_X = mybir.AxisListType.X

P = 128
B, T, HID = 8, 128, 512
C = HID // P
F = 1376
FC = 11
FTAIL = F - (FC - 1) * P
RANK = 16
HALF = 4
HT = HALF * T
LR = HALF * RANK
D, HQ, HK = 128, 32, 8
REP = HQ // HK
NPP, PSIZE = 16, 32
L = NPP * PSIZE
LC = L // P
KEYS = L + T
KC = KEYS // P
SPLIT = KEYS // 2
QW = REP * D
QKV = QW + 2 * D
UNITS = HK * B
LORA2 = 64
NCODE = 8
EPS = 1e-06
SCALE = 1.0 / float(np.sqrt(D))
NEG = -1e30
TWO_PI = 6.283185307179586
PI_A = 6.28125
PI_B = float(np.float32(TWO_PI - PI_A).view(np.uint32) & np.uint32(0xFFFFF000))
PI_B = float(np.uint32(PI_B).view(np.float32))
PI_C = float(np.float32(TWO_PI - PI_A - PI_B))
ROUND = 12582912.0
PI_IN = 3.1415925
LOWEST = -3.0e38


class Unit:

    def __init__(self, turn, k):
        self.turn, self.k = turn, k

    def __add__(self, n):
        return Unit(self.turn, self.k + n)

    def exists(self):
        return self.turn is not None or 0 <= self.k < UNITS

    @property
    def seq(self):
        return self.k % B

    @property
    def head(self):
        return self.k // B if self.turn is None else self.turn + self.k // B

    def count(self, per, n):
        return self.k * per + n if self.turn is None else self.turn * (B * per) + (self.k * per + n)

    def heads(self, per, n):
        return (self.k // B) * per + n if self.turn is None else self.turn * per + ((self.k // B) * per + n)


def run_steps(engine, step):
    for k in (-1, 0, 1):
        step(Unit(None, k))
    with engine.Fori(0, HK - 1) as turn:
        for k in range(2, 2 + B):
            step(Unit(turn, k))
    for k in range(UNITS - B + 2, UNITS + 2):
        step(Unit(None, k))


def staged(u, kind, c):
    n = c // 2 + 1 + (2 if kind == "out" else 0)
    return u.heads(4 * 16, 16 * n)


def rows(m):
    return P if m < FC - 1 else FTAIL


def cond_resid_kernel(nc, ins, out):
    ctx = ExitStack()
    with ctx:
        def dram(name, shape):
            return nc.dram_tensor(name, shape, F32, kind="Internal").ap()

        def sem(name):
            return ctx.enter_context(nc.semaphore(name))

        def keep(name, shape, dt=F32):
            return ctx.enter_context(nc.sbuf_tensor(name, shape, dt))

        k_pages = dram("k_pages", (B, L, HK, D))
        v_pages = dram("v_pages", (B, L, HK, D))
        w2_dram = dram("w2_dram", (P, C, HID))

        sc0 = ctx.enter_context(nc.psum_tensor("sc0", [P, 2, 512], F32))
        sc1 = ctx.enter_context(nc.psum_tensor("sc1", [P, 2, 512], F32))
        ring0 = ctx.enter_context(nc.psum_tensor("ring0", [P, 512], F32))
        ring1 = ctx.enter_context(nc.psum_tensor("ring1", [P, 512], F32))
        o_ps = ctx.enter_context(nc.psum_tensor("o_ps", [P, 512], F32))
        proj_ps = ctx.enter_context(nc.psum_tensor("proj_ps", [P, 512], F32))
        score_ps = [sc0, sc1]
        ring = [ring0, ring1]
        gate_ps = [sc0[:, 0, :], sc0[:, 1, :]]
        up_ps = [sc1[:, 0, :], sc1[:, 1, :]]
        down_ps = [o_ps[:, :], proj_ps[:, :]]

        x_sb = keep("x_sb", [P, B, HID])
        rope_tab = keep("rope_tab", [P, 4, B, D])
        mask = keep("mask", [P, B, KEYS], BF16)
        ident = keep("ident", [P, P])
        half_neg = keep("half_neg", [P, 8])
        idx = keep("idx", [1, B * NPP + 2 * B], I32)

        l0 = ExitStack()

        def l0_sb(name, shape, dt=F32):
            return l0.enter_context(nc.sbuf_tensor(name, shape, dt))

        wg = l0_sb("wg", [P, C, F])
        wu = l0_sb("wu", [P, C, F])
        xT0 = l0_sb("xT0", [P, C, HT])
        lbg = l0_sb("lbg", [LR, F])
        lbu = l0_sb("lbu", [LR, F])
        lag = l0_sb("lag", [P, 2, C, LR])
        lau = l0_sb("lau", [P, 2, C, LR])
        act = l0_sb("act", [P, FC, HT])
        wd = l0_sb("wd", [P, FC, HID])
        lad = l0_sb("lad", [P, 2, FC, LR])
        lbd = l0_sb("lbd", [LR, 2, HID])
        blk = l0_sb("blk", [LR, HT])
        tb = l0_sb("tb", [LR, 3, HT])
        e_sb = l0_sb("e_sb", [P, 2, HT])
        r_sb = l0_sb("r_sb", [P, HT])
        prep = l0_sb("prep", [P, 9, HID])
        l2a = l0_sb("l2a", [LORA2, HID])
        l2b = l0_sb("l2b", [LORA2, HID])
        small = l0_sb("small", [P, 64])
        len_i = l0_sb("len_i", [P, B], I32)
        pos_i = l0_sb("pos_i", [P, B], I32)
        key_i = r_sb[:, :].bitcast(I32)
        nw = l0_sb("nw", [P, 3, D])
        l0.close()

        l1 = ExitStack()

        def l1_sb(name, shape, dt=F32):
            return l1.enter_context(nc.sbuf_tensor(name, shape, dt))

        xh = l1_sb("xh", [P, B, C, T], F32R)
        xl = l1_sb("xl", [P, B, C, T], F32R)
        wh = l1_sb("wh", [P, C, QKV], F32R)
        wl = l1_sb("wl", [P, C, QKV], F32R)
        stage = l1_sb("stage", [P, 2, QKV])
        k_raw = l1_sb("k_raw", [P, 2, LC, D])
        v_sb = l1_sb("v_sb", [P, 4, KC, D])
        woh = l1_sb("woh", [P, REP, HID], F32R)
        wol = l1_sb("wol", [P, REP, HID], F32R)
        q_sb = l1_sb("q_sb", [P, QW])
        k_sb = l1_sb("k_sb", [P, D])
        sq_q = l1_sb("sq_q", [P, QW])
        sq_k = l1_sb("sq_k", [P, D])
        q_cos = l1_sb("q_cos", [P, QW])
        q_sin = l1_sb("q_sin", [P, QW])
        k_cos = l1_sb("k_cos", [P, D])
        k_sin = l1_sb("k_sin", [P, D])
        qTh = l1_sb("qTh", [P, 2, QW], F32R)
        qTl = l1_sb("qTl", [P, 2, QW], F32R)
        kTh = l1_sb("kTh", [P, 2, KEYS], F32R)
        kTl = l1_sb("kTl", [P, 2, KEYS], F32R)
        s_sb = l1_sb("s_sb", [P, 2, KEYS])
        p_sb = l1_sb("p_sb", [P, 2, REP, KEYS])
        pT = l1_sb("pT", [P, KC, QW])
        oTh = l1_sb("oTh", [P, QW], F32R)
        oTl = l1_sb("oTl", [P, QW], F32R)
        var = l1_sb("var", [P, 2, 8])
        rstd = l1_sb("rstd", [P, 2, 8])
        top = l1_sb("top", [P, 8])
        bias = l1_sb("bias", [P, 8])
        total = l1_sb("total", [P, 8])
        inv = l1_sb("inv", [P, 8])
        l1.close()

        l2 = ExitStack()

        def l2_sb(name, shape, dt=F32):
            return l2.enter_context(nc.sbuf_tensor(name, shape, dt))

        w2 = l2_sb("w2", [P, C, HID])
        w3 = l2_sb("w3", [P, 2, C, HID])
        x2T = l2_sb("x2T", [P, 2, C, T])
        x3T = l2_sb("x3T", [P, 2, C, T])
        l2.close()

        names = """idx_in x_in xT_in xT_in2 lbg_in2 lbu_in2 lag_in lau_in lad_in lbg_in lbu_in lbd_in wd_in l2_in code_in nw_in len_in
        ident_set iota_set blk_set const_set w2_put w2_in w2_ready delta delta_copied scale_exp w2_loaded
        t_gate t_up tb_gate tb_up gate_up exp_g inv_g gated act_set t_down tb_down down x1_added
        step_done ang_ready sin_ready rope_ready mask_ready x1T x1h x1l wqkv_h wqkv_l wo_h wo_l
        q_done kv_done q_copied k_copied v_copied q_sq k_sq q_ss k_ss q_var k_var q_pow k_pow
        qcos qsin qrope kcos ksin ksum krope kcT qT knT kch qh knh kcl ql knl
        score max_begun topped biased exped inverted normed pt pt_copied pv oh ol y y_added
        x2T_done x2T_copied l2_done x3_added x3T_done x3T_copied l3_done x4_added stored""".split()
        S = {n: sem(n) for n in names}
        w_in = [sem(f"w_in_{n}") for n in range(8)]
        page_in = [sem(f"page_in_{b}") for b in range(B)]
        stage_in = [sem(f"stage_in_{n}") for n in range(2)]
        k_load = [sem(f"k_load_{n}") for n in range(2)]
        v_load = [sem(f"v_load_{n}") for n in range(4)]
        w3_load = [sem(f"w3_load_{n}") for n in range(2)]

        block = ctx.enter_context(nc.Block())
        FQ = F // 4

        @block.sync
        def _(sp):
            def load(dst, src, s):
                sp.dma_start(dst, src).then_inc(s, 16)

            load(idx[:, 0:B * NPP], ins["pages"].rearrange("(a b) n -> a (b n)", a=1), S["idx_in"])
            load(idx[:, B * NPP:B * NPP + B], ins["ad0"].rearrange("(a b) -> a b", a=1), S["idx_in"])
            load(idx[:, B * NPP + B:], ins["ad3"].rearrange("(a b) -> a b", a=1), S["idx_in"])
            load(xT0[:, :, :], ins["xT"][:, :, 0:HT], S["xT_in"])
            sp.wait_ge(S["idx_in"], 48)

            def adapter(b):
                return sp.value_load(idx[0:1, B * NPP + b:B * NPP + b + 1], min_val=0, max_val=15)

            for b in range(B):
                hf, j = b // HALF, b % HALF
                r = slice(j * RANK, (j + 1) * RANK)
                a = adapter(b)
                load(lag[:, hf, :, r], ins["AgT"][bass.ds(a, 1), :, :, :].rearrange("a p c r -> (a p) c r"), S["lag_in"])
                load(lau[:, hf, :, r], ins["AuT"][bass.ds(a, 1), :, :, :].rearrange("a p c r -> (a p) c r"), S["lau_in"])
                if hf == 0:
                    load(lbg[r, :], ins["BgT"][bass.ds(a, 1), :, :].rearrange("a r f -> (a r) f"), S["lbg_in"])
                    load(lbu[r, :], ins["BuT"][bass.ds(a, 1), :, :].rearrange("a r f -> (a r) f"), S["lbu_in"])
            for n in range(4):
                load(wg[:, :, n * FQ:(n + 1) * FQ], ins["WgT"][:, :, n * FQ:(n + 1) * FQ], w_in[2 * n])
                load(wu[:, :, n * FQ:(n + 1) * FQ], ins["WuT"][:, :, n * FQ:(n + 1) * FQ], w_in[2 * n + 1])
            for b in range(B):
                hf, j = b // HALF, b % HALF
                r = slice(j * RANK, (j + 1) * RANK)
                a = adapter(b)
                load(lad[:, hf, 0:FC - 1, r], ins["AdT"][bass.ds(a, 1), :, :, :].rearrange("a p c r -> (a p) c r"), S["lad_in"])
                load(lad[0:FTAIL, hf, FC - 1, r], ins["AdTt"][bass.ds(a, 1), :, :].rearrange("a p r -> (a p) r"), S["lad_in"])
                load(lbd[r, hf, :], ins["BdT"][bass.ds(a, 1), :, :].rearrange("a r f -> (a r) f"), S["lbd_in"])
            load(wd[:, 0:FC - 1, :], ins["WdT"][0:(FC - 1) * P, :].rearrange("(c p) n -> p c n", p=P), S["wd_in"])
            load(wd[0:FTAIL, FC - 1, :], ins["WdT"][(FC - 1) * P:, :], S["wd_in"])
            load(x_sb[:, :, :], ins["x"].rearrange("b t n -> t b n"), S["x_in"])
            for b in range(B):
                for j in range(NPP):
                    n = b * NPP + j
                    pg = sp.value_load(idx[0:1, n:n + 1], min_val=0, max_val=63)
                    for src, dst in (("k_cache", k_pages), ("v_cache", v_pages)):
                        load(dst[b, j * PSIZE:(j + 1) * PSIZE, :, :].rearrange("s h d -> s (h d)"),
                             ins[src][bass.ds(pg, 1), :, :, :].rearrange("a s h d -> (a s) (h d)"), page_in[b])

            def of_head(pages, u):
                v = pages[u.seq, :, :, :].rearrange("(c p) h d -> p c (h d)", p=P)
                return v[:, :, bass.ds(u.head * D, D)]

            def load_kv(u):
                if u.turn is None and u.k < B or u.turn is not None:
                    sp.wait_ge(page_in[u.seq], 2 * NPP * 16)
                if u.turn is not None or u.k >= 2:
                    sp.wait_ge(S["kcT"], (u + -2).count(1, 1))
                sp.dma_start(k_raw[:, u.k % 2, :, :], of_head(k_pages, u)).then_inc(k_load[u.k % 2], 16)
                if u.turn is not None or u.k >= 4:
                    sp.wait_ge(S["pv"], (u + -4).count(1, 1))
                sp.dma_start(v_sb[:, u.k % 4, 0:LC, :], of_head(v_pages, u)).then_inc(v_load[u.k % 4], 16)

            def load_wqkv(u, c):
                sp.dma_start(stage[:, c % 2, :],
                             ins["Wqkv"][bass.ds(u.head, 1), :, c, :].rearrange("a p n -> (a p) n")
                             ).then_inc(stage_in[c % 2], 16)

            def load_wo(u, h):
                sp.dma_start(stage[:, h % 2, 0:HID],
                             ins["WoT"][bass.ds(u.head, 1), :, h, :].rearrange("a p n -> (a p) n")
                             ).then_inc(stage_in[h % 2], 16)

            def step(u):
                if u.k == -1:
                    first = u + 1
                    sp.wait_ge(S["down"], B)
                    sp.wait_ge(S["w2_put"], 16 * C)
                    for c in range(2):
                        load_wqkv(first, c)
                    for n in (0, 1):
                        load_kv(first + n)
                    for c in range(2, C):
                        sp.wait_ge(S["wqkv_l"], c - 1)
                        load_wqkv(first, c)
                    for h in range(REP):
                        sp.wait_ge(S["wqkv_l" if h < 2 else "wo_l"], h + 3 if h < 2 else h - 1)
                        load_wo(first, h)
                    return
                if (u + 2).exists():
                    load_kv(u + 2)
                if u.seq == 5 and (u + 3).exists():
                    for c in range(2):
                        sp.wait_ge(S["wo_l"], u.heads(REP, c + 3))
                        load_wqkv(u + 3, c)
                if u.seq == 6 and (u + 2).exists():
                    for c in range(2, C):
                        sp.wait_ge(S["wqkv_l"], (u + 2).heads(C, c - 1))
                        load_wqkv(u + 2, c)
                    for h in range(2):
                        sp.wait_ge(S["wqkv_l"], (u + 2).heads(C, h + 3))
                        load_wo(u + 2, h)
                if u.seq == 1 and u.k > 1 and u.exists():
                    for h in range(2, REP):
                        sp.wait_ge(S["wo_l"], u.heads(REP, h - 1))
                        load_wo(u, h)

            run_steps(sp, step)

            sp.wait_ge(S["kv_done"], UNITS)
            load(w2[:, :, :], w2_dram, S["w2_loaded"])
            for b in range(B):
                if b >= 2:
                    sp.wait_ge(S["l3_done"], b - 1)
                a = sp.value_load(idx[0:1, B * NPP + B + b:B * NPP + B + b + 1], min_val=0, max_val=7)
                load(w3[:, b % 2, :, :], ins["W3T"][bass.ds(a, 1), :, :, :].rearrange("a p c n -> (a p) c n"), w3_load[b % 2])
            for b in range(B):
                sp.wait_ge(S["x4_added"], b + 1)
                load(out[b, :, :], x_sb[:, b, :], S["stored"])
            sp.wait_ge(S["stored"], 16 * B)

        @block.gpsimd
        def _(pool):
            pool.memset(ident[:, :], 0.0).then_inc(S["ident_set"], 1)
            pool.memset(blk[:, :], 0.5).then_inc(S["blk_set"], 1)
            pool.wait_ge(S["ident_set"], 1)
            pool.affine_select(out=ident[:, :], in_=ident[:, :], compare_op=ALU.not_equal, fill=1.0,
                               base=0, pattern=[[-1, P]], channel_multiplier=1).then_inc(S["ident_set"], 1)
            v = blk[:, :].rearrange("p (j t) -> p j t", j=HALF)
            pool.wait_ge(S["blk_set"], 1)
            pool.affine_select(out=v, in_=v, compare_op=ALU.is_ge, fill=0.0, base=0,
                               pattern=[[-RANK, HALF], [0, T]], channel_multiplier=1).then_inc(S["blk_set"], 1)
            pool.wait_ge(S["blk_set"], 2)
            pool.affine_select(out=v, in_=v, compare_op=ALU.is_ge, fill=0.0, base=RANK - 1,
                               pattern=[[RANK, HALF], [0, T]], channel_multiplier=-1).then_inc(S["blk_set"], 1)
            pool.memset(half_neg[:, :], -0.5).then_inc(S["const_set"], 1)
            pool.iota(pos_i[:, :], pattern=[[0, B]], base=0, channel_multiplier=1).then_inc(S["iota_set"], 1)
            pool.iota(key_i[:, :], pattern=[[1, L]], base=0, channel_multiplier=0).then_inc(S["iota_set"], 1)
            pool.dma_start(small[:, 0:NCODE], ins["code"].partition_broadcast(P)).then_inc(S["code_in"], 16)
            pool.dma_start(len_i[:, :], ins["lens"].partition_broadcast(P)).then_inc(S["len_in"], 16)
            pool.dma_start(nw[:, 0, :], ins["qw"].partition_broadcast(P)).then_inc(S["nw_in"], 16)
            pool.dma_start(nw[:, 1, :], ins["kw"].partition_broadcast(P)).then_inc(S["nw_in"], 16)
            pool.dma_start(nw[:, 2, 0:D // 2], ins["inv_freq"].partition_broadcast(P)).then_inc(S["nw_in"], 16)
            pool.dma_start(l2b[:, :], ins["lbT"]).then_inc(S["l2_in"], 16)
            pool.dma_start(l2a[:, :], ins["la"]).then_inc(S["l2_in"], 16)
            pool.wait_ge(S["rope_ready"], 4)
            pool.wait_ge(S["mask_ready"], 1)
            for g in range(C):
                if g:
                    pool.wait_ge(S["w2_put"], 16 * g)
                pool.dma_start(prep[:, 0, :], ins["W2T"][:, g, :]).then_inc(S["w2_in"], 16)
                pool.dma_start(prep[:, 1, :], ins["slT"][g, :].partition_broadcast(P)).then_inc(S["w2_in"], 16)
                pool.wait_ge(S["w2_ready"], g + 1)
                pool.dma_start(w2_dram[:, g, :], prep[:, 0, :]).then_inc(S["w2_put"], 16)
            pool.wait_ge(S["gate_up"], 2 * FC)
            pool.dma_start(xT0[:, :, :], ins["xT"][:, :, HT:]).then_inc(S["xT_in2"], 16)
            pool.wait_ge(S["idx_in"], 48)
            for j in range(HALF):
                r = slice(j * RANK, (j + 1) * RANK)
                n = B * NPP + HALF + j
                a = pool.value_load(idx[0:1, n:n + 1], min_val=0, max_val=15)
                pool.dma_start(lbg[r, :], ins["BgT"][bass.ds(a, 1), :, :].rearrange("a r f -> (a r) f")).then_inc(S["lbg_in2"], 16)
                pool.dma_start(lbu[r, :], ins["BuT"][bass.ds(a, 1), :, :].rearrange("a r f -> (a r) f")).then_inc(S["lbu_in2"], 16)

            def step(u):
                n = u + 1
                if not n.exists():
                    return
                later = n.turn is not None or n.k > 0
                b = n.seq
                pool.wait_ge(S["q_copied"], n.count(1, 1))
                if later:
                    pool.wait_ge(S["qrope"], u.count(1, 1))
                src = q_sb[:, :].rearrange("p (h s d) -> p h s d", h=REP, s=2)
                dst = q_sin[:, :].rearrange("p (h s d) -> p h s d", h=REP, s=2)
                for s in range(2):
                    pool.tensor_tensor(
                        dst[:, :, s, :], src[:, :, 1 - s, :],
                        rope_tab[:, 1, b, s * 64:(s + 1) * 64].unsqueeze(1).to_broadcast([P, REP, 64]),
                        ALU.mult).then_inc(S["qsin"], 1)
                pool.wait_ge(S["q_var"], n.count(1, 1))
                if n.turn is not None or n.k >= 2:
                    pool.wait_ge(S["exped"], (n + -2).count(REP, REP))
                    pool.wait_ge(S["biased"], (n + -2).count(REP, REP))
                pool.tensor_tensor(rstd[:, n.k % 2, 0:REP], var[:, n.k % 2, 0:REP], half_neg[:, 0:REP],
                                   ALU.pow).then_inc(S["q_pow"], 1)
                pool.wait_ge(S["k_copied"], n.count(1, 1))
                if later:
                    pool.wait_ge(S["ksum"], u.count(1, 1))
                for s in range(2):
                    pool.tensor_tensor(k_sin[:, s * 64:(s + 1) * 64], k_sb[:, (1 - s) * 64:(2 - s) * 64],
                                       rope_tab[:, 3, b, s * 64:(s + 1) * 64], ALU.mult).then_inc(S["ksin"], 1)
                pool.wait_ge(S["k_var"], n.count(1, 1))
                if n.turn is not None or n.k >= 2:
                    pool.wait_ge(S["krope"], (n + -2).count(1, 1))
                pool.tensor_tensor(rstd[:, n.k % 2, REP:REP + 1], var[:, n.k % 2, REP:REP + 1], half_neg[:, 0:1],
                                   ALU.pow).then_inc(S["k_pow"], 1)

            pool.wait_ge(S["const_set"], 1)
            run_steps(pool, step)

        @block.scalar
        def _(act_e):
            act_e.wait_ge(S["ang_ready"], 2)
            for n in range(2):
                act_e.activation(prep[:, 4 + n, :], prep[:, 2 + n, :], ACT.Sin).then_inc(S["sin_ready"], 1)

            def group_scale(g):
                act_e.wait_ge(S["delta"], g + 1)
                if g:
                    act_e.wait_ge(S["w2_ready"], g)
                act_e.activation(prep[:, 2, :], ring[1][:, :], ACT.Copy).then_inc(S["delta_copied"], 1)
                act_e.wait_ge(S["w2_in"], 32 * (g + 1))
                act_e.activation(prep[:, 1, :], prep[:, 1, :], ACT.Exp).then_inc(S["scale_exp"], 1)

            for hf in range(2):
                for m in range(FC):
                    n = hf * FC + m
                    act_e.wait_ge(S["gate_up"], 2 * n + 1)
                    if n >= 2:
                        act_e.wait_ge(S["act_set"], n - 1)
                    act_e.activation(e_sb[0:rows(m), n % 2, :], gate_ps[n % 2][0:rows(m), :], ACT.Exp,
                                     scale=-1.0).then_inc(S["exp_g"], 1)
                    if hf == 0 and m % 2 == 0 and m < 2 * C:
                        group_scale(m // 2)

            for b in range(B):
                act_e.wait_ge(S["x1T"], b + 1)
                act_e.activation(xh[:, b, :, :], ring[b % 2][:, :].rearrange("p (c t) -> p c t", c=C),
                                 ACT.Copy).then_inc(S["x1h"], 1)

            def split_wqkv(u, c):
                if c < 2 and (u.turn is not None or u.k >= B):
                    act_e.wait_ge(S["kv_done"], (u).count(1, 0))
                act_e.wait_ge(stage_in[c % 2], staged(u, "in", c))
                act_e.activation(wh[:, c, :], stage[:, c % 2, :], ACT.Copy).then_inc(S["wqkv_h"], 1)

            def split_wo(u, h):
                if h < 1 and (u.turn is not None or u.k >= B):
                    act_e.wait_ge(S["y"], u.count(1, -1))
                act_e.wait_ge(stage_in[h % 2], staged(u, "out", h))
                act_e.activation(woh[:, h, :], stage[:, h % 2, 0:HID], ACT.Copy).then_inc(S["wo_h"], 1)

            def exp(u, h):
                act_e.wait_ge(S["biased"], u.count(REP, h + 1))
                if h == 0 and (u.turn is not None or u.k >= 2):
                    act_e.wait_ge(S["pt"], (u + -2).count(KC, KC))
                if h == 0 and (u.turn is not None or u.k >= 1):
                    act_e.wait_ge(S["inverted"], (u + -1).count(REP, REP))
                act_e.activation(p_sb[:, u.k % 2, h, :], s_sb[:, h % 2, :], ACT.Exp, bias=bias[:, h:h + 1],
                                 scale=rstd[:, u.k % 2, h:h + 1], accum_out=total[:, h:h + 1]
                                 ).then_inc(S["exped"], 1)

            def copy_pt(u, c):
                act_e.wait_ge(S["pt"], u.count(KC, c + 1))
                if c == 0 and (u.turn is not None or u.k >= 1):
                    act_e.wait_ge(S["pv"], u.count(1, 0))
                act_e.activation(pT[:, c, :], ring[c % 2][:, :], ACT.Copy).then_inc(S["pt_copied"], 1)

            def step(u):
                n, p, pp = u + 1, u + -1, u + -2
                after = n.turn is not None or n.k > 0
                if u.seq == 7 and n.exists():
                    for c in (2, 3):
                        if u.k >= 0:
                            split_wqkv(n, c)
                if u.k == -1:
                    for c in range(C):
                        split_wqkv(n, c)
                    for h in range(REP):
                        split_wo(n, h)
                if pp.exists():
                    act_e.wait_ge(S["pv"], pp.count(1, 1))
                    if pp.turn is not None or pp.k > 0:
                        act_e.wait_ge(S["y"], pp.count(1, 0))
                    act_e.activation(oTh[:, :], o_ps[:, :], ACT.Copy).then_inc(S["oh"], 1)
                if p.exists():
                    copy_pt(p, 0)
                    copy_pt(p, 1)
                if u.exists():
                    exp(u, 0)
                    exp(u, 1)
                if n.exists():
                    act_e.wait_ge(S["q_done"], n.count(1, 1))
                    if after:
                        act_e.wait_ge(S["qcos"], u.count(1, 1))
                        act_e.wait_ge(S["qsin"], u.count(2, 2))
                    act_e.activation(q_sb[:, :], proj_ps[:, :], ACT.Copy).then_inc(S["q_copied"], 1)
                if p.exists():
                    copy_pt(p, 2)
                if n.exists():
                    act_e.wait_ge(S["q_copied"], n.count(1, 1))
                    if after:
                        act_e.wait_ge(S["q_ss"], u.count(1, 1))
                    act_e.activation(sq_q[:, :], q_sb[:, :], ACT.Square).then_inc(S["q_sq"], 1)
                if u.seq == 1 and u.k > 1 and u.exists():
                    for h in range(REP):
                        split_wo(u, h)
                if u.exists():
                    exp(u, 2)
                if n.exists():
                    act_e.wait_ge(S["kv_done"], n.count(1, 1))
                    if after:
                        act_e.wait_ge(S["kcos"], u.count(1, 1))
                        act_e.wait_ge(S["ksin"], u.count(2, 2))
                    act_e.activation(k_sb[:, :], proj_ps[:, 0:D], ACT.Copy).then_inc(S["k_copied"], 1)
                    if n.turn is not None or n.k >= 4:
                        act_e.wait_ge(S["pv"], (n + -4).count(1, 1))
                    act_e.activation(v_sb[:, n.k % 4, LC, :], proj_ps[:, D:2 * D], ACT.Copy).then_inc(S["v_copied"], 1)
                    act_e.wait_ge(S["k_copied"], n.count(1, 1))
                    if after:
                        act_e.wait_ge(S["k_ss"], u.count(1, 1))
                    act_e.activation(sq_k[:, :], k_sb[:, :], ACT.Square).then_inc(S["k_sq"], 1)
                if p.exists():
                    copy_pt(p, 3)
                    copy_pt(p, 4)
                if n.exists():
                    if n.turn is not None or n.k >= 2:
                        act_e.wait_ge(S["score"], (n + -2).count(REP, REP))
                    act_e.wait_ge(S["kcT"], n.count(1, 1))
                    act_e.activation(kTh[:, n.k % 2, 0:L], ring[1][:, :], ACT.Copy).then_inc(S["kch"], 1)
                if u.exists():
                    exp(u, 3)
                if n.exists():
                    act_e.wait_ge(S["qT"], n.count(1, 1))
                    act_e.activation(qTh[:, n.k % 2, :], ring[0][:, :], ACT.Copy).then_inc(S["qh"], 1)
                    act_e.wait_ge(S["knT"], n.count(1, 1))
                    act_e.activation(kTh[:, n.k % 2, L:KEYS], ring[1][:, 0:T], ACT.Copy).then_inc(S["knh"], 1)
                if u.seq == 6 and (u + 2).exists():
                    for c in (0, 1):
                        split_wqkv(u + 2, c)

            run_steps(act_e, step)

            for b in range(B):
                act_e.wait_ge(S["x2T_done"], b + 1)
                if b >= 2:
                    act_e.wait_ge(S["l2_done"], b - 1)
                act_e.activation(x2T[:, b % 2, :, :], ring[0][:, :].rearrange("p (c t) -> p c t", c=C),
                                 ACT.Copy).then_inc(S["x2T_copied"], 1)
                act_e.wait_ge(S["x3T_done"], b + 1)
                if b >= 2:
                    act_e.wait_ge(S["l3_done"], b - 1)
                act_e.activation(x3T[:, b % 2, :, :], ring[1][:, :].rearrange("p (c t) -> p c t", c=C),
                                 ACT.Copy).then_inc(S["x3T_copied"], 1)

        @block.tensor
        def _(pe):
            mm = nc.tensor.matmul
            pe.wait_ge(S["ident_set"], 2)
            pe.wait_ge(S["l2_in"], 32)

            def delta(g):
                if g:
                    pe.wait_ge(S["delta_copied"], g)
                mm(ring[1][:, :], l2a[:, g * P:(g + 1) * P], l2b[:, :], start=True, stop=True).then_inc(S["delta"], 1)

            for hf in range(2):
                pe.wait_ge(S["xT_in2" if hf else "xT_in"], 16)
                pe.wait_ge(S["lag_in"], 16 * B)
                pe.wait_ge(S["lau_in"], 16 * B)
                if hf:
                    pe.wait_ge(S["delta_copied"], C)
                    pe.wait_ge(S["tb_down"], 1)
                for n, (la, name) in enumerate(((lag, "t_gate"), (lau, "t_up"))):
                    for c in range(C):
                        i = mm(ring[n][0:LR, :], la[:, hf, c, :], xT0[:, c, :], start=c == 0, stop=c == C - 1)
                    i.then_inc(S[name], 1)
                pe.wait_ge(S["lbg_in2" if hf else "lbg_in"], 16 * HALF)
                pe.wait_ge(S["lbu_in2" if hf else "lbu_in"], 16 * HALF)
                for m in range(FC):
                    n = hf * FC + m
                    fs = slice(m * P, m * P + rows(m))
                    piece = min((m * P + rows(m) - 1) // FQ, 3)
                    for k, (w, lb, bank, ready) in enumerate(((wg, lbg, gate_ps, "tb_gate"), (wu, lbu, up_ps, "tb_up"))):
                        if hf == 0:
                            pe.wait_ge(w_in[2 * piece + k], 16)
                        if n >= 2:
                            pe.wait_ge(S["act_set"], n - 1)
                        for c in range(C):
                            mm(bank[n % 2][0:rows(m), :], w[:, c, fs], xT0[:, c, :], start=c == 0, stop=False)
                        if m == 0:
                            pe.wait_ge(S[ready], hf + 1)
                        mm(bank[n % 2][0:rows(m), :], lb[:, fs], tb[:, k, :], start=False, stop=True
                           ).then_inc(S["gate_up"], 1)
                    if hf == 0 and m % 2 == 0 and m < 2 * C:
                        if m == 0:
                            pe.wait_ge(S["tb_up"], 1)
                        delta(m // 2)
                pe.wait_ge(S["act_set"], FC * (hf + 1))
                pe.wait_ge(S["lad_in"], 32 * B)
                pe.wait_ge(S["tb_gate"], hf + 1)
                for m in range(FC):
                    i = mm(ring[0][0:LR, :], lad[0:rows(m), hf, m, :], act[0:rows(m), m, :], start=m == 0, stop=m == FC - 1)
                i.then_inc(S["t_down"], 1)
                pe.wait_ge(S["wd_in"], 32)
                pe.wait_ge(S["lbd_in"], 16 * B)
                for j in range(HALF):
                    b = hf * HALF + j
                    if b >= 2:
                        pe.wait_ge(S["x1_added"], b - 1)
                    ts = slice(j * T, (j + 1) * T)
                    for m in range(FC):
                        mm(down_ps[b % 2], act[0:rows(m), m, ts], wd[0:rows(m), m, :], start=m == 0, stop=False)
                    if j == 0:
                        pe.wait_ge(S["tb_down"], hf + 1)
                    mm(down_ps[b % 2], tb[:, 2, ts], lbd[:, hf, :], start=False, stop=True).then_inc(S["down"], 1)
            for b in range(B):
                pe.wait_ge(S["x1_added"], b + 1)
                if b >= 2:
                    pe.wait_ge(S["x1l"], b - 1)
                for c in range(C):
                    i = nc.tensor.transpose(ring[b % 2][:, c * P:(c + 1) * P], x_sb[:, b, c * P:(c + 1) * P], ident[:, :])
                i.then_inc(S["x1T"], 1)

            def project(n, cols, width, name):
                b = n.seq
                if cols == 0:
                    if n.turn is None and n.k < B:
                        pe.wait_ge(S["x1l"], b + 1)
                        pe.wait_ge(S["x1h"], b + 1)
                    if b == 0:
                        pe.wait_ge(S["wqkv_h"], n.heads(C, C))
                        pe.wait_ge(S["wqkv_l"], n.heads(C, C))
                k = 0
                for c in range(C):
                    for a, w in ((xh, wh), (xh, wl), (xl, wh)):
                        i = mm(proj_ps[:, 0:width], a[:, b, c, :], w[:, c, cols:cols + width], start=k == 0, stop=k == 3 * C - 1)
                        k += 1
                i.then_inc(S[name], 1)

            def scores(u, h):
                hs = slice(h * D, (h + 1) * D)
                par = u.k % 2
                if h == 0:
                    for name in ("qh", "ql", "kch", "kcl", "knh", "knl"):
                        pe.wait_ge(S[name], u.count(1, 1))
                if h >= 2:
                    pe.wait_ge(S["topped"], u.count(REP, h - 1))
                elif u.turn is not None or u.k >= 1:
                    pe.wait_ge(S["topped"], u.count(REP, h - 1))
                for s in range(2):
                    ks = slice(s * SPLIT, (s + 1) * SPLIT)
                    for k, (a, w) in enumerate(((qTh, kTh), (qTh, kTl), (qTl, kTh))):
                        i = mm(score_ps[h % 2][:, s, 0:SPLIT], a[:, par, hs], w[:, par, ks], start=k == 0, stop=k == 2)
                i.then_inc(S["score"], 1)

            def transpose_p(p, c):
                if c == 0:
                    pe.wait_ge(S["normed"], p.count(REP, REP))
                    if (p + 1).exists():
                        pe.wait_ge(S["ql"], (p + 1).count(1, 1))
                elif c == 1:
                    if (p + 1).exists():
                        pe.wait_ge(S["knl"], (p + 1).count(1, 1))
                else:
                    pe.wait_ge(S["pt_copied"], p.count(KC, c - 1))
                for h in range(REP):
                    i = nc.tensor.transpose(ring[c % 2][:, h * P:(h + 1) * P], p_sb[:, p.k % 2, h, c * P:(c + 1) * P], ident[:, :])
                i.then_inc(S["pt"], 1)

            def attend(p, c):
                pe.wait_ge(S["pt_copied"], p.count(KC, c + 1))
                if c == 0:
                    pe.wait_ge(v_load[p.k % 4], 16 * (p.k // 4 + 1) if p.turn is None else p.turn * 32 + 16 * (p.k // 4 + 1))
                    pe.wait_ge(S["v_copied"], p.count(1, 1))
                    if p.turn is not None or p.k >= 1:
                        pe.wait_ge(S["ol"], p.count(1, 0))
                i = mm(o_ps[:, :], v_sb[:, p.k % 4, c, :], pT[:, c, :], start=c == 0, stop=c == KC - 1)
                if c == KC - 1:
                    i.then_inc(S["pv"], 1)

            def output(pp):
                pe.wait_ge(S["oh"], pp.count(1, 1))
                pe.wait_ge(S["ol"], pp.count(1, 1))
                if (pp + 2).exists():
                    pe.wait_ge(S["k_copied"], (pp + 2).count(1, 1))
                    pe.wait_ge(S["v_copied"], (pp + 2).count(1, 1))
                else:
                    pe.wait_ge(S["y_added"], pp.count(1, 0))
                if pp.seq == 0:
                    pe.wait_ge(S["wo_h"], pp.heads(REP, REP))
                    pe.wait_ge(S["wo_l"], pp.heads(REP, REP))
                k = 0
                for h in range(REP):
                    hs = slice(h * D, (h + 1) * D)
                    for a, w in ((oTh, woh), (oTh, wol), (oTl, woh)):
                        i = mm(proj_ps[:, :], a[:, hs], w[:, h, :], start=k == 0, stop=k == 3 * REP - 1)
                        k += 1
                i.then_inc(S["y"], 1)

            def transpose_keys(n):
                pe.wait_ge(k_load[n.k % 2], 16 * (n.k // 2 + 1) if n.turn is None else n.turn * 64 + 16 * (n.k // 2 + 1))
                if (n + -2).exists():
                    pe.wait_ge(S["pt_copied"], (n + -2).count(KC, 4))
                elif n.k == 0:
                    pe.wait_ge(S["x1l"], B)
                else:
                    pe.wait_ge(S["knl"], (n + -1).count(1, 1))
                for c in range(LC):
                    i = nc.tensor.transpose(ring[1][:, c * P:(c + 1) * P], k_raw[:, n.k % 2, c, :], ident[:, :])
                i.then_inc(S["kcT"], 1)

            def transpose_new(n):
                pe.wait_ge(S["qrope"], n.count(1, 1))
                if (n + -2).exists():
                    pe.wait_ge(S["pt_copied"], (n + -2).count(KC, 5))
                elif n.k == 1:
                    pe.wait_ge(S["ql"], 1)
                for h in range(REP):
                    i = nc.tensor.transpose(ring[0][:, h * P:(h + 1) * P], q_cos[:, h * P:(h + 1) * P], ident[:, :])
                i.then_inc(S["qT"], 1)
                pe.wait_ge(S["krope"], n.count(1, 1))
                pe.wait_ge(S["kcl"], n.count(1, 1))
                nc.tensor.transpose(ring[1][:, 0:P], k_cos[:, :], ident[:, :]).then_inc(S["knT"], 1)

            def step(u):
                n, p, pp = u + 1, u + -1, u + -2
                if u.exists():
                    scores(u, 0)
                if p.exists():
                    transpose_p(p, 0)
                    transpose_p(p, 1)
                if pp.exists():
                    output(pp)
                if u.exists():
                    scores(u, 1)
                if n.exists():
                    if pp.exists():
                        pe.wait_ge(S["y_added"], pp.count(1, 1))
                    elif u.exists():
                        pe.wait_ge(S["k_copied"], u.count(1, 1))
                        pe.wait_ge(S["v_copied"], u.count(1, 1))
                    else:
                        pe.wait_ge(S["x1_added"], B)
                    project(n, 0, QW, "q_done")
                if p.exists():
                    attend(p, 0)
                    transpose_p(p, 2)
                if u.exists():
                    scores(u, 2)
                if n.exists():
                    pe.wait_ge(S["q_copied"], n.count(1, 1))
                    project(n, QW, 2 * D, "kv_done")
                if p.exists():
                    attend(p, 1)
                    transpose_p(p, 3)
                    transpose_p(p, 4)
                if n.exists():
                    transpose_keys(n)
                if u.exists():
                    scores(u, 3)
                if n.exists():
                    transpose_new(n)
                if p.exists():
                    for c in range(2, KC):
                        attend(p, c)

            run_steps(pe, step)

            def layer3(b):
                pe.wait_ge(w3_load[b % 2], 16 * (b // 2 + 1))
                if b >= 1:
                    pe.wait_ge(S["x4_added"], b)
                for c in range(C):
                    i = mm(down_ps[1], x3T[:, b % 2, c, :], w3[:, b % 2, c, :], start=c == 0, stop=c == C - 1)
                i.then_inc(S["l3_done"], 1)

            def turn_x(b, slot, name, waits):
                for w, v in waits:
                    pe.wait_ge(S[w], v)
                for c in range(C):
                    i = nc.tensor.transpose(ring[slot][:, c * P:(c + 1) * P], x_sb[:, b, c * P:(c + 1) * P], ident[:, :])
                i.then_inc(S[name], 1)

            pe.wait_ge(S["pt_copied"], UNITS * KC)
            pe.wait_ge(S["w2_loaded"], 16)
            turn_x(0, 0, "x2T_done", (("y_added", UNITS),))
            for b in range(B):
                pe.wait_ge(S["x2T_copied"], b + 1)
                if b >= 1:
                    pe.wait_ge(S["x3_added"], b)
                for c in range(C):
                    i = mm(down_ps[0], x2T[:, b % 2, c, :], w2[:, c, :], start=c == 0, stop=c == C - 1)
                i.then_inc(S["l2_done"], 1)
                if b >= 1:
                    pe.wait_ge(S["x3T_copied"], b)
                    layer3(b - 1)
                turn_x(b, 1, "x3T_done", (("x3_added", b + 1),))
                if b + 1 < B:
                    turn_x(b + 1, 0, "x2T_done", ())
            pe.wait_ge(S["x3T_copied"], B)
            layer3(B - 1)

        @block.vector
        def _(dve):
            v = nc.vector
            chain = [0]

            def then(ins):
                chain[0] += 1
                ins.then_inc(S["step_done"], 1)
                dve.wait_ge(S["step_done"], chain[0])

            lens = small[:, 16:24]
            pos = small[:, 24:32]
            ang, turns = prep[:, 0, :], prep[:, 1, :]
            dve.wait_ge(S["len_in"], 16)
            dve.wait_ge(S["iota_set"], 2)
            dve.wait_ge(S["nw_in"], 48)
            v.tensor_copy(lens, len_i[:, :])
            then(v.tensor_copy(pos, pos_i[:, :]))
            then(v.tensor_tensor(pos, pos, lens, ALU.add))
            for b in range(B):
                i = v.tensor_scalar(ang[:, b * 64:(b + 1) * 64], nw[:, 2, 0:64], pos[:, b:b + 1], None, ALU.mult)
            then(i)
            for n, quarter in enumerate((0.0, 0.25)):
                red = prep[:, 2 + n, :]
                then(v.tensor_scalar(turns, ang, 1.0 / TWO_PI, quarter, ALU.mult, ALU.add))
                then(v.tensor_scalar(turns, turns, ROUND, None, ALU.add))
                then(v.tensor_scalar(turns, turns, ROUND, None, ALU.subtract))
                then(v.scalar_tensor_tensor(red, turns, -PI_A, ang, ALU.mult, ALU.add))
                then(v.scalar_tensor_tensor(red, turns, -PI_B, red, ALU.mult, ALU.add))
                then(v.scalar_tensor_tensor(red, turns, -PI_C, red, ALU.mult, ALU.add))
                then(v.tensor_scalar(red, red, quarter * TWO_PI, PI_IN, ALU.add, ALU.min))
                v.tensor_scalar(red, red, -PI_IN, None, ALU.max).then_inc(S["ang_ready"], 1)
            then(v.tensor_scalar(nw[:, 0, :], nw[:, 0, :], SCALE, None, ALU.mult))
            key = prep[:, 6, :]
            then(v.tensor_copy(key, key_i))
            v.memset(mask[:, :, L:KEYS], 0.0)
            for b in range(B):
                i = v.tensor_scalar(mask[:, b, 0:L], key, lens[:, b:b + 1], NEG, ALU.is_ge, ALU.mult)
            i.then_inc(S["mask_ready"], 1)
            sin = prep[:, 4, :].rearrange("p (b j) -> p b j", b=B)
            cos = prep[:, 5, :].rearrange("p (b j) -> p b j", b=B)
            dve.wait_ge(S["sin_ready"], 2)

            def wide(n, s):
                return nw[:, n, s * 64:(s + 1) * 64].unsqueeze(1).to_broadcast([P, B, 64])

            for n in range(2):
                v.tensor_tensor(rope_tab[:, 2 * n, :, 0:64], cos, wide(n, 0), ALU.mult)
                v.tensor_tensor(rope_tab[:, 2 * n, :, 64:128], cos, wide(n, 1), ALU.mult).then_inc(S["rope_ready"], 1)
                v.tensor_tensor(rope_tab[:, 2 * n + 1, :, 64:128], sin, wide(n, 0), ALU.mult)
                v.scalar_tensor_tensor(rope_tab[:, 2 * n + 1, :, 0:64], sin, -1.0, wide(n, 1),
                                       ALU.mult, ALU.mult).then_inc(S["rope_ready"], 1)

            dve.wait_ge(S["code_in"], 16)
            code, cmax, thr = small[:, 0:NCODE], small[:, 33:34], small[:, 8:8 + NCODE - 1]
            then(v.tensor_reduce(cmax, code, AX_X, ALU.max, apply_absolute_value=True))
            then(v.tensor_scalar(cmax, cmax, 1e-8, None, ALU.max))
            then(v.reciprocal(cmax, cmax))
            then(v.tensor_scalar(code, code, cmax, None, ALU.mult))
            then(v.tensor_tensor(thr, small[:, 0:NCODE - 1], small[:, 1:NCODE], ALU.add))
            then(v.tensor_scalar(thr, thr, 0.5, None, ALU.mult))

            def weight2(g):
                w, scale, delta, tmp, norm = (prep[:, n, :] for n in range(5))
                leaf = [prep[:, 5 + n, :] for n in range(4)]
                dve.wait_ge(S["delta_copied"], g + 1)
                dve.wait_ge(S["scale_exp"], g + 1)
                then(v.tensor_scalar(delta, delta, 0.5, None, ALU.mult))
                then(v.tensor_tensor(w, w, delta, ALU.add))
                then(v.reciprocal(tmp, scale))
                then(v.tensor_tensor(norm, w, tmp, ALU.mult))
                for n in range(4):
                    t = thr[:, 2 * n:2 * n + 1]
                    v.tensor_scalar(leaf[n], norm, t, code[:, 2 * n + 1:2 * n + 2], ALU.is_gt, ALU.mult)
                    then(v.tensor_scalar(tmp, norm, t, code[:, 2 * n:2 * n + 1], ALU.is_le, ALU.mult))
                    then(v.tensor_tensor(leaf[n], leaf[n], tmp, ALU.add))
                for t, low, high in ((1, 0, 1), (5, 2, 3), (3, 0, 2)):
                    then(v.tensor_scalar(tmp, norm, thr[:, t:t + 1], None, ALU.is_gt))
                    then(v.copy_predicated(leaf[low], tmp.bitcast(I32), leaf[high]))
                then(v.tensor_tensor(tmp, leaf[0], norm, ALU.subtract))
                then(v.tensor_tensor(tmp, tmp, norm, ALU.add))
                then(v.tensor_tensor(tmp, tmp, scale, ALU.mult))
                v.tensor_tensor(w, tmp, delta, ALU.add).then_inc(S["w2_ready"], 1)

            dve.wait_ge(S["blk_set"], 3)
            for hf in range(2):
                dve.wait_ge(S["t_gate"], hf + 1)
                v.tensor_tensor(tb[:, 0, :], ring[0][0:LR, :], blk[:, :], ALU.mult).then_inc(S["tb_gate"], 1)
                dve.wait_ge(S["t_up"], hf + 1)
                v.tensor_tensor(tb[:, 1, :], ring[1][0:LR, :], blk[:, :], ALU.mult).then_inc(S["tb_up"], 1)
                for m in range(FC):
                    n = hf * FC + m
                    r = rows(m)
                    e = e_sb[0:r, n % 2, :]
                    dve.wait_ge(S["exp_g"], n + 1)
                    v.tensor_scalar(e, e, 1.0, None, ALU.add).then_inc(S["inv_g"], 1)
                    dve.wait_ge(S["inv_g"], 2 * n + 1)
                    v.reciprocal(r_sb[0:r, :], e).then_inc(S["inv_g"], 1)
                    dve.wait_ge(S["inv_g"], 2 * n + 2)
                    v.tensor_tensor(e, gate_ps[n % 2][0:r, :], r_sb[0:r, :], ALU.mult).then_inc(S["gated"], 1)
                    dve.wait_ge(S["gated"], n + 1)
                    dve.wait_ge(S["gate_up"], 2 * n + 2)
                    if m == 0 and hf:
                        dve.wait_ge(S["down"], HALF)
                    v.tensor_tensor(act[0:r, m, :], e, up_ps[n % 2][0:r, :], ALU.mult).then_inc(S["act_set"], 1)
                    if hf == 0 and m % 2 == 0 and m < 2 * C:
                        weight2(m // 2)
                dve.wait_ge(S["t_down"], hf + 1)
                v.tensor_tensor(tb[:, 2, :], ring[0][0:LR, :], blk[:, :], ALU.mult).then_inc(S["tb_down"], 1)
                if hf == 0:
                    dve.wait_ge(S["x_in"], 16)
                for j in range(HALF):
                    b = hf * HALF + j
                    dve.wait_ge(S["down"], b + 1)
                    v.tensor_tensor(x_sb[:, b, :], x_sb[:, b, :], down_ps[b % 2], ALU.add).then_inc(S["x1_added"], 1)

            for b in range(B):
                dve.wait_ge(S["x1h"], b + 1)
                v.tensor_tensor(xl[:, b, :, :], ring[b % 2][:, :].rearrange("p (c t) -> p c t", c=C),
                                xh[:, b, :, :].bitcast(F32), ALU.subtract).then_inc(S["x1l"], 1)

            def split_wqkv(u, c):
                dve.wait_ge(S["wqkv_h"], u.heads(C, c + 1))
                v.tensor_tensor(wl[:, c, :], stage[:, c % 2, :], wh[:, c, :].bitcast(F32), ALU.subtract
                                ).then_inc(S["wqkv_l"], 1)

            def split_wo(u, h):
                dve.wait_ge(S["wo_h"], u.heads(REP, h + 1))
                v.tensor_tensor(wol[:, h, :], stage[:, h % 2, 0:HID], woh[:, h, :].bitcast(F32), ALU.subtract
                                ).then_inc(S["wo_l"], 1)

            def mask_max(u, h):
                dve.wait_ge(S["score"], u.count(REP, h + 1))
                if u.turn is not None or u.k * REP + h >= 2:
                    dve.wait_ge(S["exped"], u.count(REP, h - 1))
                dve.sem_inc(S["max_begun"], 1)
                v.tensor_tensor_reduce(out=s_sb[:, h % 2, :].rearrange("p (s k) -> p s k", s=2),
                                       in0=score_ps[h % 2][:, :, 0:SPLIT],
                                       in1=mask[:, u.seq, :].rearrange("p (s k) -> p s k", s=2),
                                       scale=1.0, scalar=LOWEST, op0=ALU.add, op1=ALU.max,
                                       accum_out=top[:, h:h + 1]).then_inc(S["topped"], 1)
                dve.wait_ge(S["topped"], u.count(REP, h + 1))
                if h == 0:
                    dve.wait_ge(S["q_pow"], u.count(1, 1))
                if u.turn is not None or u.k >= 1:
                    dve.wait_ge(S["exped"], u.count(REP, h + 1 - REP))
                v.tensor_scalar(bias[:, h:h + 1], top[:, h:h + 1], rstd[:, u.k % 2, h:h + 1], -1.0,
                                ALU.mult, ALU.mult).then_inc(S["biased"], 1)

            def normalise(u, h):
                dve.wait_ge(S["exped"], u.count(REP, h + 1))
                v.reciprocal(inv[:, h:h + 1], total[:, h:h + 1]).then_inc(S["inverted"], 1)
                dve.wait_ge(S["inverted"], u.count(REP, h + 1))
                v.tensor_scalar(p_sb[:, u.k % 2, h, :], p_sb[:, u.k % 2, h, :], inv[:, h:h + 1], None, ALU.mult
                                ).then_inc(S["normed"], 1)

            def step(u):
                n, pp = u + 1, u + -2
                after = n.turn is not None or n.k > 0
                par = n.k % 2
                if u.k == -1:
                    for c in range(C):
                        split_wqkv(n, c)
                    for h in range(REP):
                        split_wo(n, h)
                elif u.seq == 7 and n.exists():
                    for c in (2, 3):
                        split_wqkv(n, c)
                if pp.exists():
                    dve.wait_ge(S["oh"], pp.count(1, 1))
                    v.tensor_tensor(oTl[:, :], o_ps[:, :], oTh[:, :].bitcast(F32), ALU.subtract).then_inc(S["ol"], 1)
                if u.exists():
                    mask_max(u, 0)
                if pp.exists():
                    dve.wait_ge(S["y"], pp.count(1, 1))
                    v.tensor_tensor(x_sb[:, pp.seq, :], x_sb[:, pp.seq, :], proj_ps[:, :], ALU.add
                                    ).then_inc(S["y_added"], 1)
                if u.exists():
                    mask_max(u, 1)
                    normalise(u, 0)
                if n.exists():
                    dve.wait_ge(S["q_copied"], n.count(1, 1))
                    if after:
                        dve.wait_ge(S["qT"], n.count(1, 0))
                    v.tensor_tensor(q_cos[:, :].rearrange("p (h d) -> p h d", h=REP),
                                    q_sb[:, :].rearrange("p (h d) -> p h d", h=REP),
                                    rope_tab[:, 0, n.seq, :].unsqueeze(1).to_broadcast([P, REP, D]),
                                    ALU.mult).then_inc(S["qcos"], 1)
                    dve.wait_ge(S["q_sq"], n.count(1, 1))
                    if n.turn is not None or n.k >= 2:
                        dve.wait_ge(S["q_pow"], n.count(1, -1))
                    v.tensor_reduce(var[:, par, 0:REP], sq_q[:, :].rearrange("p (h d) -> p h d", h=REP), AX_X, ALU.add
                                    ).then_inc(S["q_ss"], 1)
                    dve.wait_ge(S["q_ss"], n.count(1, 1))
                    v.tensor_scalar(var[:, par, 0:REP], var[:, par, 0:REP], 1.0 / D, EPS, ALU.mult, ALU.add
                                    ).then_inc(S["q_var"], 1)
                if u.exists():
                    normalise(u, 1)
                if u.seq == 1 and u.k > 1 and u.exists():
                    for h in range(REP):
                        split_wo(u, h)
                if u.exists():
                    mask_max(u, 2)
                if n.exists():
                    dve.wait_ge(S["qsin"], n.count(2, 2))
                    dve.wait_ge(S["qcos"], n.count(1, 1))
                    v.tensor_tensor(q_cos[:, :], q_cos[:, :], q_sin[:, :], ALU.add).then_inc(S["qrope"], 1)
                    dve.wait_ge(S["k_copied"], n.count(1, 1))
                    if after:
                        dve.wait_ge(S["knT"], n.count(1, 0))
                    v.tensor_tensor(k_cos[:, :], k_sb[:, :], rope_tab[:, 2, n.seq, :], ALU.mult).then_inc(S["kcos"], 1)
                    dve.wait_ge(S["k_sq"], n.count(1, 1))
                    if n.turn is not None or n.k >= 2:
                        dve.wait_ge(S["k_pow"], n.count(1, -1))
                    v.tensor_reduce(var[:, par, REP:REP + 1], sq_k[:, :], AX_X, ALU.add).then_inc(S["k_ss"], 1)
                    dve.wait_ge(S["k_ss"], n.count(1, 1))
                    v.tensor_scalar(var[:, par, REP:REP + 1], var[:, par, REP:REP + 1], 1.0 / D, EPS, ALU.mult, ALU.add
                                    ).then_inc(S["k_var"], 1)
                    dve.wait_ge(S["ksin"], n.count(2, 2))
                    v.tensor_tensor(k_cos[:, :], k_cos[:, :], k_sin[:, :], ALU.add).then_inc(S["ksum"], 1)
                if u.exists():
                    normalise(u, 2)
                if n.exists():
                    dve.wait_ge(S["ksum"], n.count(1, 1))
                    dve.wait_ge(S["k_pow"], n.count(1, 1))
                    v.tensor_scalar(k_cos[:, :], k_cos[:, :], rstd[:, par, REP:REP + 1], None, ALU.mult
                                    ).then_inc(S["krope"], 1)
                    dve.wait_ge(S["kch"], n.count(1, 1))
                    v.tensor_tensor(kTl[:, par, 0:L], ring[1][:, :], kTh[:, par, 0:L].bitcast(F32), ALU.subtract
                                    ).then_inc(S["kcl"], 1)
                if u.exists():
                    mask_max(u, 3)
                if n.exists():
                    dve.wait_ge(S["qh"], n.count(1, 1))
                    v.tensor_tensor(qTl[:, par, :], ring[0][:, :], qTh[:, par, :].bitcast(F32), ALU.subtract
                                    ).then_inc(S["ql"], 1)
                    dve.wait_ge(S["knh"], n.count(1, 1))
                    v.tensor_tensor(kTl[:, par, L:KEYS], ring[1][:, 0:T], kTh[:, par, L:KEYS].bitcast(F32), ALU.subtract
                                    ).then_inc(S["knl"], 1)
                if u.exists():
                    normalise(u, 3)
                if u.seq == 6 and (u + 2).exists():
                    for c in (0, 1):
                        split_wqkv(u + 2, c)

            run_steps(dve, step)

            def add3(b):
                dve.wait_ge(S["l2_done"], b + 1)
                v.tensor_tensor(x_sb[:, b, :], x_sb[:, b, :], down_ps[0], ALU.add).then_inc(S["x3_added"], 1)

            def add4(b):
                dve.wait_ge(S["l3_done"], b + 1)
                dve.wait_ge(S["x3_added"], b + 1)
                v.tensor_tensor(x_sb[:, b, :], x_sb[:, b, :], down_ps[1], ALU.add).then_inc(S["x4_added"], 1)

            dve.wait_ge(S["y_added"], UNITS)
            for b in range(B):
                add3(b)
                if b:
                    add4(b - 1)
            add4(B - 1)


def kernel(**inputs):
    import numpy as _np
    import concourse.bacc as _bacc
    from concourse import mybir as _mybir
    from concourse.bass_utils import run_bass_kernel_spmd as _run

    g = {k: _np.asarray(v) for k, v in inputs.items()}

    def blocks(w):
        *lead, k, n = w.shape
        return _np.moveaxis(w.reshape(*lead, k // P, P, n), -3, -2)

    def lora_in(a):
        return blocks(a[0].transpose(0, 2, 1))

    whole = (FC - 1) * P
    ad = g["L0_cond_A_down"][0].transpose(0, 2, 1)
    wq = g["L1_cond_Wq"].T.reshape(HID, HK, QW)
    wk = g["L1_cond_Wk"].T.reshape(HID, HK, D)
    wv = g["L1_cond_Wv"].T.reshape(HID, HK, D)
    arrays = {
        "x": g["x"],
        "xT": blocks(g["x"].reshape(B * T, HID).T),
        "pages": g["itok_Bx16_0_63"],
        "ad0": g["itok_B_2_6"],
        "ad3": g["itok_B_3_7"],
        "lens": g["itok_B_207_1644"],
        "code": g["condB_codebook"],
        "inv_freq": (_np.float32(1.0) / _np.power(_np.float32(10000.0), _np.arange(0, D, 2, dtype=_np.float32) / _np.float32(D))),
        "WgT": blocks(g["L0_cond_W_gate"].T),
        "WuT": blocks(g["L0_cond_W_up"].T),
        "WdT": g["L0_cond_W_down"].T,
        "AgT": lora_in(g["L0_cond_A_gate"]),
        "AuT": lora_in(g["L0_cond_A_up"]),
        "BgT": g["L0_cond_B_gate"][0].transpose(0, 2, 1),
        "BuT": g["L0_cond_B_up"][0].transpose(0, 2, 1),
        "AdT": blocks(ad[:, :whole]),
        "AdTt": ad[:, whole:],
        "BdT": g["L0_cond_B_down"][0].transpose(0, 2, 1),
        "Wqkv": blocks(_np.concatenate([wq, wk, wv], axis=2).transpose(1, 0, 2)),
        "WoT": g["L1_cond_Wo"].T.reshape(HK, REP, D, HID).transpose(0, 2, 1, 3),
        "qw": g["L1_cond_q_norm_w"],
        "kw": g["L1_cond_k_norm_w"],
        "k_cache": g["L1_cond_k_cache"],
        "v_cache": g["L1_cond_v_cache"],
        "W2T": blocks(g["L2_cond_weight"].T),
        "slT": g["L2_cond_scale_log"][:, :, 0].T,
        "la": g["L2_cond_lora_A"],
        "lbT": g["L2_cond_lora_B"].T,
        "W3T": blocks(g["L3_cond_weight"].transpose(0, 2, 1)),
    }
    arrays = {f"in_{k}": _np.ascontiguousarray(a) for k, a in arrays.items()}
    nc = _bacc.Bacc("TRN2", target_bir_lowering=False, num_devices=1)
    ins = {k[3:]: nc.dram_tensor(k, a.shape, _mybir.dt.from_np(a.dtype), kind="ExternalInput").ap()
           for k, a in arrays.items()}
    out = nc.dram_tensor("out", (B, T, HID), F32, kind="ExternalOutput").ap()
    cond_resid_kernel(nc, ins, out)
    r = _run(nc, [arrays], core_ids=[0])
    return r.results[0]["out"]
```

```python
from contextlib import ExitStack

import numpy as np

import concourse.bass as bass
from concourse import mybir

F32 = mybir.dt.float32
F32R = mybir.dt.float32r
BF16 = mybir.dt.bfloat16
I32 = mybir.dt.int32
ALU = mybir.AluOpType
ACT = mybir.ActivationFunctionType
AX_X = mybir.AxisListType.X

P = 128
B, T, HID = 8, 128, 512
C = HID // P
F = 1376
FC = 11
FTAIL = F - (FC - 1) * P
RANK = 16
HALF = 4
HT = HALF * T
LR = HALF * RANK
D, HQ, HK = 128, 32, 8
REP = HQ // HK
NPP, PSIZE = 16, 32
L = NPP * PSIZE
LC = L // P
KEYS = L + T
KC = KEYS // P
SPLIT = KEYS // 2
QW = REP * D
QKV = QW + 2 * D
DEPTH = 4
UNITS = HK * B
LORA2 = 64
NCODE = 8
EPS = 1e-06
SCALE = 1.0 / float(np.sqrt(D))
NEG = -1e30
TWO_PI = 6.283185307179586
PI_A = 6.28125
PI_B = float(np.float32(TWO_PI - PI_A).view(np.uint32) & np.uint32(0xFFFFF000))
PI_B = float(np.uint32(PI_B).view(np.float32))
PI_C = float(np.float32(TWO_PI - PI_A - PI_B))
ROUND = 12582912.0
PI_IN = 3.1415925
LOWEST = -3.0e38


class Unit:

    def __init__(self, turn, k):
        self.turn, self.k = turn, k

    def __add__(self, n):
        return Unit(self.turn, self.k + n)

    def exists(self):
        return self.turn is not None or 0 <= self.k < UNITS

    def back(self, n):
        return self.turn is not None or self.k >= n

    def new_head(self):
        return self.k % B == 0 and self.exists() and (self.turn is not None or self.k > 0)

    @property
    def seq(self):
        return self.k % B

    @property
    def head(self):
        return self.k // B if self.turn is None else self.turn + self.k // B

    def count(self, per, n):
        return self.k * per + n if self.turn is None else self.turn * (B * per) + (self.k * per + n)

    def heads(self, per, n):
        return (self.k // B) * per + n if self.turn is None else self.turn * per + ((self.k // B) * per + n)


def run_steps(engine, step):
    for k in range(DEPTH):
        step(Unit(None, k))
    with engine.Fori(0, HK - 1) as turn:
        for k in range(DEPTH, DEPTH + B):
            step(Unit(turn, k))
    for k in range(UNITS - B + DEPTH, UNITS + DEPTH - 1):
        step(Unit(None, k))


def staged(u, kind, c):
    n = c // 2 + 1 + (2 if kind == "out" else 0)
    return u.heads(4 * 16, 16 * n)


def p_slot(u, h):
    return 2 * (u.k % 2) + h if h < 2 else 2 + h


def rows(m):
    return P if m < FC - 1 else FTAIL


def cond_resid_kernel(nc, ins, out):
    ctx = ExitStack()
    with ctx:
        def dram(name, shape):
            return nc.dram_tensor(name, shape, F32, kind="Internal").ap()

        def sem(name):
            return ctx.enter_context(nc.semaphore(name))

        def keep(name, shape, dt=F32):
            return ctx.enter_context(nc.sbuf_tensor(name, shape, dt))

        k_pages = dram("k_pages", (B, L, HK, D))
        v_pages = dram("v_pages", (B, L, HK, D))
        w2_dram = dram("w2_dram", (P, C, HID))

        sc0 = ctx.enter_context(nc.psum_tensor("sc0", [P, 2, 512], F32))
        sc1 = ctx.enter_context(nc.psum_tensor("sc1", [P, 2, 512], F32))
        ring0 = ctx.enter_context(nc.psum_tensor("ring0", [P, 512], F32))
        ring1 = ctx.enter_context(nc.psum_tensor("ring1", [P, 512], F32))
        o_ps = ctx.enter_context(nc.psum_tensor("o_ps", [P, 512], F32))
        proj_ps = ctx.enter_context(nc.psum_tensor("proj_ps", [P, 512], F32))
        score_ps = [sc0, sc1]
        ring = [ring0, ring1]
        gate_ps = [sc0[:, 0, :], sc0[:, 1, :]]
        up_ps = [sc1[:, 0, :], sc1[:, 1, :]]
        down_ps = [o_ps[:, :], proj_ps[:, :]]

        x_sb = keep("x_sb", [P, B, HID])
        rope_tab = keep("rope_tab", [P, 4, B, D])
        mask = keep("mask", [P, B, KEYS], BF16)
        ident = keep("ident", [P, P])
        half_neg = keep("half_neg", [P, 8])
        idx = keep("idx", [1, B * NPP + 2 * B], I32)

        l0 = ExitStack()

        def l0_sb(name, shape, dt=F32):
            return l0.enter_context(nc.sbuf_tensor(name, shape, dt))

        wg = l0_sb("wg", [P, C, F])
        wu = l0_sb("wu", [P, C, F])
        xT0 = l0_sb("xT0", [P, C, HT])
        lbg = l0_sb("lbg", [LR, F])
        lbu = l0_sb("lbu", [LR, F])
        lag = l0_sb("lag", [P, 2, C, LR])
        lau = l0_sb("lau", [P, 2, C, LR])
        act = l0_sb("act", [P, FC, HT])
        wd = l0_sb("wd", [P, FC, HID])
        lad = l0_sb("lad", [P, 2, FC, LR])
        lbd = l0_sb("lbd", [LR, 2, HID])
        blk = l0_sb("blk", [LR, HT])
        tb = l0_sb("tb", [LR, 3, HT])
        e_sb = l0_sb("e_sb", [P, 2, HT])
        r_sb = l0_sb("r_sb", [P, HT])
        prep = l0_sb("prep", [P, 9, HID])
        l2a = l0_sb("l2a", [LORA2, HID])
        l2b = l0_sb("l2b", [LORA2, HID])
        small = l0_sb("small", [P, 64])
        len_i = l0_sb("len_i", [P, B], I32)
        pos_i = l0_sb("pos_i", [P, B], I32)
        key_i = r_sb[:, :].bitcast(I32)
        nw = l0_sb("nw", [P, 3, D])
        l0.close()

        l1 = ExitStack()

        def l1_sb(name, shape, dt=F32):
            return l1.enter_context(nc.sbuf_tensor(name, shape, dt))

        xh = l1_sb("xh", [P, B, C, T], F32R)
        xl = l1_sb("xl", [P, B, C, T], F32R)
        wh = l1_sb("wh", [P, C, QKV], F32R)
        wl = l1_sb("wl", [P, C, QKV], F32R)
        stage = l1_sb("stage", [P, 2, QKV])
        k_raw = l1_sb("k_raw", [P, LC, D])
        v_raw = l1_sb("v_raw", [P, LC, D])
        vh = l1_sb("vh", [P, 2, LC, D], F32R)
        vl = l1_sb("vl", [P, 2, LC, D], F32R)
        vnh = l1_sb("vnh", [P, 4, D], F32R)
        vnl = l1_sb("vnl", [P, 4, D], F32R)
        woh = l1_sb("woh", [P, REP, HID], F32R)
        wol = l1_sb("wol", [P, REP, HID], F32R)
        q_sb = l1_sb("q_sb", [P, QW])
        k_sb = l1_sb("k_sb", [P, D])
        sq_q = l1_sb("sq_q", [P, QW])
        sq_k = l1_sb("sq_k", [P, D])
        q_cos = l1_sb("q_cos", [P, QW])
        q_sin = l1_sb("q_sin", [P, QW])
        k_cos = l1_sb("k_cos", [P, D])
        k_sin = l1_sb("k_sin", [P, D])
        qTh = l1_sb("qTh", [P, 2, QW], F32R)
        qTl = l1_sb("qTl", [P, 2, QW], F32R)
        kTh = l1_sb("kTh", [P, 2, KEYS], F32R)
        kTl = l1_sb("kTl", [P, 2, KEYS], F32R)
        p_sb = l1_sb("p_sb", [P, 6, KEYS])
        pTh = l1_sb("pTh", [P, KC, QW], F32R)
        pTl = l1_sb("pTl", [P, KC, QW], F32R)
        oTh = l1_sb("oTh", [P, QW], F32R)
        oTl = l1_sb("oTl", [P, QW], F32R)
        var = l1_sb("var", [P, 2, 8])
        rstd = l1_sb("rstd", [P, 2, 8])
        top = l1_sb("top", [P, 8])
        bias = l1_sb("bias", [P, 8])
        total = l1_sb("total", [P, 8])
        inv = l1_sb("inv", [P, 8])
        l1.close()

        l2 = ExitStack()

        def l2_sb(name, shape, dt=F32):
            return l2.enter_context(nc.sbuf_tensor(name, shape, dt))

        w2 = l2_sb("w2", [P, C, HID])
        w3 = l2_sb("w3", [P, 2, C, HID])
        x2T = l2_sb("x2T", [P, 2, C, T])
        x3T = l2_sb("x3T", [P, 2, C, T])
        l2.close()

        names = """idx_in x_in xT_in xT_in2 lbg_in2 lbu_in2 lad_in lbg_in lbu_in lbd_in wd_in l2_in code_in nw_in len_in
        ident_set iota_set blk_set const_set w2_put w2_in w2_ready delta delta_copied scale_exp w2_loaded
        t_gate t_up tb_gate tb_up gate_up exp_g ln_g sigmoid gated act_set t_down tb_down down x1_added
        step_done ang_ready sin_ready rope_ready mask_ready x1T x1h x1l wqkv_h wqkv_l wo_h wo_l
        q_done kv_done q_copied k_copied q_sq k_sq q_ss k_ss q_var k_var q_pow k_pow
        qcos qsin qrope kcos ksin ksum krope kcT qT knT kch qh knh kcl ql knl
        score max_begun topped biased exped inverted normed_v normed_s pt pth ptl pv
        vh_set vl_set vnh_set vnl_set oh ol y y_added
        x2T_done x2T_copied l2_done x3_added x3T_done x3T_copied l3_done x4_added stored""".split()
        S = {n: sem(n) for n in names}
        w_in = [sem(f"w_in_{n}") for n in range(8)]
        lag_in = [sem(f"lag_in_{n}") for n in range(2)]
        lau_in = [sem(f"lau_in_{n}") for n in range(2)]
        page_in = [sem(f"page_in_{b}") for b in range(B)]
        stage_in = [sem(f"stage_in_{n}") for n in range(2)]
        k_load = sem("k_load")
        v_load = sem("v_load")
        w3_load = [sem(f"w3_load_{n}") for n in range(2)]

        block = ctx.enter_context(nc.Block())
        FQ = F // 4

        @block.sync
        def _(sp):
            def load(dst, src, s):
                sp.dma_start(dst, src).then_inc(s, 16)

            load(idx[:, 0:B * NPP], ins["pages"].rearrange("(a b) n -> a (b n)", a=1), S["idx_in"])
            load(idx[:, B * NPP:B * NPP + B], ins["ad0"].rearrange("(a b) -> a b", a=1), S["idx_in"])
            load(idx[:, B * NPP + B:], ins["ad3"].rearrange("(a b) -> a b", a=1), S["idx_in"])
            load(xT0[:, :, :], ins["xT"][:, :, 0:HT], S["xT_in"])
            sp.wait_ge(S["idx_in"], 48)

            def adapter(b):
                return sp.value_load(idx[0:1, B * NPP + b:B * NPP + b + 1], min_val=0, max_val=15)

            def lora_gate_up(hf):
                for j in range(HALF):
                    r = slice(j * RANK, (j + 1) * RANK)
                    a = adapter(hf * HALF + j)
                    load(lag[:, hf, :, r], ins["AgT"][bass.ds(a, 1), :, :, :].rearrange("a p c r -> (a p) c r"), lag_in[hf])
                    load(lau[:, hf, :, r], ins["AuT"][bass.ds(a, 1), :, :, :].rearrange("a p c r -> (a p) c r"), lau_in[hf])
                    if hf == 0:
                        load(lbg[r, :], ins["BgT"][bass.ds(a, 1), :, :].rearrange("a r f -> (a r) f"), S["lbg_in"])
                        load(lbu[r, :], ins["BuT"][bass.ds(a, 1), :, :].rearrange("a r f -> (a r) f"), S["lbu_in"])

            def piece(n):
                load(wg[:, :, n * FQ:(n + 1) * FQ], ins["WgT"][:, :, n * FQ:(n + 1) * FQ], w_in[2 * n])
                load(wu[:, :, n * FQ:(n + 1) * FQ], ins["WuT"][:, :, n * FQ:(n + 1) * FQ], w_in[2 * n + 1])

            piece(0)
            lora_gate_up(0)
            for n in range(1, 4):
                piece(n)
            lora_gate_up(1)
            for b in range(B):
                hf, j = b // HALF, b % HALF
                r = slice(j * RANK, (j + 1) * RANK)
                a = adapter(b)
                load(lad[:, hf, 0:FC - 1, r], ins["AdT"][bass.ds(a, 1), :, :, :].rearrange("a p c r -> (a p) c r"), S["lad_in"])
                load(lad[0:FTAIL, hf, FC - 1, r], ins["AdTt"][bass.ds(a, 1), :, :].rearrange("a p r -> (a p) r"), S["lad_in"])
                load(lbd[r, hf, :], ins["BdT"][bass.ds(a, 1), :, :].rearrange("a r f -> (a r) f"), S["lbd_in"])
            load(wd[:, 0:FC - 1, :], ins["WdT"][0:(FC - 1) * P, :].rearrange("(c p) n -> p c n", p=P), S["wd_in"])
            load(wd[0:FTAIL, FC - 1, :], ins["WdT"][(FC - 1) * P:, :], S["wd_in"])
            load(x_sb[:, :, :], ins["x"].rearrange("b t n -> t b n"), S["x_in"])
            for b in range(B):
                for j in range(NPP):
                    n = b * NPP + j
                    pg = sp.value_load(idx[0:1, n:n + 1], min_val=0, max_val=63)
                    for src, dst in (("k_cache", k_pages), ("v_cache", v_pages)):
                        load(dst[b, j * PSIZE:(j + 1) * PSIZE, :, :].rearrange("s h d -> s (h d)"),
                             ins[src][bass.ds(pg, 1), :, :, :].rearrange("a s h d -> (a s) (h d)"), page_in[b])

            def of_head(pages, u):
                v = pages[u.seq, :, :, :].rearrange("(c p) h d -> p c (h d)", p=P)
                return v[:, :, bass.ds(u.head * D, D)]

            def load_k(u):
                if u.turn is None and u.k < B or u.turn is not None:
                    sp.wait_ge(page_in[u.seq], 2 * NPP * 16)
                if u.turn is not None or u.k >= 1:
                    sp.wait_ge(S["kcT"], u.count(1, 0))
                sp.dma_start(k_raw[:, :, :], of_head(k_pages, u)).then_inc(k_load, 16)

            def load_v(u):
                if u.turn is not None or u.k >= 1:
                    sp.wait_ge(S["vl_set"], u.count(1, 0))
                sp.dma_start(v_raw[:, :, :], of_head(v_pages, u)).then_inc(v_load, 16)

            def load_wqkv(u, c):
                sp.dma_start(stage[:, c % 2, :],
                             ins["Wqkv"][bass.ds(u.head, 1), :, c, :].rearrange("a p n -> (a p) n")
                             ).then_inc(stage_in[c % 2], 16)

            def load_wo(u, h):
                sp.dma_start(stage[:, h % 2, 0:HID],
                             ins["WoT"][bass.ds(u.head, 1), :, h, :].rearrange("a p n -> (a p) n")
                             ).then_inc(stage_in[h % 2], 16)

            first = Unit(None, 0)
            sp.wait_ge(S["down"], B)
            sp.wait_ge(S["w2_put"], 16 * C)
            for c in range(2):
                load_wqkv(first, c)
            load_k(first)
            for c in range(2, C):
                sp.wait_ge(S["wqkv_l"], c - 1)
                load_wqkv(first, c)
            load_v(first)
            for h in range(REP):
                sp.wait_ge(S["wqkv_l" if h < 2 else "wo_l"], h + 3 if h < 2 else h - 1)
                load_wo(first, h)

            def load_out(u, h):
                if u.new_head():
                    if h < 2:
                        sp.wait_ge(S["wqkv_l"], u.heads(C, h + 3))
                    else:
                        sp.wait_ge(S["wo_l"], u.heads(REP, h - 1))
                    load_wo(u, h)

            def load_in(u, c):
                if u.new_head():
                    if c < 2:
                        sp.wait_ge(S["wo_l"], (u + -1).heads(REP, c + 3))
                    else:
                        sp.wait_ge(S["wqkv_l"], u.heads(C, c - 1))
                    load_wqkv(u, c)

            def step(u):
                load_out(u + -3, 3)
                load_out(u + -1, 0)
                if u.exists() and (u.turn is not None or u.k > 0):
                    load_k(u)
                load_in(u + 4, 0)
                load_out(u + -1, 1)
                if (u + -1).exists() and (u.turn is not None or u.k > 1):
                    load_v(u + -1)
                load_in(u + 1, 2)
                load_in(u + 1, 3)
                load_in(u + 4, 1)
                load_out(u + -1, 2)

            run_steps(sp, step)

            sp.wait_ge(S["kv_done"], UNITS)
            load(w2[:, :, :], w2_dram, S["w2_loaded"])
            for b in range(B):
                if b >= 2:
                    sp.wait_ge(S["l3_done"], b - 1)
                a = sp.value_load(idx[0:1, B * NPP + B + b:B * NPP + B + b + 1], min_val=0, max_val=7)
                load(w3[:, b % 2, :, :], ins["W3T"][bass.ds(a, 1), :, :, :].rearrange("a p c n -> (a p) c n"), w3_load[b % 2])
            for b in range(B):
                sp.wait_ge(S["x4_added"], b + 1)
                load(out[b, :, :], x_sb[:, b, :], S["stored"])
            sp.wait_ge(S["stored"], 16 * B)

        @block.gpsimd
        def _(pool):
            pool.memset(ident[:, :], 0.0).then_inc(S["ident_set"], 1)
            pool.memset(blk[:, :], 0.5).then_inc(S["blk_set"], 1)
            pool.wait_ge(S["ident_set"], 1)
            pool.affine_select(out=ident[:, :], in_=ident[:, :], compare_op=ALU.not_equal, fill=1.0,
                               base=0, pattern=[[-1, P]], channel_multiplier=1).then_inc(S["ident_set"], 1)
            v = blk[:, :].rearrange("p (j t) -> p j t", j=HALF)
            pool.wait_ge(S["blk_set"], 1)
            pool.affine_select(out=v, in_=v, compare_op=ALU.is_ge, fill=0.0, base=0,
                               pattern=[[-RANK, HALF], [0, T]], channel_multiplier=1).then_inc(S["blk_set"], 1)
            pool.wait_ge(S["blk_set"], 2)
            pool.affine_select(out=v, in_=v, compare_op=ALU.is_ge, fill=0.0, base=RANK - 1,
                               pattern=[[RANK, HALF], [0, T]], channel_multiplier=-1).then_inc(S["blk_set"], 1)
            pool.memset(half_neg[:, :], -0.5).then_inc(S["const_set"], 1)
            pool.iota(pos_i[:, :], pattern=[[0, B]], base=0, channel_multiplier=1).then_inc(S["iota_set"], 1)
            pool.iota(key_i[:, :], pattern=[[1, L]], base=0, channel_multiplier=0).then_inc(S["iota_set"], 1)
            pool.dma_start(small[:, 0:NCODE], ins["code"].partition_broadcast(P)).then_inc(S["code_in"], 16)
            pool.dma_start(len_i[:, :], ins["lens"].partition_broadcast(P)).then_inc(S["len_in"], 16)
            pool.dma_start(nw[:, 0, :], ins["qw"].partition_broadcast(P)).then_inc(S["nw_in"], 16)
            pool.dma_start(nw[:, 1, :], ins["kw"].partition_broadcast(P)).then_inc(S["nw_in"], 16)
            pool.dma_start(nw[:, 2, 0:D // 2], ins["inv_freq"].partition_broadcast(P)).then_inc(S["nw_in"], 16)
            pool.dma_start(l2b[:, :], ins["lbT"]).then_inc(S["l2_in"], 16)
            pool.dma_start(l2a[:, :], ins["la"]).then_inc(S["l2_in"], 16)
            def second_half():
                pool.wait_ge(S["gate_up"], 2 * FC)
                pool.dma_start(xT0[:, :, :], ins["xT"][:, :, HT:]).then_inc(S["xT_in2"], 16)
                pool.wait_ge(S["idx_in"], 48)
                for j in range(HALF):
                    r = slice(j * RANK, (j + 1) * RANK)
                    n = B * NPP + HALF + j
                    a = pool.value_load(idx[0:1, n:n + 1], min_val=0, max_val=15)
                    pool.dma_start(lbg[r, :], ins["BgT"][bass.ds(a, 1), :, :].rearrange("a r f -> (a r) f")).then_inc(S["lbg_in2"], 16)
                    pool.dma_start(lbu[r, :], ins["BuT"][bass.ds(a, 1), :, :].rearrange("a r f -> (a r) f")).then_inc(S["lbu_in2"], 16)

            pool.wait_ge(S["rope_ready"], 4)
            pool.wait_ge(S["mask_ready"], 1)
            for g in range(C):
                if g == 2:
                    second_half()
                if g:
                    pool.wait_ge(S["w2_put"], 16 * g)
                pool.dma_start(prep[:, 0, :], ins["W2T"][:, g, :]).then_inc(S["w2_in"], 16)
                pool.dma_start(prep[:, 1, :], ins["slT"][g, :].partition_broadcast(P)).then_inc(S["w2_in"], 16)
                pool.wait_ge(S["w2_ready"], g + 1)
                pool.dma_start(w2_dram[:, g, :], prep[:, 0, :]).then_inc(S["w2_put"], 16)

            def split_v(u):
                if not u.exists():
                    return
                pool.wait_ge(S["vh_set"], u.count(1, 1))
                pool.tensor_tensor(vl[:, u.k % 2, :, :], v_raw[:, :, :], vh[:, u.k % 2, :, :].bitcast(F32), ALU.subtract
                                   ).then_inc(S["vl_set"], 1)

            def turn_and_norm(u):
                if not u.exists():
                    return
                b = u.seq
                pool.wait_ge(S["q_copied"], u.count(1, 1))
                src = q_sb[:, :].rearrange("p (h s d) -> p h s d", h=REP, s=2)
                dst = q_sin[:, :].rearrange("p (h s d) -> p h s d", h=REP, s=2)
                for s in range(2):
                    pool.tensor_tensor(
                        dst[:, :, s, :], src[:, :, 1 - s, :],
                        rope_tab[:, 1, b, s * 64:(s + 1) * 64].unsqueeze(1).to_broadcast([P, REP, 64]),
                        ALU.mult).then_inc(S["qsin"], 1)
                pool.wait_ge(S["qsin"], u.count(2, 2))
                pool.wait_ge(S["qcos"], u.count(1, 1))
                pool.tensor_tensor(q_cos[:, :], q_cos[:, :], q_sin[:, :], ALU.add).then_inc(S["qrope"], 1)
                pool.wait_ge(S["k_copied"], u.count(1, 1))
                if u.back(1):
                    pool.wait_ge(S["ksum"], u.count(1, 0))
                for s in range(2):
                    pool.tensor_tensor(k_sin[:, s * 64:(s + 1) * 64], k_sb[:, (1 - s) * 64:(2 - s) * 64],
                                       rope_tab[:, 3, b, s * 64:(s + 1) * 64], ALU.mult).then_inc(S["ksin"], 1)
                pool.wait_ge(S["k_var"], u.count(1, 1))
                if u.back(2):
                    pool.wait_ge(S["krope"], u.count(1, -1))
                pool.tensor_tensor(rstd[:, u.k % 2, REP:REP + 1], var[:, u.k % 2, REP:REP + 1], half_neg[:, 0:1],
                                   ALU.pow).then_inc(S["k_pow"], 1)
                pool.wait_ge(S["q_var"], u.count(1, 1))
                if u.back(2):
                    pool.wait_ge(S["exped"], (u + -2).count(REP, REP))
                    pool.wait_ge(S["biased"], (u + -2).count(REP, REP))
                pool.tensor_tensor(rstd[:, u.k % 2, 0:REP], var[:, u.k % 2, 0:REP], half_neg[:, 0:REP],
                                   ALU.pow).then_inc(S["q_pow"], 1)

            def step(u):
                turn_and_norm(u)
                split_v(u + -1)

            pool.wait_ge(S["const_set"], 1)
            run_steps(pool, step)

        @block.scalar
        def _(act_e):
            act_e.wait_ge(S["ang_ready"], 2)
            for n in range(2):
                act_e.activation(prep[:, 4 + n, :], prep[:, 2 + n, :], ACT.Sin).then_inc(S["sin_ready"], 1)

            def group_scale(g):
                act_e.wait_ge(S["delta"], g + 1)
                if g:
                    act_e.wait_ge(S["w2_ready"], g)
                act_e.activation(prep[:, 2, :], ring[1][:, :], ACT.Copy).then_inc(S["delta_copied"], 1)
                act_e.wait_ge(S["w2_in"], 32 * (g + 1))
                act_e.activation(prep[:, 1, :], prep[:, 1, :], ACT.Exp).then_inc(S["scale_exp"], 1)

            for hf in range(2):
                for m in range(FC):
                    n = hf * FC + m
                    act_e.wait_ge(S["gate_up"], 2 * n + 1)
                    if n >= 2:
                        act_e.wait_ge(S["act_set"], n - 1)
                    e = e_sb[0:rows(m), n % 2, :]
                    act_e.activation(e, gate_ps[n % 2][0:rows(m), :], ACT.Exp, scale=-1.0).then_inc(S["exp_g"], 1)
                    act_e.wait_ge(S["exp_g"], n + 1)
                    act_e.activation(e, e, ACT.Ln, bias=1.0).then_inc(S["ln_g"], 1)
                    act_e.wait_ge(S["ln_g"], n + 1)
                    act_e.activation(e, e, ACT.Exp, scale=-1.0).then_inc(S["sigmoid"], 1)
                    if n >= 2 and (n - 2) % 4 == 0 and (n - 2) // 4 < C:
                        group_scale((n - 2) // 4)

            for b in range(B):
                act_e.wait_ge(S["x1T"], b + 1)
                act_e.activation(xh[:, b, :, :], ring[b % 2][:, :].rearrange("p (c t) -> p c t", c=C),
                                 ACT.Copy).then_inc(S["x1h"], 1)

            def split_wqkv(u, c):
                if c == 0 and u.back(1):
                    act_e.wait_ge(S["kv_done"], u.count(1, 0))
                act_e.wait_ge(stage_in[c % 2], staged(u, "in", c))
                act_e.activation(wh[:, c, :], stage[:, c % 2, :], ACT.Copy).then_inc(S["wqkv_h"], 1)

            def split_wo(u, h):
                if h == 0 and u.back(1):
                    act_e.wait_ge(S["y"], u.count(1, 0))
                act_e.wait_ge(stage_in[h % 2], staged(u, "out", h))
                act_e.activation(woh[:, h, :], stage[:, h % 2, 0:HID], ACT.Copy).then_inc(S["wo_h"], 1)

            def new_wqkv(u, c):
                if u.new_head():
                    split_wqkv(u, c)

            def new_wo(u, h):
                if u.new_head():
                    split_wo(u, h)

            def exp(u, h):
                if not u.exists():
                    return
                act_e.wait_ge(S["biased"], u.count(REP, h + 1))
                if h == 0 and u.back(1):
                    act_e.wait_ge(S["inverted"], u.count(REP, 0))
                act_e.activation(p_sb[:, p_slot(u, h), :], p_sb[:, p_slot(u, h), :], ACT.Exp, bias=bias[:, h:h + 1],
                                 scale=rstd[:, u.k % 2, h:h + 1], accum_out=total[:, h:h + 1]
                                 ).then_inc(S["exped"], 1)

            def normalise(u, h):
                if not u.exists():
                    return
                act_e.wait_ge(S["inverted"], u.count(REP, h + 1))
                act_e.activation(p_sb[:, p_slot(u, h), :], p_sb[:, p_slot(u, h), :], ACT.Copy,
                                 scale=inv[:, h:h + 1]).then_inc(S["normed_s"], 1)

            def high_pt(u, c):
                if not u.exists():
                    return
                act_e.wait_ge(S["pt"], u.count(KC, c + 1))
                if u.back(1):
                    act_e.wait_ge(S["pv"], u.count(KC, c + 1 - KC))
                act_e.activation(pTh[:, c, :], ring[c % 2][:, :], ACT.Copy).then_inc(S["pth"], 1)

            def high_v(u):
                if not u.exists():
                    return
                act_e.wait_ge(v_load, u.count(16, 16))
                if u.back(2):
                    act_e.wait_ge(S["pv"], (u + -2).count(KC, KC))
                act_e.activation(vh[:, u.k % 2, :, :], v_raw[:, :, :], ACT.Copy).then_inc(S["vh_set"], 1)

            def high_o(u):
                if not u.exists():
                    return
                act_e.wait_ge(S["pv"], u.count(KC, KC))
                if u.back(1):
                    act_e.wait_ge(S["y"], u.count(1, 0))
                act_e.activation(oTh[:, :], o_ps[:, :], ACT.Copy).then_inc(S["oh"], 1)

            def copy_q(u):
                if not u.exists():
                    return
                act_e.wait_ge(S["q_done"], u.count(1, 1))
                if u.back(1):
                    act_e.wait_ge(S["qcos"], u.count(1, 0))
                    act_e.wait_ge(S["qsin"], u.count(2, 0))
                act_e.activation(q_sb[:, :], proj_ps[:, :], ACT.Copy).then_inc(S["q_copied"], 1)

            def square_q(u):
                if not u.exists():
                    return
                act_e.wait_ge(S["q_copied"], u.count(1, 1))
                if u.back(1):
                    act_e.wait_ge(S["q_ss"], u.count(1, 0))
                act_e.activation(sq_q[:, :], q_sb[:, :], ACT.Square).then_inc(S["q_sq"], 1)

            def copy_k(u):
                if not u.exists():
                    return
                act_e.wait_ge(S["kv_done"], u.count(1, 1))
                if u.back(1):
                    act_e.wait_ge(S["kcos"], u.count(1, 0))
                    act_e.wait_ge(S["ksin"], u.count(2, 0))
                act_e.activation(k_sb[:, :], proj_ps[:, 0:D], ACT.Copy).then_inc(S["k_copied"], 1)

            def high_new_v(u):
                if not u.exists():
                    return
                act_e.wait_ge(S["kv_done"], u.count(1, 1))
                if u.back(4):
                    act_e.wait_ge(S["pv"], (u + -4).count(KC, KC))
                act_e.activation(vnh[:, u.k % 4, :], proj_ps[:, D:2 * D], ACT.Copy).then_inc(S["vnh_set"], 1)

            def square_k(u):
                if not u.exists():
                    return
                act_e.wait_ge(S["k_copied"], u.count(1, 1))
                if u.back(1):
                    act_e.wait_ge(S["k_ss"], u.count(1, 0))
                act_e.activation(sq_k[:, :], k_sb[:, :], ACT.Square).then_inc(S["k_sq"], 1)

            def slot_free(u):
                if u.back(2):
                    act_e.wait_ge(S["score"], (u + -2).count(REP, REP))

            def high_cached_k(u):
                if not u.exists():
                    return
                slot_free(u)
                act_e.wait_ge(S["kcT"], u.count(1, 1))
                act_e.activation(kTh[:, u.k % 2, 0:L], ring[1][:, :], ACT.Copy).then_inc(S["kch"], 1)

            def high_q(u):
                if not u.exists():
                    return
                slot_free(u)
                act_e.wait_ge(S["qT"], u.count(1, 1))
                act_e.activation(qTh[:, u.k % 2, :], ring[0][:, :], ACT.Copy).then_inc(S["qh"], 1)

            def high_new_k(u):
                if not u.exists():
                    return
                slot_free(u)
                act_e.wait_ge(S["knT"], u.count(1, 1))
                act_e.activation(kTh[:, u.k % 2, L:KEYS], ring[1][:, 0:T], ACT.Copy).then_inc(S["knh"], 1)

            for c in range(C):
                split_wqkv(Unit(None, 0), c)
            for h in range(REP):
                split_wo(Unit(None, 0), h)

            def step(u):
                high_v(u + -2)
                high_o(u + -3)
                exp(u + -2, 1)
                high_q(u + -1)
                new_wqkv(u, 2)
                high_new_k(u + -1)
                exp(u + -2, 2)
                new_wqkv(u, 3)
                new_wo(u + -2, 0)
                exp(u + -2, 3)
                normalise(u + -2, 1)
                normalise(u + -2, 2)
                new_wo(u + -2, 1)
                copy_q(u)
                high_pt(u + -2, 0)
                high_pt(u + -2, 1)
                exp(u + -1, 0)
                copy_k(u)
                high_pt(u + -2, 2)
                high_new_v(u)
                new_wqkv(u + 1, 0)
                square_k(u)
                high_pt(u + -2, 3)
                new_wo(u + -2, 2)
                high_pt(u + -2, 4)
                square_q(u)
                new_wqkv(u + 1, 1)
                high_cached_k(u)
                new_wo(u + -2, 3)
            run_steps(act_e, step)

            for b in range(B):
                act_e.wait_ge(S["x2T_done"], b + 1)
                if b >= 2:
                    act_e.wait_ge(S["l2_done"], b - 1)
                act_e.activation(x2T[:, b % 2, :, :], ring[0][:, :].rearrange("p (c t) -> p c t", c=C),
                                 ACT.Copy).then_inc(S["x2T_copied"], 1)
                act_e.wait_ge(S["x3T_done"], b + 1)
                if b >= 2:
                    act_e.wait_ge(S["l3_done"], b - 1)
                act_e.activation(x3T[:, b % 2, :, :], ring[1][:, :].rearrange("p (c t) -> p c t", c=C),
                                 ACT.Copy).then_inc(S["x3T_copied"], 1)

        @block.tensor
        def _(pe):
            mm = nc.tensor.matmul
            pe.wait_ge(S["ident_set"], 2)

            def delta(g):
                if g:
                    pe.wait_ge(S["delta_copied"], g)
                else:
                    pe.wait_ge(S["l2_in"], 32)
                mm(ring[1][:, :], l2a[:, g * P:(g + 1) * P], l2b[:, :], start=True, stop=True).then_inc(S["delta"], 1)

            for hf in range(2):
                pe.wait_ge(S["xT_in2" if hf else "xT_in"], 16)
                pe.wait_ge(lag_in[hf], 16 * HALF)
                pe.wait_ge(lau_in[hf], 16 * HALF)
                if hf:
                    pe.wait_ge(S["delta_copied"], 3)
                    pe.wait_ge(S["tb_down"], 1)
                for n, (la, name) in enumerate(((lag, "t_gate"), (lau, "t_up"))):
                    for c in range(C):
                        i = mm(ring[n][0:LR, :], la[:, hf, c, :], xT0[:, c, :], start=c == 0, stop=c == C - 1)
                    i.then_inc(S[name], 1)
                pe.wait_ge(S["lbg_in2" if hf else "lbg_in"], 16 * HALF)
                pe.wait_ge(S["lbu_in2" if hf else "lbu_in"], 16 * HALF)
                for m in range(FC):
                    n = hf * FC + m
                    fs = slice(m * P, m * P + rows(m))
                    piece = min((m * P + rows(m) - 1) // FQ, 3)
                    for k, (w, lb, bank, ready) in enumerate(((wg, lbg, gate_ps, "tb_gate"), (wu, lbu, up_ps, "tb_up"))):
                        if hf == 0:
                            pe.wait_ge(w_in[2 * piece + k], 16)
                        if n >= 2:
                            pe.wait_ge(S["act_set"], n - 1)
                        for c in range(C):
                            mm(bank[n % 2][0:rows(m), :], w[:, c, fs], xT0[:, c, :], start=c == 0, stop=False)
                        if m == 0:
                            pe.wait_ge(S[ready], hf + 1)
                        mm(bank[n % 2][0:rows(m), :], lb[:, fs], tb[:, k, :], start=False, stop=True
                           ).then_inc(S["gate_up"], 1)
                    if n % 4 == 1 and n // 4 < C:
                        if n == 1:
                            pe.wait_ge(S["tb_up"], 1)
                        delta(n // 4)
                pe.wait_ge(S["act_set"], FC * (hf + 1))
                pe.wait_ge(S["lad_in"], 32 * B)
                pe.wait_ge(S["tb_gate"], hf + 1)
                for m in range(FC):
                    i = mm(ring[0][0:LR, :], lad[0:rows(m), hf, m, :], act[0:rows(m), m, :], start=m == 0, stop=m == FC - 1)
                i.then_inc(S["t_down"], 1)
                pe.wait_ge(S["wd_in"], 32)
                pe.wait_ge(S["lbd_in"], 16 * B)
                for j in range(HALF):
                    b = hf * HALF + j
                    if b >= 2:
                        pe.wait_ge(S["x1_added"], b - 1)
                    ts = slice(j * T, (j + 1) * T)
                    for m in range(FC):
                        mm(down_ps[b % 2], act[0:rows(m), m, ts], wd[0:rows(m), m, :], start=m == 0, stop=False)
                    if j == 0:
                        pe.wait_ge(S["tb_down"], hf + 1)
                    mm(down_ps[b % 2], tb[:, 2, ts], lbd[:, hf, :], start=False, stop=True).then_inc(S["down"], 1)
            for b in range(B):
                pe.wait_ge(S["x1_added"], b + 1)
                if b >= 2:
                    pe.wait_ge(S["x1l"], b - 1)
                for c in range(C):
                    i = nc.tensor.transpose(ring[b % 2][:, c * P:(c + 1) * P], x_sb[:, b, c * P:(c + 1) * P], ident[:, :])
                i.then_inc(S["x1T"], 1)

            def project(u, cols, width, name):
                b = u.seq
                if cols == 0 and u.turn is None and u.k < B:
                    pe.wait_ge(S["x1l"], b + 1)
                    pe.wait_ge(S["x1h"], b + 1)
                k = 0
                for c in range(C):
                    if cols == 0 and b == 0:
                        pe.wait_ge(S["wqkv_h"], u.heads(C, c + 1))
                        pe.wait_ge(S["wqkv_l"], u.heads(C, c + 1))
                    for a, w in ((xh, wh), (xh, wl), (xl, wh)):
                        i = mm(proj_ps[:, 0:width], a[:, b, c, :], w[:, c, cols:cols + width], start=k == 0, stop=k == 3 * C - 1)
                        k += 1
                i.then_inc(S[name], 1)

            def project_q(u):
                if not u.exists():
                    return
                if u.back(3):
                    pe.wait_ge(S["y_added"], (u + -3).count(1, 1))
                elif u.k >= 1:
                    pe.wait_ge(S["k_copied"], u.count(1, 0))
                    pe.wait_ge(S["vnl_set"], u.count(1, 0))
                else:
                    pe.wait_ge(S["x1_added"], B)
                project(u, 0, QW, "q_done")

            def project_kv(u):
                if not u.exists():
                    return
                pe.wait_ge(S["q_copied"], u.count(1, 1))
                project(u, QW, 2 * D, "kv_done")

            def scores(u, h):
                if not u.exists():
                    return
                hs = slice(h * D, (h + 1) * D)
                par = u.k % 2
                if h == 0:
                    for name in ("qh", "ql", "kch", "kcl", "knh", "knl"):
                        pe.wait_ge(S[name], u.count(1, 1))
                if h >= 2 or u.back(1):
                    pe.wait_ge(S["topped"], u.count(REP, h - 1))
                for s in range(2):
                    ks = slice(s * SPLIT, (s + 1) * SPLIT)
                    for k, (a, w) in enumerate(((qTh, kTh), (qTh, kTl), (qTl, kTh))):
                        i = mm(score_ps[h % 2][:, s, 0:SPLIT], a[:, par, hs], w[:, par, ks], start=k == 0, stop=k == 2)
                i.then_inc(S["score"], 1)

            def transpose_p(u, c):
                if not u.exists():
                    return
                if c == 0:
                    pe.wait_ge(S["normed_v"], u.count(2, 2))
                    pe.wait_ge(S["normed_s"], u.count(2, 2))
                    if (u + 1).exists():
                        pe.wait_ge(S["ql"], (u + 1).count(1, 1))
                elif c == 1:
                    if (u + 1).exists():
                        pe.wait_ge(S["knl"], (u + 1).count(1, 1))
                else:
                    pe.wait_ge(S["ptl"], u.count(KC, c - 1))
                for h in range(REP):
                    i = nc.tensor.transpose(ring[c % 2][:, h * P:(h + 1) * P], p_sb[:, p_slot(u, h), c * P:(c + 1) * P], ident[:, :])
                i.then_inc(S["pt"], 1)

            def attend(u, c):
                if not u.exists():
                    return
                pe.wait_ge(S["ptl"], u.count(KC, c + 1))
                if c == 0:
                    pe.wait_ge(S["vl_set"], u.count(1, 1))
                    pe.wait_ge(S["vnl_set"], u.count(1, 1))
                    if u.back(1):
                        pe.wait_ge(S["ol"], u.count(1, 0))
                if c < LC:
                    high, low = vh[:, u.k % 2, c, :], vl[:, u.k % 2, c, :]
                else:
                    high, low = vnh[:, u.k % 4, :], vnl[:, u.k % 4, :]
                for k, (a, w) in enumerate(((high, pTh), (high, pTl), (low, pTh))):
                    i = mm(o_ps[:, :], a, w[:, c, :], start=c == 0 and k == 0, stop=c == KC - 1 and k == 2)
                i.then_inc(S["pv"], 1)

            def output(u):
                if not u.exists():
                    return
                pe.wait_ge(S["oh"], u.count(1, 1))
                pe.wait_ge(S["ol"], u.count(1, 1))
                if (u + 2).exists():
                    pe.wait_ge(S["k_copied"], (u + 2).count(1, 1))
                    pe.wait_ge(S["vnl_set"], (u + 2).count(1, 1))
                else:
                    pe.wait_ge(S["y_added"], u.count(1, 0))
                k = 0
                for h in range(REP):
                    if u.seq == 0:
                        pe.wait_ge(S["wo_h"], u.heads(REP, h + 1))
                        pe.wait_ge(S["wo_l"], u.heads(REP, h + 1))
                    hs = slice(h * D, (h + 1) * D)
                    for a, w in ((oTh, woh), (oTh, wol), (oTl, woh)):
                        i = mm(proj_ps[:, :], a[:, hs], w[:, h, :], start=k == 0, stop=k == 3 * REP - 1)
                        k += 1
                i.then_inc(S["y"], 1)

            def transpose_keys(u):
                if not u.exists():
                    return
                pe.wait_ge(k_load, u.count(16, 16))
                if u.back(2):
                    pe.wait_ge(S["ptl"], (u + -2).count(KC, 4))
                elif u.k == 0:
                    pe.wait_ge(S["x1l"], B)
                else:
                    pe.wait_ge(S["knl"], u.count(1, 0))
                for c in range(LC):
                    i = nc.tensor.transpose(ring[1][:, c * P:(c + 1) * P], k_raw[:, c, :], ident[:, :])
                i.then_inc(S["kcT"], 1)

            def transpose_queries(u):
                if not u.exists():
                    return
                pe.wait_ge(S["qrope"], u.count(1, 1))
                if u.back(2):
                    pe.wait_ge(S["ptl"], (u + -2).count(KC, 5))
                elif u.k == 1:
                    pe.wait_ge(S["ql"], 1)
                for h in range(REP):
                    i = nc.tensor.transpose(ring[0][:, h * P:(h + 1) * P], q_cos[:, h * P:(h + 1) * P], ident[:, :])
                i.then_inc(S["qT"], 1)

            def transpose_new(u):
                if not u.exists():
                    return
                pe.wait_ge(S["krope"], u.count(1, 1))
                pe.wait_ge(S["kcl"], u.count(1, 1))
                nc.tensor.transpose(ring[1][:, 0:P], k_cos[:, :], ident[:, :]).then_inc(S["knT"], 1)

            def step(u):
                project_q(u)
                transpose_p(u + -2, 0)
                transpose_p(u + -2, 1)
                project_kv(u)
                transpose_p(u + -2, 2)
                attend(u + -2, 0)
                transpose_p(u + -2, 3)
                attend(u + -2, 1)
                transpose_p(u + -2, 4)
                attend(u + -2, 2)
                transpose_keys(u)
                attend(u + -2, 3)
                attend(u + -2, 4)
                scores(u + -1, 2)
                transpose_queries(u)
                scores(u + -1, 3)
                transpose_new(u)
                output(u + -2)
                scores(u, 0)
                scores(u, 1)

            run_steps(pe, step)

            def layer3(b):
                pe.wait_ge(w3_load[b % 2], 16 * (b // 2 + 1))
                if b >= 1:
                    pe.wait_ge(S["x4_added"], b)
                for c in range(C):
                    i = mm(down_ps[1], x3T[:, b % 2, c, :], w3[:, b % 2, c, :], start=c == 0, stop=c == C - 1)
                i.then_inc(S["l3_done"], 1)

            def turn_x(b, slot, name, waits):
                for w, v in waits:
                    pe.wait_ge(S[w], v)
                for c in range(C):
                    i = nc.tensor.transpose(ring[slot][:, c * P:(c + 1) * P], x_sb[:, b, c * P:(c + 1) * P], ident[:, :])
                i.then_inc(S[name], 1)

            pe.wait_ge(S["ptl"], UNITS * KC)
            pe.wait_ge(S["w2_loaded"], 16)
            turn_x(0, 0, "x2T_done", (("y_added", UNITS),))
            for b in range(B):
                pe.wait_ge(S["x2T_copied"], b + 1)
                if b >= 1:
                    pe.wait_ge(S["x3_added"], b)
                for c in range(C):
                    i = mm(down_ps[0], x2T[:, b % 2, c, :], w2[:, c, :], start=c == 0, stop=c == C - 1)
                i.then_inc(S["l2_done"], 1)
                if b >= 1:
                    pe.wait_ge(S["x3T_copied"], b)
                    layer3(b - 1)
                turn_x(b, 1, "x3T_done", (("x3_added", b + 1),))
                if b + 1 < B:
                    turn_x(b + 1, 0, "x2T_done", ())
            pe.wait_ge(S["x3T_copied"], B)
            layer3(B - 1)

        @block.vector
        def _(dve):
            v = nc.vector
            chain = [0]

            def then(ins):
                chain[0] += 1
                ins.then_inc(S["step_done"], 1)
                dve.wait_ge(S["step_done"], chain[0])

            lens = small[:, 16:24]
            pos = small[:, 24:32]
            ang, turns = prep[:, 0, :], prep[:, 1, :]
            dve.wait_ge(S["len_in"], 16)
            dve.wait_ge(S["iota_set"], 2)
            dve.wait_ge(S["nw_in"], 48)
            v.tensor_copy(lens, len_i[:, :])
            then(v.tensor_copy(pos, pos_i[:, :]))
            then(v.tensor_tensor(pos, pos, lens, ALU.add))
            for b in range(B):
                i = v.tensor_scalar(ang[:, b * 64:(b + 1) * 64], nw[:, 2, 0:64], pos[:, b:b + 1], None, ALU.mult)
            then(i)
            for n, quarter in enumerate((0.0, 0.25)):
                red = prep[:, 2 + n, :]
                then(v.tensor_scalar(turns, ang, 1.0 / TWO_PI, quarter, ALU.mult, ALU.add))
                then(v.tensor_scalar(turns, turns, ROUND, None, ALU.add))
                then(v.tensor_scalar(turns, turns, ROUND, None, ALU.subtract))
                then(v.scalar_tensor_tensor(red, turns, -PI_A, ang, ALU.mult, ALU.add))
                then(v.scalar_tensor_tensor(red, turns, -PI_B, red, ALU.mult, ALU.add))
                then(v.scalar_tensor_tensor(red, turns, -PI_C, red, ALU.mult, ALU.add))
                then(v.tensor_scalar(red, red, quarter * TWO_PI, PI_IN, ALU.add, ALU.min))
                v.tensor_scalar(red, red, -PI_IN, None, ALU.max).then_inc(S["ang_ready"], 1)
            then(v.tensor_scalar(nw[:, 0, :], nw[:, 0, :], SCALE, None, ALU.mult))
            key = prep[:, 6, :]
            then(v.tensor_copy(key, key_i))
            v.memset(mask[:, :, L:KEYS], 0.0)
            for b in range(B):
                i = v.tensor_scalar(mask[:, b, 0:L], key, lens[:, b:b + 1], NEG, ALU.is_ge, ALU.mult)
            i.then_inc(S["mask_ready"], 1)
            sin = prep[:, 4, :].rearrange("p (b j) -> p b j", b=B)
            cos = prep[:, 5, :].rearrange("p (b j) -> p b j", b=B)
            dve.wait_ge(S["sin_ready"], 2)

            def wide(n, s):
                return nw[:, n, s * 64:(s + 1) * 64].unsqueeze(1).to_broadcast([P, B, 64])

            for n in range(2):
                v.tensor_tensor(rope_tab[:, 2 * n, :, 0:64], cos, wide(n, 0), ALU.mult)
                v.tensor_tensor(rope_tab[:, 2 * n, :, 64:128], cos, wide(n, 1), ALU.mult).then_inc(S["rope_ready"], 1)
                v.tensor_tensor(rope_tab[:, 2 * n + 1, :, 64:128], sin, wide(n, 0), ALU.mult)
                v.scalar_tensor_tensor(rope_tab[:, 2 * n + 1, :, 0:64], sin, -1.0, wide(n, 1),
                                       ALU.mult, ALU.mult).then_inc(S["rope_ready"], 1)

            dve.wait_ge(S["code_in"], 16)
            code, cmax, thr = small[:, 0:NCODE], small[:, 33:34], small[:, 8:8 + NCODE - 1]
            then(v.tensor_reduce(cmax, code, AX_X, ALU.max, apply_absolute_value=True))
            then(v.tensor_scalar(cmax, cmax, 1e-8, None, ALU.max))
            then(v.reciprocal(cmax, cmax))
            then(v.tensor_scalar(code, code, cmax, None, ALU.mult))
            then(v.tensor_tensor(thr, small[:, 0:NCODE - 1], small[:, 1:NCODE], ALU.add))
            then(v.tensor_scalar(thr, thr, 0.5, None, ALU.mult))

            def weight2(g, part):
                w, scale, delta, tmp, norm = (prep[:, n, :] for n in range(5))
                leaf = [prep[:, 5 + n, :] for n in range(4)]
                if part == 0:
                    dve.wait_ge(S["delta_copied"], g + 1)
                    dve.wait_ge(S["scale_exp"], g + 1)
                    then(v.tensor_scalar(delta, delta, 0.5, None, ALU.mult))
                    then(v.tensor_tensor(w, w, delta, ALU.add))
                    then(v.reciprocal(tmp, scale))
                    then(v.tensor_tensor(norm, w, tmp, ALU.mult))
                elif part < 3:
                    for n in (2 * part - 2, 2 * part - 1):
                        t = thr[:, 2 * n:2 * n + 1]
                        v.tensor_scalar(leaf[n], norm, t, code[:, 2 * n + 1:2 * n + 2], ALU.is_gt, ALU.mult)
                        then(v.tensor_scalar(tmp, norm, t, code[:, 2 * n:2 * n + 1], ALU.is_le, ALU.mult))
                        then(v.tensor_tensor(leaf[n], leaf[n], tmp, ALU.add))
                else:
                    for t, low, high in ((1, 0, 1), (5, 2, 3), (3, 0, 2)):
                        then(v.tensor_scalar(tmp, norm, thr[:, t:t + 1], None, ALU.is_gt))
                        then(v.copy_predicated(leaf[low], tmp.bitcast(I32), leaf[high]))
                    then(v.tensor_tensor(tmp, leaf[0], norm, ALU.subtract))
                    then(v.tensor_tensor(tmp, tmp, norm, ALU.add))
                    then(v.tensor_tensor(tmp, tmp, scale, ALU.mult))
                    v.tensor_tensor(w, tmp, delta, ALU.add).then_inc(S["w2_ready"], 1)

            dve.wait_ge(S["blk_set"], 3)
            for hf in range(2):
                dve.wait_ge(S["t_gate"], hf + 1)
                v.tensor_tensor(tb[:, 0, :], ring[0][0:LR, :], blk[:, :], ALU.mult).then_inc(S["tb_gate"], 1)
                dve.wait_ge(S["t_up"], hf + 1)
                v.tensor_tensor(tb[:, 1, :], ring[1][0:LR, :], blk[:, :], ALU.mult).then_inc(S["tb_up"], 1)
                for m in range(FC):
                    n = hf * FC + m
                    r = rows(m)
                    e = e_sb[0:r, n % 2, :]
                    dve.wait_ge(S["sigmoid"], n + 1)
                    v.tensor_tensor(e, gate_ps[n % 2][0:r, :], e, ALU.mult).then_inc(S["gated"], 1)
                    dve.wait_ge(S["gated"], n + 1)
                    dve.wait_ge(S["gate_up"], 2 * n + 2)
                    if m == 0 and hf:
                        dve.wait_ge(S["down"], HALF)
                    v.tensor_tensor(act[0:r, m, :], e, up_ps[n % 2][0:r, :], ALU.mult).then_inc(S["act_set"], 1)
                    if 3 <= n < 3 + 4 * C:
                        weight2((n - 3) // 4, (n - 3) % 4)
                dve.wait_ge(S["t_down"], hf + 1)
                v.tensor_tensor(tb[:, 2, :], ring[0][0:LR, :], blk[:, :], ALU.mult).then_inc(S["tb_down"], 1)
                if hf == 0:
                    dve.wait_ge(S["x_in"], 16)
                for j in range(HALF):
                    b = hf * HALF + j
                    dve.wait_ge(S["down"], b + 1)
                    v.tensor_tensor(x_sb[:, b, :], x_sb[:, b, :], down_ps[b % 2], ALU.add).then_inc(S["x1_added"], 1)

            for b in range(B):
                dve.wait_ge(S["x1h"], b + 1)
                v.tensor_tensor(xl[:, b, :, :], ring[b % 2][:, :].rearrange("p (c t) -> p c t", c=C),
                                xh[:, b, :, :].bitcast(F32), ALU.subtract).then_inc(S["x1l"], 1)

            def split_wqkv(u, c):
                dve.wait_ge(S["wqkv_h"], u.heads(C, c + 1))
                v.tensor_tensor(wl[:, c, :], stage[:, c % 2, :], wh[:, c, :].bitcast(F32), ALU.subtract
                                ).then_inc(S["wqkv_l"], 1)

            def split_wo(u, h):
                dve.wait_ge(S["wo_h"], u.heads(REP, h + 1))
                v.tensor_tensor(wol[:, h, :], stage[:, h % 2, 0:HID], woh[:, h, :].bitcast(F32), ALU.subtract
                                ).then_inc(S["wo_l"], 1)

            def new_wqkv(u, c):
                if u.new_head():
                    split_wqkv(u, c)

            def new_wo(u, h):
                if u.new_head():
                    split_wo(u, h)

            def mask_max(u, h):
                if not u.exists():
                    return
                dve.wait_ge(S["score"], u.count(REP, h + 1))
                ago = 2 if h < 2 else 1
                if u.back(ago):
                    dve.wait_ge(S["pt"], (u + -ago).count(KC, KC))
                dve.sem_inc(S["max_begun"], 1)
                v.tensor_tensor_reduce(out=p_sb[:, p_slot(u, h), :].rearrange("p (s k) -> p s k", s=2),
                                       in0=score_ps[h % 2][:, :, 0:SPLIT],
                                       in1=mask[:, u.seq, :].rearrange("p (s k) -> p s k", s=2),
                                       scale=1.0, scalar=LOWEST, op0=ALU.add, op1=ALU.max,
                                       accum_out=top[:, h:h + 1]).then_inc(S["topped"], 1)
                dve.wait_ge(S["topped"], u.count(REP, h + 1))
                if h == 0:
                    dve.wait_ge(S["q_pow"], u.count(1, 1))
                if u.back(1):
                    dve.wait_ge(S["exped"], u.count(REP, h + 1 - REP))
                v.tensor_scalar(bias[:, h:h + 1], top[:, h:h + 1], rstd[:, u.k % 2, h:h + 1], -1.0,
                                ALU.mult, ALU.mult).then_inc(S["biased"], 1)

            def invert(u, h):
                if not u.exists():
                    return
                dve.wait_ge(S["exped"], u.count(REP, h + 1))
                if (h == 1 or h == 2) and u.back(1):
                    dve.wait_ge(S["normed_s"], u.count(2, h - 2))
                v.reciprocal(inv[:, h:h + 1], total[:, h:h + 1]).then_inc(S["inverted"], 1)

            def normalise(u, h):
                if not u.exists():
                    return
                dve.wait_ge(S["inverted"], u.count(REP, h + 1))
                v.tensor_scalar(p_sb[:, p_slot(u, h), :], p_sb[:, p_slot(u, h), :], inv[:, h:h + 1], None, ALU.mult
                                ).then_inc(S["normed_v"], 1)

            def low_pt(u, c):
                if not u.exists():
                    return
                dve.wait_ge(S["pth"], u.count(KC, c + 1))
                v.tensor_tensor(pTl[:, c, :], ring[c % 2][:, :], pTh[:, c, :].bitcast(F32), ALU.subtract
                                ).then_inc(S["ptl"], 1)

            def low_o(u):
                if not u.exists():
                    return
                dve.wait_ge(S["oh"], u.count(1, 1))
                v.tensor_tensor(oTl[:, :], o_ps[:, :], oTh[:, :].bitcast(F32), ALU.subtract).then_inc(S["ol"], 1)

            def add_y(u):
                if not u.exists():
                    return
                dve.wait_ge(S["y"], u.count(1, 1))
                v.tensor_tensor(x_sb[:, u.seq, :], x_sb[:, u.seq, :], proj_ps[:, :], ALU.add).then_inc(S["y_added"], 1)

            def cos_q(u):
                if not u.exists():
                    return
                dve.wait_ge(S["q_copied"], u.count(1, 1))
                if u.back(1):
                    dve.wait_ge(S["qT"], u.count(1, 0))
                v.tensor_tensor(q_cos[:, :].rearrange("p (h d) -> p h d", h=REP),
                                q_sb[:, :].rearrange("p (h d) -> p h d", h=REP),
                                rope_tab[:, 0, u.seq, :].unsqueeze(1).to_broadcast([P, REP, D]),
                                ALU.mult).then_inc(S["qcos"], 1)

            def mean_square_q(u):
                if not u.exists():
                    return
                par = u.k % 2
                dve.wait_ge(S["q_sq"], u.count(1, 1))
                if u.back(2):
                    dve.wait_ge(S["q_pow"], u.count(1, -1))
                v.tensor_reduce(var[:, par, 0:REP], sq_q[:, :].rearrange("p (h d) -> p h d", h=REP), AX_X, ALU.add
                                ).then_inc(S["q_ss"], 1)
                dve.wait_ge(S["q_ss"], u.count(1, 1))
                v.tensor_scalar(var[:, par, 0:REP], var[:, par, 0:REP], 1.0 / D, EPS, ALU.mult, ALU.add
                                ).then_inc(S["q_var"], 1)

            def low_cached_k(u):
                if not u.exists():
                    return
                dve.wait_ge(S["kch"], u.count(1, 1))
                v.tensor_tensor(kTl[:, u.k % 2, 0:L], ring[1][:, :], kTh[:, u.k % 2, 0:L].bitcast(F32), ALU.subtract
                                ).then_inc(S["kcl"], 1)

            def cos_k(u):
                if not u.exists():
                    return
                dve.wait_ge(S["k_copied"], u.count(1, 1))
                if u.back(1):
                    dve.wait_ge(S["knT"], u.count(1, 0))
                v.tensor_tensor(k_cos[:, :], k_sb[:, :], rope_tab[:, 2, u.seq, :], ALU.mult).then_inc(S["kcos"], 1)

            def mean_square_k(u):
                if not u.exists():
                    return
                par = u.k % 2
                dve.wait_ge(S["k_sq"], u.count(1, 1))
                if u.back(2):
                    dve.wait_ge(S["k_pow"], u.count(1, -1))
                v.tensor_reduce(var[:, par, REP:REP + 1], sq_k[:, :], AX_X, ALU.add).then_inc(S["k_ss"], 1)
                dve.wait_ge(S["k_ss"], u.count(1, 1))
                v.tensor_scalar(var[:, par, REP:REP + 1], var[:, par, REP:REP + 1], 1.0 / D, EPS, ALU.mult, ALU.add
                                ).then_inc(S["k_var"], 1)

            def low_new_v(u):
                if not u.exists():
                    return
                dve.wait_ge(S["vnh_set"], u.count(1, 1))
                v.tensor_tensor(vnl[:, u.k % 4, :], proj_ps[:, D:2 * D], vnh[:, u.k % 4, :].bitcast(F32), ALU.subtract
                                ).then_inc(S["vnl_set"], 1)

            def sum_k(u):
                if not u.exists():
                    return
                dve.wait_ge(S["ksin"], u.count(2, 2))
                dve.wait_ge(S["kcos"], u.count(1, 1))
                v.tensor_tensor(k_cos[:, :], k_cos[:, :], k_sin[:, :], ALU.add).then_inc(S["ksum"], 1)

            def scale_k(u):
                if not u.exists():
                    return
                dve.wait_ge(S["ksum"], u.count(1, 1))
                dve.wait_ge(S["k_pow"], u.count(1, 1))
                v.tensor_scalar(k_cos[:, :], k_cos[:, :], rstd[:, u.k % 2, REP:REP + 1], None, ALU.mult
                                ).then_inc(S["krope"], 1)

            def low_q(u):
                if not u.exists():
                    return
                dve.wait_ge(S["qh"], u.count(1, 1))
                v.tensor_tensor(qTl[:, u.k % 2, :], ring[0][:, :], qTh[:, u.k % 2, :].bitcast(F32), ALU.subtract
                                ).then_inc(S["ql"], 1)

            def low_new_k(u):
                if not u.exists():
                    return
                dve.wait_ge(S["knh"], u.count(1, 1))
                v.tensor_tensor(kTl[:, u.k % 2, L:KEYS], ring[1][:, 0:T], kTh[:, u.k % 2, L:KEYS].bitcast(F32), ALU.subtract
                                ).then_inc(S["knl"], 1)

            for c in range(C):
                split_wqkv(Unit(None, 0), c)
            for h in range(REP):
                split_wo(Unit(None, 0), h)

            def step(u):
                mean_square_q(u + -1)
                invert(u + -2, 2)
                normalise(u + -2, 0)
                invert(u + -2, 3)
                new_wo(u + -2, 0)
                normalise(u + -2, 3)
                mask_max(u + -1, 0)
                new_wo(u + -2, 1)
                mask_max(u + -1, 1)
                low_pt(u + -2, 0)
                low_pt(u + -2, 1)
                cos_q(u)
                cos_k(u)
                low_pt(u + -2, 2)
                invert(u + -1, 0)
                low_new_v(u)
                new_wqkv(u + 1, 0)
                low_pt(u + -2, 3)
                mean_square_k(u)
                low_pt(u + -2, 4)
                sum_k(u)
                new_wqkv(u + 1, 1)
                new_wo(u + -2, 2)
                low_cached_k(u)
                new_wo(u + -2, 3)
                scale_k(u)
                low_o(u + -2)
                mask_max(u + -1, 2)
                low_q(u)
                invert(u + -1, 1)
                low_new_k(u)
                new_wqkv(u + 1, 2)
                mask_max(u + -1, 3)
                add_y(u + -2)
                new_wqkv(u + 1, 3)

            run_steps(dve, step)

            def add3(b):
                dve.wait_ge(S["l2_done"], b + 1)
                v.tensor_tensor(x_sb[:, b, :], x_sb[:, b, :], down_ps[0], ALU.add).then_inc(S["x3_added"], 1)

            def add4(b):
                dve.wait_ge(S["l3_done"], b + 1)
                dve.wait_ge(S["x3_added"], b + 1)
                v.tensor_tensor(x_sb[:, b, :], x_sb[:, b, :], down_ps[1], ALU.add).then_inc(S["x4_added"], 1)

            dve.wait_ge(S["y_added"], UNITS)
            for b in range(B):
                add3(b)
                if b:
                    add4(b - 1)
            add4(B - 1)


def kernel(**inputs):
    import numpy as _np
    import concourse.bacc as _bacc
    from concourse import mybir as _mybir
    from concourse.bass_utils import run_bass_kernel_spmd as _run

    g = {k: _np.asarray(v) for k, v in inputs.items()}

    def blocks(w):
        *lead, k, n = w.shape
        return _np.moveaxis(w.reshape(*lead, k // P, P, n), -3, -2)

    def lora_in(a):
        return blocks(a[0].transpose(0, 2, 1))

    whole = (FC - 1) * P
    ad = g["L0_cond_A_down"][0].transpose(0, 2, 1)
    wq = g["L1_cond_Wq"].T.reshape(HID, HK, QW)
    wk = g["L1_cond_Wk"].T.reshape(HID, HK, D)
    wv = g["L1_cond_Wv"].T.reshape(HID, HK, D)
    arrays = {
        "x": g["x"],
        "xT": blocks(g["x"].reshape(B * T, HID).T),
        "pages": g["itok_Bx16_0_63"],
        "ad0": g["itok_B_2_6"],
        "ad3": g["itok_B_3_7"],
        "lens": g["itok_B_207_1644"],
        "code": g["condB_codebook"],
        "inv_freq": _np.float32(1.0) / _np.power(10000.0, _np.arange(0, D, 2) / D).astype(_np.float32),
        "WgT": blocks(g["L0_cond_W_gate"].T),
        "WuT": blocks(g["L0_cond_W_up"].T),
        "WdT": g["L0_cond_W_down"].T,
        "AgT": lora_in(g["L0_cond_A_gate"]),
        "AuT": lora_in(g["L0_cond_A_up"]),
        "BgT": g["L0_cond_B_gate"][0].transpose(0, 2, 1),
        "BuT": g["L0_cond_B_up"][0].transpose(0, 2, 1),
        "AdT": blocks(ad[:, :whole]),
        "AdTt": ad[:, whole:],
        "BdT": g["L0_cond_B_down"][0].transpose(0, 2, 1),
        "Wqkv": blocks(_np.concatenate([wq, wk, wv], axis=2).transpose(1, 0, 2)),
        "WoT": g["L1_cond_Wo"].T.reshape(HK, REP, D, HID).transpose(0, 2, 1, 3),
        "qw": g["L1_cond_q_norm_w"],
        "kw": g["L1_cond_k_norm_w"],
        "k_cache": g["L1_cond_k_cache"],
        "v_cache": g["L1_cond_v_cache"],
        "W2T": blocks(g["L2_cond_weight"].T),
        "slT": g["L2_cond_scale_log"][:, :, 0].T,
        "la": g["L2_cond_lora_A"],
        "lbT": g["L2_cond_lora_B"].T,
        "W3T": blocks(g["L3_cond_weight"].transpose(0, 2, 1)),
    }
    arrays = {f"in_{k}": _np.ascontiguousarray(a) for k, a in arrays.items()}
    nc = _bacc.Bacc("TRN2", target_bir_lowering=False, num_devices=1)
    ins = {k[3:]: nc.dram_tensor(k, a.shape, _mybir.dt.from_np(a.dtype), kind="ExternalInput").ap()
           for k, a in arrays.items()}
    out = nc.dram_tensor("out", (B, T, HID), F32, kind="ExternalOutput").ap()
    cond_resid_kernel(nc, ins, out)
    r = _run(nc, [arrays], core_ids=[0])
    return r.results[0]["out"]
```

```python
from contextlib import ExitStack

import numpy as np

import concourse.bass as bass
from concourse import mybir

F32 = mybir.dt.float32
F32R = mybir.dt.float32r
BF16 = mybir.dt.bfloat16
I32 = mybir.dt.int32
ALU = mybir.AluOpType
ACT = mybir.ActivationFunctionType
AX_X = mybir.AxisListType.X

P = 128
B, T, HID = 8, 128, 512
C = HID // P
F = 1376
FC = 11
FTAIL = F - (FC - 1) * P
RANK = 16
HALF = 4
HT = HALF * T
FP = FC * P
CH = FC + 1
D, HQ, HK = 128, 32, 8
REP = HQ // HK
NPP, PSIZE = 16, 32
L = NPP * PSIZE
LC = L // P
KEYS = L + T
KC = KEYS // P
SPLIT = KEYS // 2
QW = REP * D
QKV = QW + 2 * D
DEPTH = 4
UNITS = HK * B
LORA2 = 64
NCODE = 8
EPS = 1e-06
SCALE = 1.0 / float(np.sqrt(D))
NEG = -1e30
TWO_PI = 6.283185307179586
PI_A = 6.28125
PI_B = float(np.float32(TWO_PI - PI_A).view(np.uint32) & np.uint32(0xFFFFF000))
PI_B = float(np.uint32(PI_B).view(np.float32))
PI_C = float(np.float32(TWO_PI - PI_A - PI_B))
ROUND = 12582912.0
PI_IN = 3.1415925
LOWEST = -3.0e38


class Unit:

    def __init__(self, turn, k):
        self.turn, self.k = turn, k

    def __add__(self, n):
        return Unit(self.turn, self.k + n)

    def exists(self):
        return self.turn is not None or 0 <= self.k < UNITS

    def back(self, n):
        return self.turn is not None or self.k >= n

    def new_head(self):
        return self.k % B == 0 and self.exists() and (self.turn is not None or self.k > 0)

    @property
    def seq(self):
        return self.k % B

    @property
    def head(self):
        return self.k // B if self.turn is None else self.turn + self.k // B

    def count(self, per, n):
        return self.k * per + n if self.turn is None else self.turn * (B * per) + (self.k * per + n)

    def heads(self, per, n):
        return (self.k // B) * per + n if self.turn is None else self.turn * per + ((self.k // B) * per + n)


def run_steps(engine, step):
    for k in range(DEPTH):
        step(Unit(None, k))
    with engine.Fori(0, HK - 1) as turn:
        for k in range(DEPTH, DEPTH + B):
            step(Unit(turn, k))
    for k in range(UNITS - B + DEPTH, UNITS + DEPTH - 1):
        step(Unit(None, k))


def staged(u, kind, c):
    n = c // 2 + 1 + (2 if kind == "out" else 0)
    return u.heads(4 * 16, 16 * n)


def p_slot(u, h):
    return 2 * (u.k % 2) + h if h < 2 else 2 + h


def rows(m):
    return P if m < FC - 1 else FTAIL


def cond_resid_kernel(nc, ins, out):
    ctx = ExitStack()
    with ctx:
        def dram(name, shape):
            return nc.dram_tensor(name, shape, F32, kind="Internal").ap()

        def sem(name):
            return ctx.enter_context(nc.semaphore(name))

        def keep(name, shape, dt=F32):
            return ctx.enter_context(nc.sbuf_tensor(name, shape, dt))

        k_pages = dram("k_pages", (B, L, HK, D))
        v_pages = dram("v_pages", (B, L, HK, D))
        w2_dram = dram("w2_dram", (P, C, HID))

        sc0 = ctx.enter_context(nc.psum_tensor("sc0", [P, 2, 512], F32))
        sc1 = ctx.enter_context(nc.psum_tensor("sc1", [P, 2, 512], F32))
        ring0 = ctx.enter_context(nc.psum_tensor("ring0", [P, 512], F32))
        ring1 = ctx.enter_context(nc.psum_tensor("ring1", [P, 512], F32))
        o_ps = ctx.enter_context(nc.psum_tensor("o_ps", [P, 512], F32))
        proj_ps = ctx.enter_context(nc.psum_tensor("proj_ps", [P, 512], F32))
        score_ps = [sc0, sc1]
        ring = [ring0, ring1]
        gate_ps = [sc0[:, 0, :], sc0[:, 1, :]]
        up_ps = [sc1[:, 0, :], sc1[:, 1, :]]
        seq_ps = [o_ps[:, :], proj_ps[:, :], sc0[:, 0, :], sc1[:, 0, :]]
        down_ps = [o_ps[:, :], proj_ps[:, :]]

        x_sb = keep("x_sb", [P, B, HID])
        rope_tab = keep("rope_tab", [P, 4, B, D])
        mask = keep("mask", [P, B, KEYS], BF16)
        ident = keep("ident", [P, P])
        half_neg = keep("half_neg", [P, 8])
        idx = keep("idx", [1, B * NPP + 2 * B], I32)

        l0 = ExitStack()

        def l0_sb(name, shape, dt=F32):
            return l0.enter_context(nc.sbuf_tensor(name, shape, dt))

        xT_h = l0_sb("xT_h", [P, C, HT], F32R)
        xT_l = l0_sb("xT_l", [P, C, HT], F32R)
        w_raw = l0_sb("w_raw", [P, 2, 2 * C * P])
        w_h = l0_sb("w_h", [P, 2, 2, C + 1, P], F32R)
        w_l = l0_sb("w_l", [P, 2, 2, C + 1, P], F32R)
        lb = l0_sb("lb", [P, 2, FP])
        act_h = l0_sb("act_h", [P, FC, HT], F32R)
        act_l = l0_sb("act_l", [P, FC, HT], F32R)
        lad = l0_sb("lad", [P, B, FC, RANK])
        lad_h = l0_sb("lad_h", [P, 2, P], F32R)
        lad_l = l0_sb("lad_l", [P, 2, P], F32R)
        blk = l0_sb("blk", [P, 2 * HT], BF16)
        tb_h = l0_sb("tb_h", [P, 3, HT], F32R)
        tb_l = l0_sb("tb_l", [P, 3, HT], F32R)
        e_sb = l0_sb("e_sb", [P, 2, HT])
        wd_raw = l0_sb("wd_raw", [P, 3, HID])
        lbd = l0_sb("lbd", [P, HID])
        wd_h = l0_sb("wd_h", [P, 2, HID], F32R)
        wd_l = l0_sb("wd_l", [P, 2, HID], F32R)
        prep = l0_sb("prep", [P, 9, HID])
        l2a = l0_sb("l2a", [LORA2, HID])
        l2b = l0_sb("l2b", [LORA2, HID])
        small = l0_sb("small", [P, 40])
        len_i = l0_sb("len_i", [P, B], I32)
        pos_i = l0_sb("pos_i", [P, B], I32)
        nw = l0_sb("nw", [P, 3, D])
        key_i = e_sb[:, 1, :].bitcast(I32)
        tb_raw = e_sb[:, 0, :]
        xT_raw = x_sb[:, HALF:, :]
        l0.close()

        l1 = ExitStack()

        def l1_sb(name, shape, dt=F32):
            return l1.enter_context(nc.sbuf_tensor(name, shape, dt))

        stage = l1_sb("stage", [P, 2, QKV])
        wh = l1_sb("wh", [P, C, QKV], F32R)
        wl = l1_sb("wl", [P, C, QKV], F32R)
        woh = l1_sb("woh", [P, REP, HID], F32R)
        wol = l1_sb("wol", [P, REP, HID], F32R)
        k_raw = l1_sb("k_raw", [P, LC, D])
        v_raw = l1_sb("v_raw", [P, LC, D])
        xh = l1_sb("xh", [P, B, C, T], F32R)
        xl = l1_sb("xl", [P, B, C, T], F32R)
        vh = l1_sb("vh", [P, 2, LC, D], F32R)
        vl = l1_sb("vl", [P, 2, LC, D], F32R)
        vnh = l1_sb("vnh", [P, 4, D], F32R)
        vnl = l1_sb("vnl", [P, 4, D], F32R)
        q_sb = l1_sb("q_sb", [P, QW])
        k_sb = l1_sb("k_sb", [P, D])
        sq_q = l1_sb("sq_q", [P, QW])
        sq_k = l1_sb("sq_k", [P, D])
        q_cos = l1_sb("q_cos", [P, QW])
        q_sin = l1_sb("q_sin", [P, QW])
        k_cos = l1_sb("k_cos", [P, D])
        k_sin = l1_sb("k_sin", [P, D])
        qTh = l1_sb("qTh", [P, 2, QW], F32R)
        qTl = l1_sb("qTl", [P, 2, QW], F32R)
        kTh = l1_sb("kTh", [P, 2, KEYS], F32R)
        kTl = l1_sb("kTl", [P, 2, KEYS], F32R)
        p_sb = l1_sb("p_sb", [P, 6, KEYS])
        pTh = l1_sb("pTh", [P, KC, QW], F32R)
        pTl = l1_sb("pTl", [P, KC, QW], F32R)
        oTh = l1_sb("oTh", [P, QW], F32R)
        oTl = l1_sb("oTl", [P, QW], F32R)
        var = l1_sb("var", [P, 2, 8])
        rstd = l1_sb("rstd", [P, 2, 8])
        top = l1_sb("top", [P, 8])
        bias = l1_sb("bias", [P, 8])
        total = l1_sb("total", [P, 8])
        inv = l1_sb("inv", [P, 8])
        l1.close()

        l2 = ExitStack()

        def l2_sb(name, shape, dt=F32):
            return l2.enter_context(nc.sbuf_tensor(name, shape, dt))

        w2_raw = l2_sb("w2_raw", [P, C, HID])
        w3_raw = l2_sb("w3_raw", [P, 2, C, HID])
        x2T_h = l2_sb("x2T_h", [P, 2, C * T], F32R)
        x2T_l = l2_sb("x2T_l", [P, 2, C * T], F32R)
        x3T_h = l2_sb("x3T_h", [P, 2, C * T], F32R)
        x3T_l = l2_sb("x3T_l", [P, 2, C * T], F32R)
        w3_h = l2_sb("w3_h", [P, 2, C, HID], F32R)
        w2_h = l2_sb("w2_h", [P, C, HID], F32R)
        w2_l = l2_sb("w2_l", [P, C, HID], F32R)
        w3_l = l2_sb("w3_l", [P, 2, C, HID], F32R)
        l2.close()

        names = """idx_in xT_in lad_in lb_in lbd_in zero_set w_zero wd_zero xh_set xl_set w_hi w_lo wd_hi wd_lo wd_used lad_hi lad_lo t_masked t_hi t_lo act_f act_hi act_lo key_copied l2_in code_in nw_in len_in
        ident_set iota_set blk_set const_set w2_put w2_in w2_ready delta delta_copied scale_exp w2_loaded
        t_done gate_up exp_g ln_g sigmoid gated lad_used down x1_added
        step_done ang_ready sin_ready rope_ready mask_ready x1T x1h x1l wqkv_h wqkv_l wo_h wo_l
        q_done kv_done q_copied k_copied q_sq k_sq q_ss k_ss q_var k_var q_pow k_pow
        qcos qsin qrope kcos ksin ksum krope kcT qT knT kch qh knh kcl ql knl
        score max_begun topped biased exped inverted normed_v normed_s pt pth ptl pv
        vh_set vl_set vnh_set vnl_set oh ol y y_added
        w2_hi w2_lo w3_hi w3_lo x2T_done x2T_hi x2T_lo l2_done x3_added x3T_done x3T_hi x3T_lo l3_done x4_added stored""".split()
        S = {n: sem(n) for n in names}
        w_in = [sem(f"w_in_{n}") for n in range(2)]
        wd_in = [sem(f"wd_in_{n}") for n in range(3)]
        x_in = [sem(f"x_in_{n}") for n in range(2)]
        k_page_in = [sem(f"k_page_in_{b}") for b in range(B)]
        v_page_in = [sem(f"v_page_in_{b}") for b in range(B)]
        stage_in = [sem(f"stage_in_{n}") for n in range(2)]
        k_load = sem("k_load")
        v_load = sem("v_load")
        w3_load = [sem(f"w3_load_{n}") for n in range(2)]

        block = ctx.enter_context(nc.Block())

        def w_count(q):
            whole, n = divmod(q, CH)
            if q % 2 == 0:
                return (whole * (B + CH // 2 - 1) + B + n // 2) * 16
            return (whole * (CH // 2) + n // 2 + 1) * 16

        def wd_block(q):
            whole, n = divmod(q, CH)
            return whole * FC + n

        def wd_source(q):
            return lbd[:, :] if q % CH == FC else wd_raw[:, wd_block(q) % 3, :]

        def lora_factors(slot):
            return w_raw[:, slot, :].rearrange("p (b k c r) -> p k b c r", k=2, b=B, c=C)

        def w_blocks(slot):
            return w_raw[:, slot, :].rearrange("p (k c n) -> p k c n", k=2, c=C)

        @block.sync
        def _(sp):
            def load(dst, src, s):
                sp.dma_start(dst, src).then_inc(s, 16)

            load(idx[:, 0:B * NPP], ins["pages"].rearrange("(a b) n -> a (b n)", a=1), S["idx_in"])
            load(idx[:, B * NPP:B * NPP + B], ins["ad0"].rearrange("(a b) -> a b", a=1), S["idx_in"])
            load(idx[:, B * NPP + B:], ins["ad3"].rearrange("(a b) -> a b", a=1), S["idx_in"])
            load(xT_raw, ins["xT"][:, :, 0:HT], S["xT_in"])
            sp.wait_ge(S["idx_in"], 48)

            def adapter(b):
                return sp.value_load(idx[0:1, B * NPP + b:B * NPP + b + 1], min_val=0, max_val=15)

            def load_w(q):
                hf, n = divmod(q, CH)
                if q >= 2:
                    sp.wait_ge(S["w_lo"], q - 1)
                if n == 0:
                    for b in range(B):
                        load(w_raw[:, q % 2, b * 2 * C * RANK:(b + 1) * 2 * C * RANK],
                             ins["AguT"][bass.ds(adapter(b), 1), :, :].rearrange("a p n -> (a p) n"), w_in[q % 2])
                    return
                m = n - 1
                if m == FC - 1:
                    sp.wait_ge(S["w_zero"], hf + 1)
                if m < FC - 1:
                    load(w_raw[:, q % 2, :], ins["WguT"][m, :, :], w_in[q % 2])
                else:
                    load(w_raw[:, q % 2, :].rearrange("p (k n) -> p k n", n=P)[:, :, 0:FTAIL], ins["WguTt"], w_in[q % 2])

            def load_wd(q):
                hf, n = divmod(q, CH)
                r = wd_block(q)
                if r >= 3:
                    before = r - 3
                    sp.wait_ge(S["wd_lo"], before // FC * CH + before % FC + 1)
                if n == FC - 1:
                    sp.wait_ge(S["wd_zero"], hf + 1)
                load(wd_raw[0:rows(n), r % 3, :], ins["WdT"][n * P:n * P + rows(n), :], wd_in[r % 3])

            copied = [0]

            def copy_keys(many):
                for n in range(copied[0], min(copied[0] + many, B * NPP)):
                    b, j = divmod(n, NPP)
                    pg = sp.value_load(idx[0:1, n:n + 1], min_val=0, max_val=63)
                    load(k_pages[b, j * PSIZE:(j + 1) * PSIZE, :, :].rearrange("s h d -> s (h d)"),
                         ins["k_cache"][bass.ds(pg, 1), :, :, :].rearrange("a s h d -> (a s) (h d)"), k_page_in[b])
                copied[0] += many

            load_w(0)
            load_w(1)
            load_w(2)
            load_w(3)
            sp.wait_ge(S["xl_set"], C)
            load(xT_raw, ins["xT"][:, :, HT:], S["xT_in"])
            load(x_sb[:, 0:HALF, :], ins["x"][0:HALF].rearrange("b t n -> t b n"), x_in[0])
            for b in range(B):
                load(lbd[b * RANK:(b + 1) * RANK, :],
                     ins["BdT"][bass.ds(adapter(b), 1), :, :].rearrange("a r f -> (a r) f"), S["lbd_in"])
            for q in range(4, CH):
                load_w(q)
                copy_keys(5)
            for n in range(3):
                load_wd(n)
            load_w(CH)
            load_w(CH + 1)
            for n in range(3, FC):
                load_wd(n)
                copy_keys(1)
            sp.wait_ge(S["xl_set"], 2 * C)
            load(x_sb[:, HALF:, :], ins["x"][HALF:].rearrange("b t n -> t b n"), x_in[1])
            for q in range(CH + 2, 2 * CH):
                load_w(q)
                copy_keys(5)

            def of_head(pages, u):
                v = pages[u.seq, :, :, :].rearrange("(c p) h d -> p c (h d)", p=P)
                return v[:, :, bass.ds(u.head * D, D)]

            def load_k(u):
                if u.turn is None and u.k < B or u.turn is not None:
                    sp.wait_ge(k_page_in[u.seq], NPP * 16)
                if u.turn is not None or u.k >= 1:
                    sp.wait_ge(S["kcT"], u.count(1, 0))
                sp.dma_start(k_raw[:, :, :], of_head(k_pages, u)).then_inc(k_load, 16)

            def load_v(u):
                if u.turn is None and u.k < B or u.turn is not None:
                    sp.wait_ge(v_page_in[u.seq], NPP * 16)
                if u.turn is not None or u.k >= 1:
                    sp.wait_ge(S["vl_set"], u.count(1, 0))
                sp.dma_start(v_raw[:, :, :], of_head(v_pages, u)).then_inc(v_load, 16)

            def load_wqkv(u, c):
                sp.dma_start(stage[:, c % 2, :],
                             ins["Wqkv"][bass.ds(u.head, 1), :, c, :].rearrange("a p n -> (a p) n")
                             ).then_inc(stage_in[c % 2], 16)

            def load_wo(u, h):
                sp.dma_start(stage[:, h % 2, 0:HID],
                             ins["WoT"][bass.ds(u.head, 1), :, h, :].rearrange("a p n -> (a p) n")
                             ).then_inc(stage_in[h % 2], 16)

            first = Unit(None, 0)
            for n in range(FC):
                load_wd(CH + n)
                copy_keys(1)
                if n == 2:
                    sp.wait_ge(S["gate_up"], 4 * FC)
                    load_wqkv(first, 0)
                    load_wqkv(first, 1)
                    load_k(first)
                if n == 4:
                    for c in (2, 3):
                        sp.wait_ge(S["wqkv_l"], c - 1)
                        load_wqkv(first, c)
                    load_v(first)
                if n == 6:
                    for h in (0, 1):
                        sp.wait_ge(S["wqkv_l"], h + 3)
                        load_wo(first, h)
                if n == 8:
                    for h in (2, 3):
                        sp.wait_ge(S["wo_l"], h - 1)
                        load_wo(first, h)
            copy_keys(B * NPP)

            def load_out(u, h):
                if u.new_head():
                    if h < 2:
                        sp.wait_ge(S["wqkv_l"], u.heads(C, h + 3))
                    else:
                        sp.wait_ge(S["wo_l"], u.heads(REP, h - 1))
                    load_wo(u, h)

            def load_in(u, c):
                if u.new_head():
                    if c < 2:
                        sp.wait_ge(S["wo_l"], (u + -1).heads(REP, c + 3))
                    else:
                        sp.wait_ge(S["wqkv_l"], u.heads(C, c - 1))
                    load_wqkv(u, c)

            def step(u):
                load_out(u + -3, 3)
                load_out(u + -1, 0)
                if u.exists() and (u.turn is not None or u.k > 0):
                    load_k(u)
                load_in(u + 4, 0)
                load_out(u + -1, 1)
                if (u + -1).exists() and (u.turn is not None or u.k > 1):
                    load_v(u + -1)
                load_in(u + 1, 2)
                load_in(u + 1, 3)
                load_in(u + 4, 1)
                load_out(u + -1, 2)

            run_steps(sp, step)

            sp.wait_ge(S["kv_done"], UNITS)
            load(w2_raw[:, :, :], w2_dram, S["w2_loaded"])
            for b in range(B):
                if b >= 2:
                    sp.wait_ge(S["w3_lo"], b - 1)
                a = sp.value_load(idx[0:1, B * NPP + B + b:B * NPP + B + b + 1], min_val=0, max_val=7)
                load(w3_raw[:, b % 2, :, :], ins["W3T"][bass.ds(a, 1), :, :, :].rearrange("a p c n -> (a p) c n"), w3_load[b % 2])
            for b in range(B):
                sp.wait_ge(S["x4_added"], b + 1)
                load(out[b, :, :], x_sb[:, b, :], S["stored"])
            sp.wait_ge(S["stored"], 16 * B)

        @block.gpsimd
        def _(pool):
            pool.dma_start(len_i[:, :], ins["lens"].partition_broadcast(P)).then_inc(S["len_in"], 16)
            pool.dma_start(nw[:, 2, 0:D // 2], ins["inv_freq"].partition_broadcast(P)).then_inc(S["nw_in"], 16)
            pool.dma_start(nw[:, 0, :], ins["qw"].partition_broadcast(P)).then_inc(S["nw_in"], 16)
            pool.dma_start(nw[:, 1, :], ins["kw"].partition_broadcast(P)).then_inc(S["nw_in"], 16)
            pool.iota(pos_i[:, :], pattern=[[0, B]], base=0, channel_multiplier=1).then_inc(S["iota_set"], 1)
            pool.iota(key_i[:, :], pattern=[[1, L]], base=0, channel_multiplier=0).then_inc(S["iota_set"], 1)
            pool.memset(lb[:, :, F:], 0.0).then_inc(S["zero_set"], 1)
            pool.wait_ge(S["zero_set"], 1)
            pool.memset(lad[FTAIL:, :, FC - 1, :], 0.0).then_inc(S["zero_set"], 1)
            pool.wait_ge(S["zero_set"], 2)
            pool.memset(blk[:, :], 0.5).then_inc(S["blk_set"], 1)
            v = blk[:, :].rearrange("p (j t) -> p j t", j=B)
            pool.wait_ge(S["blk_set"], 1)
            pool.affine_select(out=v, in_=v, compare_op=ALU.is_ge, fill=0.0, base=0,
                               pattern=[[-RANK, B], [0, T]], channel_multiplier=1).then_inc(S["blk_set"], 1)
            pool.wait_ge(S["blk_set"], 2)
            pool.affine_select(out=v, in_=v, compare_op=ALU.is_ge, fill=0.0, base=RANK - 1,
                               pattern=[[RANK, B], [0, T]], channel_multiplier=-1).then_inc(S["blk_set"], 1)
            pool.memset(half_neg[:, :], -0.5).then_inc(S["const_set"], 1)
            pool.memset(ident[:, :], 0.0).then_inc(S["ident_set"], 1)
            pool.wait_ge(S["ident_set"], 1)
            pool.affine_select(out=ident[:, :], in_=ident[:, :], compare_op=ALU.not_equal, fill=1.0,
                               base=0, pattern=[[-1, P]], channel_multiplier=1).then_inc(S["ident_set"], 1)
            pool.dma_start(small[:, 0:NCODE], ins["code"].partition_broadcast(P)).then_inc(S["code_in"], 16)
            pool.wait_ge(S["idx_in"], 48)
            for b in range(B):
                n = B * NPP + b
                a = pool.value_load(idx[0:1, n:n + 1], min_val=0, max_val=15)
                pool.dma_start(lad[:, b, 0:FC - 1, :],
                               ins["AdT"][bass.ds(a, 1), :, :, :].rearrange("a p c r -> (a p) c r")).then_inc(S["lad_in"], 16)
                pool.dma_start(lad[0:FTAIL, b, FC - 1, :],
                               ins["AdTt"][bass.ds(a, 1), :, :].rearrange("a p r -> (a p) r")).then_inc(S["lad_in"], 16)
            pool.dma_start(l2b[:, :], ins["lbT"]).then_inc(S["l2_in"], 16)
            pool.dma_start(l2a[:, :], ins["la"]).then_inc(S["l2_in"], 16)
            def copy_values(first, last):
                for n in range(first, last):
                    b, j = divmod(n, NPP)
                    pg = pool.value_load(idx[0:1, n:n + 1], min_val=0, max_val=63)
                    pool.dma_start(v_pages[b, j * PSIZE:(j + 1) * PSIZE, :, :].rearrange("s h d -> s (h d)"),
                                   ins["v_cache"][bass.ds(pg, 1), :, :, :].rearrange("a s h d -> (a s) (h d)")
                                   ).then_inc(v_page_in[b], 16)

            pool.wait_ge(S["idx_in"], 48)
            pool.wait_ge(S["rope_ready"], 4)
            pool.wait_ge(S["mask_ready"], 1)
            for g in range(C):
                if g:
                    pool.wait_ge(S["w2_put"], 16 * g)
                pool.dma_start(prep[:, 0, :], ins["W2T"][:, g, :]).then_inc(S["w2_in"], 16)
                pool.dma_start(prep[:, 1, :], ins["slT"][g, :].partition_broadcast(P)).then_inc(S["w2_in"], 16)
                copy_values(g * 2 * NPP, (g + 1) * 2 * NPP)
                pool.wait_ge(S["w2_ready"], g + 1)
                pool.dma_start(w2_dram[:, g, :], prep[:, 0, :]).then_inc(S["w2_put"], 16)

            def split_v(u):
                if not u.exists():
                    return
                pool.wait_ge(S["vh_set"], u.count(1, 1))
                pool.tensor_tensor(vl[:, u.k % 2, :, :], v_raw[:, :, :], vh[:, u.k % 2, :, :].bitcast(F32), ALU.subtract
                                   ).then_inc(S["vl_set"], 1)

            def turn_and_norm(u):
                if not u.exists():
                    return
                b = u.seq
                pool.wait_ge(S["q_copied"], u.count(1, 1))
                src = q_sb[:, :].rearrange("p (h s d) -> p h s d", h=REP, s=2)
                dst = q_sin[:, :].rearrange("p (h s d) -> p h s d", h=REP, s=2)
                for s in range(2):
                    pool.tensor_tensor(
                        dst[:, :, s, :], src[:, :, 1 - s, :],
                        rope_tab[:, 1, b, s * 64:(s + 1) * 64].unsqueeze(1).to_broadcast([P, REP, 64]),
                        ALU.mult).then_inc(S["qsin"], 1)
                pool.wait_ge(S["qsin"], u.count(2, 2))
                pool.wait_ge(S["qcos"], u.count(1, 1))
                pool.tensor_tensor(q_cos[:, :], q_cos[:, :], q_sin[:, :], ALU.add).then_inc(S["qrope"], 1)
                pool.wait_ge(S["k_copied"], u.count(1, 1))
                if u.back(1):
                    pool.wait_ge(S["ksum"], u.count(1, 0))
                for s in range(2):
                    pool.tensor_tensor(k_sin[:, s * 64:(s + 1) * 64], k_sb[:, (1 - s) * 64:(2 - s) * 64],
                                       rope_tab[:, 3, b, s * 64:(s + 1) * 64], ALU.mult).then_inc(S["ksin"], 1)
                pool.wait_ge(S["k_var"], u.count(1, 1))
                if u.back(2):
                    pool.wait_ge(S["krope"], u.count(1, -1))
                pool.tensor_tensor(rstd[:, u.k % 2, REP:REP + 1], var[:, u.k % 2, REP:REP + 1], half_neg[:, 0:1],
                                   ALU.pow).then_inc(S["k_pow"], 1)
                pool.wait_ge(S["q_var"], u.count(1, 1))
                if u.back(2):
                    pool.wait_ge(S["exped"], (u + -2).count(REP, REP))
                    pool.wait_ge(S["biased"], (u + -2).count(REP, REP))
                pool.tensor_tensor(rstd[:, u.k % 2, 0:REP], var[:, u.k % 2, 0:REP], half_neg[:, 0:REP],
                                   ALU.pow).then_inc(S["q_pow"], 1)

            def step(u):
                turn_and_norm(u)
                split_v(u + -1)

            pool.wait_ge(S["const_set"], 1)
            run_steps(pool, step)

        @block.scalar
        def _(act_e):
            def sines():
                act_e.wait_ge(S["ang_ready"], 2)
                for n in range(2):
                    act_e.activation(prep[:, 4 + n, :], prep[:, 2 + n, :], ACT.Sin).then_inc(S["sin_ready"], 1)

            def group_scale(g):
                act_e.wait_ge(S["delta"], g + 1)
                if g:
                    act_e.wait_ge(S["w2_ready"], g)
                act_e.activation(prep[:, 2, :], ring[1][:, :], ACT.Copy).then_inc(S["delta_copied"], 1)
                act_e.wait_ge(S["w2_in"], 32 * (g + 1))
                act_e.activation(prep[:, 1, :], prep[:, 1, :], ACT.Exp).then_inc(S["scale_exp"], 1)

            def split_x(hf):
                act_e.wait_ge(S["xT_in"], 16 * (hf + 1))
                if hf:
                    act_e.wait_ge(S["gate_up"], 2 * FC)
                for c in range(C):
                    act_e.activation(xT_h[:, c, :], xT_raw[:, c, :], ACT.Copy).then_inc(S["xh_set"], 1)

            def split_w(q):
                hf, n = divmod(q, CH)
                act_e.wait_ge(w_in[q % 2], w_count(q))
                if n == 0:
                    if hf:
                        act_e.wait_ge(S["gate_up"], 2 * (hf * FC - 1))
                    for k in range(2):
                        i = act_e.activation(w_h[:, q % 2, k, 0:C, :].rearrange("p c (b r) -> p b c r", b=B),
                                             lora_factors(q % 2)[:, k, :, :, :], ACT.Copy)
                    i.then_inc(S["w_hi"], 1)
                    return
                m = n - 1
                if m == 0:
                    if hf:
                        act_e.wait_ge(S["gate_up"], 2 * hf * FC)
                elif m == 1:
                    act_e.wait_ge(S["t_done"], 2 * hf + 2)
                else:
                    act_e.wait_ge(S["gate_up"], 2 * (hf * FC + m - 1))
                if q == 1:
                    act_e.wait_ge(S["lb_in"], B * 16)
                act_e.activation(w_h[:, q % 2, :, 0:C, :], w_blocks(q % 2), ACT.Copy)
                act_e.activation(w_h[:, q % 2, :, C, :], lb[:, :, m * P:(m + 1) * P], ACT.Copy).then_inc(S["w_hi"], 1)

            def high_t(hf, k):
                act_e.wait_ge(S["t_masked"], 3 * hf + k + 1)
                act_e.activation(tb_h[:, k, :], tb_raw, ACT.Copy).then_inc(S["t_hi"], 1)

            def high_act(n):
                act_e.wait_ge(S["act_f"], n + 1)
                if n == FC:
                    act_e.wait_ge(S["down"], HALF)
                act_e.activation(act_h[:, n % FC, :], e_sb[:, n % 2, :], ACT.Copy).then_inc(S["act_hi"], 1)
                if n == 0:
                    act_e.wait_ge(S["lad_in"], 2 * B * 16)
                if n >= 2:
                    act_e.wait_ge(S["lad_used"], n - 1)
                act_e.activation(lad_h[:, n % 2, :].rearrange("p (b r) -> p b r", b=B), lad[:, :, n % FC, :], ACT.Copy
                                 ).then_inc(S["lad_hi"], 1)

            def split_wd(q):
                if q % CH == FC:
                    act_e.wait_ge(S["lbd_in"], 16 * B)
                else:
                    act_e.wait_ge(wd_in[wd_block(q) % 3], 16 * (wd_block(q) // 3 + 1))
                if q >= 2:
                    before, n = divmod(q - 2, CH)
                    if n == FC:
                        act_e.wait_ge(S["down"], HALF * (before + 1))
                    else:
                        act_e.wait_ge(S["wd_used"], before * FC + n + 1)
                act_e.activation(wd_h[:, q % 2, :], wd_source(q), ACT.Copy).then_inc(S["wd_hi"], 1)

            def split_wqkv(u, c):
                if c == 0 and u.back(1):
                    act_e.wait_ge(S["kv_done"], u.count(1, 0))
                act_e.wait_ge(stage_in[c % 2], staged(u, "in", c))
                act_e.activation(wh[:, c, :], stage[:, c % 2, :], ACT.Copy).then_inc(S["wqkv_h"], 1)

            def split_wo(u, h):
                if h == 0 and u.back(1):
                    act_e.wait_ge(S["y"], u.count(1, 0))
                act_e.wait_ge(stage_in[h % 2], staged(u, "out", h))
                act_e.activation(woh[:, h, :], stage[:, h % 2, 0:HID], ACT.Copy).then_inc(S["wo_h"], 1)

            act_e.wait_ge(S["idx_in"], 48)
            act_e.wait_ge(S["zero_set"], 1)
            for b in range(B):
                n = B * NPP + b
                a = act_e.value_load(idx[0:1, n:n + 1], min_val=0, max_val=15)
                act_e.dma_start(lb[b * RANK:(b + 1) * RANK, :, 0:F],
                                ins["BguT"][bass.ds(a, 1), :, :, :].rearrange("a r k f -> (a r) k f")).then_inc(S["lb_in"], 16)
                if b == 3:
                    split_x(0)
            split_w(0)
            split_w(1)
            high_t(0, 0)
            high_t(0, 1)
            sines()
            for hf in range(2):
                for m in range(FC):
                    n = hf * FC + m
                    if m < FC - 1:
                        split_w(hf * CH + m + 2)
                    act_e.wait_ge(S["gate_up"], 2 * n + 1)
                    if n >= 2:
                        act_e.wait_ge(S["act_lo"], n - 1)
                    if m == 0:
                        act_e.wait_ge(S["t_lo"], 3 * hf + 2)
                    if n == 1:
                        act_e.wait_ge(S["key_copied"], 1)
                    e = e_sb[:, n % 2, :]
                    act_e.activation(e, gate_ps[n % 2], ACT.Exp, scale=-1.0).then_inc(S["exp_g"], 1)
                    if m:
                        high_act(n - 1)
                    act_e.wait_ge(S["exp_g"], n + 1)
                    act_e.activation(e, e, ACT.Ln, bias=1.0).then_inc(S["ln_g"], 1)
                    act_e.wait_ge(S["ln_g"], n + 1)
                    act_e.activation(e, e, ACT.Exp, scale=-1.0).then_inc(S["sigmoid"], 1)
                    if m == 3:
                        group_scale(2 * hf)
                high_act(hf * FC + FC - 1)
                split_wd(hf * CH)
                split_wd(hf * CH + 1)
                high_t(hf, 2)
                for k in range(2, CH):
                    split_wd(hf * CH + k)
                    if k == 2:
                        group_scale(2 * hf + 1)
                    if hf and k in (3, 5):
                        split_wqkv(Unit(None, 0), k - 3)
                        split_wqkv(Unit(None, 0), k - 2)
                    if hf and k in (7, 9):
                        split_wo(Unit(None, 0), k - 7)
                        split_wo(Unit(None, 0), k - 6)
                    if hf == 0 and k == 3:
                        split_w(CH)
                        split_x(1)
                    if hf == 0 and k == 7:
                        split_w(CH + 1)
                        high_t(1, 0)
                        high_t(1, 1)

            for b in range(B):
                act_e.wait_ge(S["x1T"], b + 1)
                act_e.activation(xh[:, b, :, :], ring[b % 2][:, :].rearrange("p (c t) -> p c t", c=C),
                                 ACT.Copy).then_inc(S["x1h"], 1)

            def new_wqkv(u, c):
                if u.new_head():
                    split_wqkv(u, c)

            def new_wo(u, h):
                if u.new_head():
                    split_wo(u, h)

            def exp(u, h):
                if not u.exists():
                    return
                act_e.wait_ge(S["biased"], u.count(REP, h + 1))
                if h == 0 and u.back(1):
                    act_e.wait_ge(S["inverted"], u.count(REP, 0))
                act_e.activation(p_sb[:, p_slot(u, h), :], p_sb[:, p_slot(u, h), :], ACT.Exp, bias=bias[:, h:h + 1],
                                 scale=rstd[:, u.k % 2, h:h + 1], accum_out=total[:, h:h + 1]
                                 ).then_inc(S["exped"], 1)

            def normalise(u, h):
                if not u.exists():
                    return
                act_e.wait_ge(S["inverted"], u.count(REP, h + 1))
                act_e.activation(p_sb[:, p_slot(u, h), :], p_sb[:, p_slot(u, h), :], ACT.Copy,
                                 scale=inv[:, h:h + 1]).then_inc(S["normed_s"], 1)

            def high_pt(u, c):
                if not u.exists():
                    return
                act_e.wait_ge(S["pt"], u.count(KC, c + 1))
                if u.back(1):
                    act_e.wait_ge(S["pv"], u.count(KC, c + 1 - KC))
                act_e.activation(pTh[:, c, :], ring[c % 2][:, :], ACT.Copy).then_inc(S["pth"], 1)

            def high_v(u):
                if not u.exists():
                    return
                act_e.wait_ge(v_load, u.count(16, 16))
                if u.back(2):
                    act_e.wait_ge(S["pv"], (u + -2).count(KC, KC))
                act_e.activation(vh[:, u.k % 2, :, :], v_raw[:, :, :], ACT.Copy).then_inc(S["vh_set"], 1)

            def high_o(u):
                if not u.exists():
                    return
                act_e.wait_ge(S["pv"], u.count(KC, KC))
                if u.back(1):
                    act_e.wait_ge(S["y"], u.count(1, 0))
                act_e.activation(oTh[:, :], o_ps[:, :], ACT.Copy).then_inc(S["oh"], 1)

            def copy_q(u):
                if not u.exists():
                    return
                act_e.wait_ge(S["q_done"], u.count(1, 1))
                if u.back(1):
                    act_e.wait_ge(S["qcos"], u.count(1, 0))
                    act_e.wait_ge(S["qsin"], u.count(2, 0))
                act_e.activation(q_sb[:, :], proj_ps[:, :], ACT.Copy).then_inc(S["q_copied"], 1)

            def square_q(u):
                if not u.exists():
                    return
                act_e.wait_ge(S["q_copied"], u.count(1, 1))
                if u.back(1):
                    act_e.wait_ge(S["q_ss"], u.count(1, 0))
                act_e.activation(sq_q[:, :], q_sb[:, :], ACT.Square).then_inc(S["q_sq"], 1)

            def copy_k(u):
                if not u.exists():
                    return
                act_e.wait_ge(S["kv_done"], u.count(1, 1))
                if u.back(1):
                    act_e.wait_ge(S["kcos"], u.count(1, 0))
                    act_e.wait_ge(S["ksin"], u.count(2, 0))
                act_e.activation(k_sb[:, :], proj_ps[:, 0:D], ACT.Copy).then_inc(S["k_copied"], 1)

            def high_new_v(u):
                if not u.exists():
                    return
                act_e.wait_ge(S["kv_done"], u.count(1, 1))
                if u.back(4):
                    act_e.wait_ge(S["pv"], (u + -4).count(KC, KC))
                act_e.activation(vnh[:, u.k % 4, :], proj_ps[:, D:2 * D], ACT.Copy).then_inc(S["vnh_set"], 1)

            def square_k(u):
                if not u.exists():
                    return
                act_e.wait_ge(S["k_copied"], u.count(1, 1))
                if u.back(1):
                    act_e.wait_ge(S["k_ss"], u.count(1, 0))
                act_e.activation(sq_k[:, :], k_sb[:, :], ACT.Square).then_inc(S["k_sq"], 1)

            def slot_free(u):
                if u.back(2):
                    act_e.wait_ge(S["score"], (u + -2).count(REP, REP))

            def high_cached_k(u):
                if not u.exists():
                    return
                slot_free(u)
                act_e.wait_ge(S["kcT"], u.count(1, 1))
                act_e.activation(kTh[:, u.k % 2, 0:L], ring[1][:, :], ACT.Copy).then_inc(S["kch"], 1)

            def high_q(u):
                if not u.exists():
                    return
                slot_free(u)
                act_e.wait_ge(S["qT"], u.count(1, 1))
                act_e.activation(qTh[:, u.k % 2, :], ring[0][:, :], ACT.Copy).then_inc(S["qh"], 1)

            def high_new_k(u):
                if not u.exists():
                    return
                slot_free(u)
                act_e.wait_ge(S["knT"], u.count(1, 1))
                act_e.activation(kTh[:, u.k % 2, L:KEYS], ring[1][:, 0:T], ACT.Copy).then_inc(S["knh"], 1)

            def step(u):
                high_v(u + -2)
                high_o(u + -3)
                exp(u + -2, 1)
                high_q(u + -1)
                new_wqkv(u, 2)
                high_new_k(u + -1)
                exp(u + -2, 2)
                new_wqkv(u, 3)
                new_wo(u + -2, 0)
                exp(u + -2, 3)
                normalise(u + -2, 1)
                normalise(u + -2, 2)
                new_wo(u + -2, 1)
                copy_q(u)
                high_pt(u + -2, 0)
                high_pt(u + -2, 1)
                exp(u + -1, 0)
                copy_k(u)
                high_pt(u + -2, 2)
                high_new_v(u)
                new_wqkv(u + 1, 0)
                square_k(u)
                high_pt(u + -2, 3)
                new_wo(u + -2, 2)
                high_pt(u + -2, 4)
                square_q(u)
                new_wqkv(u + 1, 1)
                high_cached_k(u)
                new_wo(u + -2, 3)
            act_e.wait_ge(S["w2_put"], 16 * C)
            run_steps(act_e, step)

            def high_w3(b):
                act_e.wait_ge(w3_load[b % 2], 16 * (b // 2 + 1))
                if b < 2:
                    act_e.wait_ge(S["y"], UNITS)
                else:
                    act_e.wait_ge(S["l3_done"], b - 1)
                act_e.activation(w3_h[:, b % 2, :, :], w3_raw[:, b % 2, :, :], ACT.Copy).then_inc(S["w3_hi"], 1)

            def high_x2(b):
                act_e.wait_ge(S["x2T_done"], b + 1)
                if b >= 2:
                    act_e.wait_ge(S["l2_done"], b - 1)
                act_e.activation(x2T_h[:, b % 2, :], ring[0][:, :], ACT.Copy).then_inc(S["x2T_hi"], 1)

            def high_x3(b):
                act_e.wait_ge(S["x3T_done"], b + 1)
                if b >= 2:
                    act_e.wait_ge(S["l3_done"], b - 1)
                act_e.activation(x3T_h[:, b % 2, :], ring[1][:, :], ACT.Copy).then_inc(S["x3T_hi"], 1)

            act_e.wait_ge(S["kv_done"], UNITS)
            act_e.wait_ge(S["w2_loaded"], 16)
            act_e.activation(w2_h[:, :, :], w2_raw[:, :, :], ACT.Copy).then_inc(S["w2_hi"], 1)
            high_x2(0)
            high_w3(0)
            for b in range(B):
                if b + 1 < B:
                    high_x2(b + 1)
                high_x3(b)
                if b + 1 < B:
                    high_w3(b + 1)

        @block.tensor
        def _(pe):
            mm = nc.tensor.matmul
            pe.wait_ge(S["ident_set"], 2)

            def delta(g):
                if g:
                    pe.wait_ge(S["delta_copied"], g)
                else:
                    pe.wait_ge(S["l2_in"], 32)
                mm(ring[1][:, :], l2a[:, g * P:(g + 1) * P], l2b[:, :], start=True, stop=True).then_inc(S["delta"], 1)

            def three(out, parts, start, stop):
                k, last = 0, 3 * len(parts) - 1
                for (a_h, a_l), (b_h, b_l) in parts:
                    for a, b in ((a_h, b_h), (a_h, b_l), (a_l, b_h)):
                        i = mm(out, a, b, start=start and k == 0, stop=stop and k == last)
                        k += 1
                return i

            def lora_in(hf):
                q = hf * CH
                pe.wait_ge(S["w_hi"], q + 1)
                pe.wait_ge(S["w_lo"], q + 1)
                pe.wait_ge(S["xh_set"], C * (hf + 1))
                pe.wait_ge(S["xl_set"], C * (hf + 1))
                for k in range(2):
                    if hf and k == 0:
                        pe.wait_ge(S["t_masked"], 3)
                    if hf and k == 1:
                        pe.wait_ge(S["delta_copied"], 2)
                    three(ring[k][:, :], [((w_h[:, q % 2, k, c, :], w_l[:, q % 2, k, c, :]), (xT_h[:, c, :], xT_l[:, c, :]))
                                          for c in range(C)], True, True).then_inc(S["t_done"], 1)

            def gate_up(n):
                hf, m = divmod(n, FC)
                q = hf * CH + m + 1
                pe.wait_ge(S["w_hi"], q + 1)
                pe.wait_ge(S["w_lo"], q + 1)
                for k, bank in enumerate((gate_ps, up_ps)):
                    if n >= 2:
                        pe.wait_ge(S["act_f"], n - 1)
                    if n == FC + 1:
                        pe.wait_ge(S["x1_added"], HALF)
                    three(bank[n % 2], [((w_h[:, q % 2, k, c, :], w_l[:, q % 2, k, c, :]), (xT_h[:, c, :], xT_l[:, c, :]))
                                        for c in range(C)], True, False)
                    if m == 0:
                        pe.wait_ge(S["t_lo"], 3 * hf + k + 1)
                    three(bank[n % 2], [((w_h[:, q % 2, k, C, :], w_l[:, q % 2, k, C, :]), (tb_h[:, k, :], tb_l[:, k, :]))],
                          False, True).then_inc(S["gate_up"], 1)

            def lora_down(n):
                hf, m = divmod(n, FC)
                pe.wait_ge(S["act_lo"], n + 1)
                pe.wait_ge(S["lad_lo"], n + 1)
                if m == 0:
                    pe.wait_ge(S["t_lo"], 3 * hf + 1)
                i = three(ring[0][:, :], [((lad_h[:, n % 2, :], lad_l[:, n % 2, :]), (act_h[:, m, :], act_l[:, m, :]))],
                          m == 0, m == FC - 1)
                i.then_inc(S["lad_used"], 1)

            def down(hf, k):
                q = hf * CH + k
                pe.wait_ge(S["wd_hi"], q + 1)
                pe.wait_ge(S["wd_lo"], q + 1)
                if k == FC:
                    pe.wait_ge(S["t_lo"], 3 * hf + 3)
                if k == 0:
                    pe.wait_ge(S["act_f"], (hf + 1) * FC)
                if k == 0 and hf:
                    pe.wait_ge(S["x1_added"], HALF)
                for j in range(HALF):
                    ts = slice(j * T, (j + 1) * T)
                    a = (act_h[:, k, ts], act_l[:, k, ts]) if k < FC else (tb_h[:, 2, ts], tb_l[:, 2, ts])
                    i = three(seq_ps[j], [(a, (wd_h[:, q % 2, :], wd_l[:, q % 2, :]))], k == 0, k == FC)
                    if k == FC:
                        i.then_inc(S["down"], 1)
                    elif j == HALF - 1:
                        i.then_inc(S["wd_used"], 1)

            lora_in(0)
            for hf in range(2):
                for m in range(FC):
                    n = hf * FC + m
                    gate_up(n)
                    if m >= 2:
                        lora_down(n - 2)
                    if m == 1:
                        delta(2 * hf)
                lora_down(hf * FC + FC - 2)
                lora_down(hf * FC + FC - 1)
                delta(2 * hf + 1)
                for k in range(CH):
                    down(hf, k)
                    if hf == 0 and k == 7:
                        lora_in(1)
            for b in range(B):
                pe.wait_ge(S["x1_added"], b + 1)
                if b >= 2:
                    pe.wait_ge(S["x1l"], b - 1)
                for c in range(C):
                    i = nc.tensor.transpose(ring[b % 2][:, c * P:(c + 1) * P], x_sb[:, b, c * P:(c + 1) * P], ident[:, :])
                i.then_inc(S["x1T"], 1)

            def project(u, cols, width, name):
                b = u.seq
                if cols == 0 and u.turn is None and u.k < B:
                    pe.wait_ge(S["x1l"], b + 1)
                    pe.wait_ge(S["x1h"], b + 1)
                k = 0
                for c in range(C):
                    if cols == 0 and b == 0:
                        pe.wait_ge(S["wqkv_h"], u.heads(C, c + 1))
                        pe.wait_ge(S["wqkv_l"], u.heads(C, c + 1))
                    for a, w in ((xh, wh), (xh, wl), (xl, wh)):
                        i = mm(proj_ps[:, 0:width], a[:, b, c, :], w[:, c, cols:cols + width], start=k == 0, stop=k == 3 * C - 1)
                        k += 1
                i.then_inc(S[name], 1)

            def project_q(u):
                if not u.exists():
                    return
                if u.back(3):
                    pe.wait_ge(S["y_added"], (u + -3).count(1, 1))
                elif u.k >= 1:
                    pe.wait_ge(S["k_copied"], u.count(1, 0))
                    pe.wait_ge(S["vnl_set"], u.count(1, 0))
                else:
                    pe.wait_ge(S["x1_added"], B)
                project(u, 0, QW, "q_done")

            def project_kv(u):
                if not u.exists():
                    return
                pe.wait_ge(S["q_copied"], u.count(1, 1))
                project(u, QW, 2 * D, "kv_done")

            def scores(u, h):
                if not u.exists():
                    return
                hs = slice(h * D, (h + 1) * D)
                par = u.k % 2
                if h == 0:
                    for name in ("qh", "ql", "kch", "kcl", "knh", "knl"):
                        pe.wait_ge(S[name], u.count(1, 1))
                if h >= 2 or u.back(1):
                    pe.wait_ge(S["topped"], u.count(REP, h - 1))
                for s in range(2):
                    ks = slice(s * SPLIT, (s + 1) * SPLIT)
                    for k, (a, w) in enumerate(((qTh, kTh), (qTh, kTl), (qTl, kTh))):
                        i = mm(score_ps[h % 2][:, s, 0:SPLIT], a[:, par, hs], w[:, par, ks], start=k == 0, stop=k == 2)
                i.then_inc(S["score"], 1)

            def transpose_p(u, c):
                if not u.exists():
                    return
                if c == 0:
                    pe.wait_ge(S["normed_v"], u.count(2, 2))
                    pe.wait_ge(S["normed_s"], u.count(2, 2))
                    if (u + 1).exists():
                        pe.wait_ge(S["ql"], (u + 1).count(1, 1))
                elif c == 1:
                    if (u + 1).exists():
                        pe.wait_ge(S["knl"], (u + 1).count(1, 1))
                else:
                    pe.wait_ge(S["ptl"], u.count(KC, c - 1))
                for h in range(REP):
                    i = nc.tensor.transpose(ring[c % 2][:, h * P:(h + 1) * P], p_sb[:, p_slot(u, h), c * P:(c + 1) * P], ident[:, :])
                i.then_inc(S["pt"], 1)

            def attend(u, c):
                if not u.exists():
                    return
                pe.wait_ge(S["ptl"], u.count(KC, c + 1))
                if c == 0:
                    pe.wait_ge(S["vl_set"], u.count(1, 1))
                    pe.wait_ge(S["vnl_set"], u.count(1, 1))
                    if u.back(1):
                        pe.wait_ge(S["ol"], u.count(1, 0))
                if c < LC:
                    high, low = vh[:, u.k % 2, c, :], vl[:, u.k % 2, c, :]
                else:
                    high, low = vnh[:, u.k % 4, :], vnl[:, u.k % 4, :]
                for k, (a, w) in enumerate(((high, pTh), (high, pTl), (low, pTh))):
                    i = mm(o_ps[:, :], a, w[:, c, :], start=c == 0 and k == 0, stop=c == KC - 1 and k == 2)
                i.then_inc(S["pv"], 1)

            def output(u):
                if not u.exists():
                    return
                pe.wait_ge(S["oh"], u.count(1, 1))
                pe.wait_ge(S["ol"], u.count(1, 1))
                if (u + 2).exists():
                    pe.wait_ge(S["k_copied"], (u + 2).count(1, 1))
                    pe.wait_ge(S["vnl_set"], (u + 2).count(1, 1))
                else:
                    pe.wait_ge(S["y_added"], u.count(1, 0))
                k = 0
                for h in range(REP):
                    if u.seq == 0:
                        pe.wait_ge(S["wo_h"], u.heads(REP, h + 1))
                        pe.wait_ge(S["wo_l"], u.heads(REP, h + 1))
                    hs = slice(h * D, (h + 1) * D)
                    for a, w in ((oTh, woh), (oTh, wol), (oTl, woh)):
                        i = mm(proj_ps[:, :], a[:, hs], w[:, h, :], start=k == 0, stop=k == 3 * REP - 1)
                        k += 1
                i.then_inc(S["y"], 1)

            def transpose_keys(u):
                if not u.exists():
                    return
                pe.wait_ge(k_load, u.count(16, 16))
                if u.back(2):
                    pe.wait_ge(S["ptl"], (u + -2).count(KC, 4))
                elif u.k == 0:
                    pe.wait_ge(S["x1l"], B)
                else:
                    pe.wait_ge(S["knl"], u.count(1, 0))
                for c in range(LC):
                    i = nc.tensor.transpose(ring[1][:, c * P:(c + 1) * P], k_raw[:, c, :], ident[:, :])
                i.then_inc(S["kcT"], 1)

            def transpose_queries(u):
                if not u.exists():
                    return
                pe.wait_ge(S["qrope"], u.count(1, 1))
                if u.back(2):
                    pe.wait_ge(S["ptl"], (u + -2).count(KC, 5))
                elif u.k == 1:
                    pe.wait_ge(S["ql"], 1)
                for h in range(REP):
                    i = nc.tensor.transpose(ring[0][:, h * P:(h + 1) * P], q_cos[:, h * P:(h + 1) * P], ident[:, :])
                i.then_inc(S["qT"], 1)

            def transpose_new(u):
                if not u.exists():
                    return
                pe.wait_ge(S["krope"], u.count(1, 1))
                pe.wait_ge(S["kcl"], u.count(1, 1))
                nc.tensor.transpose(ring[1][:, 0:P], k_cos[:, :], ident[:, :]).then_inc(S["knT"], 1)

            def step(u):
                project_q(u)
                transpose_p(u + -2, 0)
                transpose_p(u + -2, 1)
                project_kv(u)
                transpose_p(u + -2, 2)
                attend(u + -2, 0)
                transpose_p(u + -2, 3)
                attend(u + -2, 1)
                transpose_p(u + -2, 4)
                attend(u + -2, 2)
                transpose_keys(u)
                attend(u + -2, 3)
                attend(u + -2, 4)
                scores(u + -1, 2)
                transpose_queries(u)
                scores(u + -1, 3)
                transpose_new(u)
                output(u + -2)
                scores(u, 0)
                scores(u, 1)

            run_steps(pe, step)

            def layer3(b):
                pe.wait_ge(S["x3T_lo"], b + 1)
                pe.wait_ge(S["w3_lo"], b + 1)
                if b >= 1:
                    pe.wait_ge(S["x4_added"], b)
                three(down_ps[1], [((x3T_h[:, b % 2, c * T:(c + 1) * T], x3T_l[:, b % 2, c * T:(c + 1) * T]),
                                    (w3_h[:, b % 2, c, :], w3_l[:, b % 2, c, :])) for c in range(C)], True, True
                      ).then_inc(S["l3_done"], 1)

            def layer2(b):
                pe.wait_ge(S["x2T_lo"], b + 1)
                if b == 0:
                    pe.wait_ge(S["w2_lo"], 1)
                else:
                    pe.wait_ge(S["x3_added"], b)
                three(down_ps[0], [((x2T_h[:, b % 2, c * T:(c + 1) * T], x2T_l[:, b % 2, c * T:(c + 1) * T]),
                                    (w2_h[:, c, :], w2_l[:, c, :])) for c in range(C)], True, True
                      ).then_inc(S["l2_done"], 1)

            def turn_x(b, slot, name):
                for c in range(C):
                    i = nc.tensor.transpose(ring[slot][:, c * P:(c + 1) * P], x_sb[:, b, c * P:(c + 1) * P], ident[:, :])
                i.then_inc(S[name], 1)

            pe.wait_ge(S["ptl"], UNITS * KC)
            pe.wait_ge(S["y_added"], UNITS - B + 1)
            turn_x(0, 0, "x2T_done")
            pe.wait_ge(S["y_added"], UNITS)
            for b in range(B):
                layer2(b)
                if b + 1 < B:
                    turn_x(b + 1, 0, "x2T_done")
                if b:
                    layer3(b - 1)
                pe.wait_ge(S["x3_added"], b + 1)
                turn_x(b, 1, "x3T_done")
            layer3(B - 1)

        @block.vector
        def _(dve):
            v = nc.vector
            chain = [0]

            def then(ins):
                chain[0] += 1
                ins.then_inc(S["step_done"], 1)
                dve.wait_ge(S["step_done"], chain[0])

            lens = small[:, 16:24]
            pos = small[:, 24:32]
            ang, turns = prep[:, 0, :], prep[:, 1, :]
            dve.wait_ge(S["len_in"], 16)
            dve.wait_ge(S["iota_set"], 2)
            dve.wait_ge(S["nw_in"], 48)
            v.tensor_copy(lens, len_i[:, :])
            then(v.tensor_copy(pos, pos_i[:, :]))
            then(v.tensor_tensor(pos, pos, lens, ALU.add))
            for b in range(B):
                i = v.tensor_scalar(ang[:, b * 64:(b + 1) * 64], nw[:, 2, 0:64], pos[:, b:b + 1], None, ALU.mult)
            then(i)
            def reduce_angles(n):
                quarter = 0.25 * n
                red = prep[:, 2 + n, :]
                then(v.tensor_scalar(turns, ang, 1.0 / TWO_PI, quarter, ALU.mult, ALU.add))
                then(v.tensor_scalar(turns, turns, ROUND, None, ALU.add))
                then(v.tensor_scalar(turns, turns, ROUND, None, ALU.subtract))
                then(v.scalar_tensor_tensor(red, turns, -PI_A, ang, ALU.mult, ALU.add))
                then(v.scalar_tensor_tensor(red, turns, -PI_B, red, ALU.mult, ALU.add))
                then(v.scalar_tensor_tensor(red, turns, -PI_C, red, ALU.mult, ALU.add))
                then(v.tensor_scalar(red, red, quarter * TWO_PI, PI_IN, ALU.add, ALU.min))
                v.tensor_scalar(red, red, -PI_IN, None, ALU.max).then_inc(S["ang_ready"], 1)

            def split_x(hf):
                for c in range(C):
                    dve.wait_ge(S["xh_set"], C * hf + c + 1)
                    v.tensor_tensor(xT_l[:, c, :], xT_raw[:, c, :], xT_h[:, c, :].bitcast(F32), ALU.subtract
                                    ).then_inc(S["xl_set"], 1)

            def split_w(q):
                hf, n = divmod(q, CH)
                dve.wait_ge(S["w_hi"], q + 1)
                if n == 0:
                    for k in range(2):
                        i = v.tensor_tensor(w_l[:, q % 2, k, 0:C, :].rearrange("p c (b r) -> p b c r", b=B),
                                            lora_factors(q % 2)[:, k, :, :, :],
                                            w_h[:, q % 2, k, 0:C, :].rearrange("p c (b r) -> p b c r", b=B).bitcast(F32),
                                            ALU.subtract)
                    i.then_inc(S["w_lo"], 1)
                    return
                m = n - 1
                v.tensor_tensor(w_l[:, q % 2, :, C, :], lb[:, :, m * P:(m + 1) * P], w_h[:, q % 2, :, C, :].bitcast(F32),
                                ALU.subtract)
                v.tensor_tensor(w_l[:, q % 2, :, 0:C, :], w_blocks(q % 2), w_h[:, q % 2, :, 0:C, :].bitcast(F32),
                                ALU.subtract).then_inc(S["w_lo"], 1)
                if m == FC - 3:
                    dve.wait_ge(S["w_lo"], q + 1)
                    v.memset(w_blocks(q % 2)[:, :, :, FTAIL:], 0.0).then_inc(S["w_zero"], 1)

            def mask_t(hf, k):
                if k < 2:
                    dve.wait_ge(S["t_done"], 2 * hf + k + 1)
                else:
                    dve.wait_ge(S["lad_used"], (hf + 1) * FC)
                    dve.wait_ge(S["act_hi"], (hf + 1) * FC)
                if k == 1:
                    dve.wait_ge(S["t_lo"], 3 * hf + 1)
                v.tensor_tensor(tb_raw, ring[k % 2][:, :], blk[:, hf * HT:(hf + 1) * HT], ALU.mult
                                ).then_inc(S["t_masked"], 1)
                dve.wait_ge(S["t_hi"], 3 * hf + k + 1)
                v.tensor_tensor(tb_l[:, k, :], tb_raw, tb_h[:, k, :].bitcast(F32), ALU.subtract).then_inc(S["t_lo"], 1)

            def split_wd(q):
                dve.wait_ge(S["wd_hi"], q + 1)
                v.tensor_tensor(wd_l[:, q % 2, :], wd_source(q), wd_h[:, q % 2, :].bitcast(F32), ALU.subtract
                                ).then_inc(S["wd_lo"], 1)
                if q % CH == FC - 4:
                    dve.wait_ge(S["wd_lo"], q + 1)
                    v.memset(wd_raw[FTAIL:, wd_block(q) % 3, :], 0.0).then_inc(S["wd_zero"], 1)

            split_x(0)
            split_w(0)
            reduce_angles(0)
            reduce_angles(1)
            split_w(1)
            dve.wait_ge(S["blk_set"], 3)
            mask_t(0, 0)
            mask_t(0, 1)
            key = prep[:, 6, :]
            v.tensor_copy(key, key_i).then_inc(S["key_copied"], 1)

            def masks():
                dve.wait_ge(S["key_copied"], 1)
                then(v.tensor_scalar(nw[:, 0, :], nw[:, 0, :], SCALE, None, ALU.mult))
                v.memset(mask[:, :, L:KEYS], 0.0)
                for b in range(B):
                    i = v.tensor_scalar(mask[:, b, 0:L], key, lens[:, b:b + 1], NEG, ALU.is_ge, ALU.mult)
                i.then_inc(S["mask_ready"], 1)

            def rotary_tables():
                sin = prep[:, 4, :].rearrange("p (b j) -> p b j", b=B)
                cos = prep[:, 5, :].rearrange("p (b j) -> p b j", b=B)
                dve.wait_ge(S["sin_ready"], 2)

                def wide(n, s):
                    return nw[:, n, s * 64:(s + 1) * 64].unsqueeze(1).to_broadcast([P, B, 64])

                for n in range(2):
                    v.tensor_tensor(rope_tab[:, 2 * n, :, 0:64], cos, wide(n, 0), ALU.mult)
                    v.tensor_tensor(rope_tab[:, 2 * n, :, 64:128], cos, wide(n, 1), ALU.mult).then_inc(S["rope_ready"], 1)
                    v.tensor_tensor(rope_tab[:, 2 * n + 1, :, 64:128], sin, wide(n, 0), ALU.mult)
                    v.scalar_tensor_tensor(rope_tab[:, 2 * n + 1, :, 0:64], sin, -1.0, wide(n, 1),
                                           ALU.mult, ALU.mult).then_inc(S["rope_ready"], 1)


            code, cmax, thr = small[:, 0:NCODE], small[:, 33:34], small[:, 8:8 + NCODE - 1]

            def codebook():
                dve.wait_ge(S["code_in"], 16)
                then(v.tensor_reduce(cmax, code, AX_X, ALU.max, apply_absolute_value=True))
                then(v.tensor_scalar(cmax, cmax, 1e-8, None, ALU.max))
                then(v.reciprocal(cmax, cmax))
                then(v.tensor_scalar(code, code, cmax, None, ALU.mult))
                then(v.tensor_tensor(thr, small[:, 0:NCODE - 1], small[:, 1:NCODE], ALU.add))
                then(v.tensor_scalar(thr, thr, 0.5, None, ALU.mult))

            def weight2(g, part):
                w, scale, delta, tmp, norm = (prep[:, n, :] for n in range(5))
                leaf = [prep[:, 5 + n, :] for n in range(4)]
                if part == 0:
                    dve.wait_ge(S["delta_copied"], g + 1)
                    dve.wait_ge(S["scale_exp"], g + 1)
                    then(v.tensor_scalar(delta, delta, 0.5, None, ALU.mult))
                    then(v.tensor_tensor(w, w, delta, ALU.add))
                    then(v.reciprocal(tmp, scale))
                elif part == 1:
                    then(v.tensor_tensor(norm, w, tmp, ALU.mult))
                if part == 1 or part == 2:
                    for n in (2 * part - 2, 2 * part - 1):
                        t = thr[:, 2 * n:2 * n + 1]
                        v.tensor_scalar(leaf[n], norm, t, code[:, 2 * n + 1:2 * n + 2], ALU.is_gt, ALU.mult)
                        then(v.tensor_scalar(tmp, norm, t, code[:, 2 * n:2 * n + 1], ALU.is_le, ALU.mult))
                        then(v.tensor_tensor(leaf[n], leaf[n], tmp, ALU.add))
                elif part == 3:
                    for t, low, high in ((1, 0, 1), (5, 2, 3), (3, 0, 2)):
                        then(v.tensor_scalar(tmp, norm, thr[:, t:t + 1], None, ALU.is_gt))
                        then(v.copy_predicated(leaf[low], tmp.bitcast(I32), leaf[high]))
                elif part == 4:
                    then(v.tensor_tensor(tmp, leaf[0], norm, ALU.subtract))
                    then(v.tensor_tensor(tmp, tmp, norm, ALU.add))
                    then(v.tensor_tensor(tmp, tmp, scale, ALU.mult))
                    v.tensor_tensor(w, tmp, delta, ALU.add).then_inc(S["w2_ready"], 1)

            def low_act(n):
                dve.wait_ge(S["act_hi"], n + 1)
                v.tensor_tensor(act_l[:, n % FC, :], e_sb[:, n % 2, :], act_h[:, n % FC, :].bitcast(F32), ALU.subtract
                                ).then_inc(S["act_lo"], 1)
                dve.wait_ge(S["lad_hi"], n + 1)
                v.tensor_tensor(lad_l[:, n % 2, :].rearrange("p (b r) -> p b r", b=B), lad[:, :, n % FC, :],
                                lad_h[:, n % 2, :].rearrange("p (b r) -> p b r", b=B).bitcast(F32), ALU.subtract
                                ).then_inc(S["lad_lo"], 1)

            def split_wqkv(u, c):
                dve.wait_ge(S["wqkv_h"], u.heads(C, c + 1))
                v.tensor_tensor(wl[:, c, :], stage[:, c % 2, :], wh[:, c, :].bitcast(F32), ALU.subtract
                                ).then_inc(S["wqkv_l"], 1)

            def split_wo(u, h):
                dve.wait_ge(S["wo_h"], u.heads(REP, h + 1))
                v.tensor_tensor(wol[:, h, :], stage[:, h % 2, 0:HID], woh[:, h, :].bitcast(F32), ALU.subtract
                                ).then_inc(S["wo_l"], 1)

            for hf in range(2):
                for m in range(FC):
                    n = hf * FC + m
                    if m < FC - 1:
                        split_w(hf * CH + m + 2)
                    if m:
                        low_act(n - 1)
                    e = e_sb[:, n % 2, :]
                    dve.wait_ge(S["sigmoid"], n + 1)
                    v.tensor_tensor(e, gate_ps[n % 2], e, ALU.mult).then_inc(S["gated"], 1)
                    dve.wait_ge(S["gated"], n + 1)
                    dve.wait_ge(S["gate_up"], 2 * n + 2)
                    v.tensor_tensor(e, up_ps[n % 2], e, ALU.mult).then_inc(S["act_f"], 1)
                    if n == 0:
                        masks()
                    elif n == 1:
                        rotary_tables()
                    elif n == 2:
                        codebook()
                    if 4 <= m < 9:
                        weight2(2 * hf, m - 4)
                low_act(hf * FC + FC - 1)
                split_wd(hf * CH)
                split_wd(hf * CH + 1)
                mask_t(hf, 2)
                for k in range(2, CH):
                    split_wd(hf * CH + k)
                    if hf and k in (3, 5):
                        split_wqkv(Unit(None, 0), k - 3)
                        split_wqkv(Unit(None, 0), k - 2)
                    if hf and k in (7, 9):
                        split_wo(Unit(None, 0), k - 7)
                        split_wo(Unit(None, 0), k - 6)
                    if k % 2 == 0 and k < 11:
                        weight2(2 * hf + 1, k // 2 - 1)
                    if hf == 0 and k == 3:
                        split_w(CH)
                        split_x(1)
                    if hf == 0 and k == 7:
                        split_w(CH + 1)
                        mask_t(1, 0)
                        mask_t(1, 1)
                dve.wait_ge(x_in[hf], 16)
                for j in range(HALF):
                    b = hf * HALF + j
                    dve.wait_ge(S["down"], b + 1)
                    v.tensor_tensor(x_sb[:, b, :], x_sb[:, b, :], seq_ps[j], ALU.add).then_inc(S["x1_added"], 1)

            for b in range(B):
                dve.wait_ge(S["x1h"], b + 1)
                v.tensor_tensor(xl[:, b, :, :], ring[b % 2][:, :].rearrange("p (c t) -> p c t", c=C),
                                xh[:, b, :, :].bitcast(F32), ALU.subtract).then_inc(S["x1l"], 1)

            def new_wqkv(u, c):
                if u.new_head():
                    split_wqkv(u, c)

            def new_wo(u, h):
                if u.new_head():
                    split_wo(u, h)

            def mask_max(u, h):
                if not u.exists():
                    return
                dve.wait_ge(S["score"], u.count(REP, h + 1))
                ago = 2 if h < 2 else 1
                if u.back(ago):
                    dve.wait_ge(S["pt"], (u + -ago).count(KC, KC))
                dve.sem_inc(S["max_begun"], 1)
                v.tensor_tensor_reduce(out=p_sb[:, p_slot(u, h), :].rearrange("p (s k) -> p s k", s=2),
                                       in0=score_ps[h % 2][:, :, 0:SPLIT],
                                       in1=mask[:, u.seq, :].rearrange("p (s k) -> p s k", s=2),
                                       scale=1.0, scalar=LOWEST, op0=ALU.add, op1=ALU.max,
                                       accum_out=top[:, h:h + 1]).then_inc(S["topped"], 1)
                dve.wait_ge(S["topped"], u.count(REP, h + 1))
                if h == 0:
                    dve.wait_ge(S["q_pow"], u.count(1, 1))
                if u.back(1):
                    dve.wait_ge(S["exped"], u.count(REP, h + 1 - REP))
                v.tensor_scalar(bias[:, h:h + 1], top[:, h:h + 1], rstd[:, u.k % 2, h:h + 1], -1.0,
                                ALU.mult, ALU.mult).then_inc(S["biased"], 1)

            def invert(u, h):
                if not u.exists():
                    return
                dve.wait_ge(S["exped"], u.count(REP, h + 1))
                if (h == 1 or h == 2) and u.back(1):
                    dve.wait_ge(S["normed_s"], u.count(2, h - 2))
                v.reciprocal(inv[:, h:h + 1], total[:, h:h + 1]).then_inc(S["inverted"], 1)

            def normalise(u, h):
                if not u.exists():
                    return
                dve.wait_ge(S["inverted"], u.count(REP, h + 1))
                v.tensor_scalar(p_sb[:, p_slot(u, h), :], p_sb[:, p_slot(u, h), :], inv[:, h:h + 1], None, ALU.mult
                                ).then_inc(S["normed_v"], 1)

            def low_pt(u, c):
                if not u.exists():
                    return
                dve.wait_ge(S["pth"], u.count(KC, c + 1))
                v.tensor_tensor(pTl[:, c, :], ring[c % 2][:, :], pTh[:, c, :].bitcast(F32), ALU.subtract
                                ).then_inc(S["ptl"], 1)

            def low_o(u):
                if not u.exists():
                    return
                dve.wait_ge(S["oh"], u.count(1, 1))
                v.tensor_tensor(oTl[:, :], o_ps[:, :], oTh[:, :].bitcast(F32), ALU.subtract).then_inc(S["ol"], 1)

            def add_y(u):
                if not u.exists():
                    return
                dve.wait_ge(S["y"], u.count(1, 1))
                v.tensor_tensor(x_sb[:, u.seq, :], x_sb[:, u.seq, :], proj_ps[:, :], ALU.add).then_inc(S["y_added"], 1)

            def cos_q(u):
                if not u.exists():
                    return
                dve.wait_ge(S["q_copied"], u.count(1, 1))
                if u.back(1):
                    dve.wait_ge(S["qT"], u.count(1, 0))
                v.tensor_tensor(q_cos[:, :].rearrange("p (h d) -> p h d", h=REP),
                                q_sb[:, :].rearrange("p (h d) -> p h d", h=REP),
                                rope_tab[:, 0, u.seq, :].unsqueeze(1).to_broadcast([P, REP, D]),
                                ALU.mult).then_inc(S["qcos"], 1)

            def mean_square_q(u):
                if not u.exists():
                    return
                par = u.k % 2
                dve.wait_ge(S["q_sq"], u.count(1, 1))
                if u.back(2):
                    dve.wait_ge(S["q_pow"], u.count(1, -1))
                v.tensor_reduce(var[:, par, 0:REP], sq_q[:, :].rearrange("p (h d) -> p h d", h=REP), AX_X, ALU.add
                                ).then_inc(S["q_ss"], 1)
                dve.wait_ge(S["q_ss"], u.count(1, 1))
                v.tensor_scalar(var[:, par, 0:REP], var[:, par, 0:REP], 1.0 / D, EPS, ALU.mult, ALU.add
                                ).then_inc(S["q_var"], 1)

            def low_cached_k(u):
                if not u.exists():
                    return
                dve.wait_ge(S["kch"], u.count(1, 1))
                v.tensor_tensor(kTl[:, u.k % 2, 0:L], ring[1][:, :], kTh[:, u.k % 2, 0:L].bitcast(F32), ALU.subtract
                                ).then_inc(S["kcl"], 1)

            def cos_k(u):
                if not u.exists():
                    return
                dve.wait_ge(S["k_copied"], u.count(1, 1))
                if u.back(1):
                    dve.wait_ge(S["knT"], u.count(1, 0))
                v.tensor_tensor(k_cos[:, :], k_sb[:, :], rope_tab[:, 2, u.seq, :], ALU.mult).then_inc(S["kcos"], 1)

            def mean_square_k(u):
                if not u.exists():
                    return
                par = u.k % 2
                dve.wait_ge(S["k_sq"], u.count(1, 1))
                if u.back(2):
                    dve.wait_ge(S["k_pow"], u.count(1, -1))
                v.tensor_reduce(var[:, par, REP:REP + 1], sq_k[:, :], AX_X, ALU.add).then_inc(S["k_ss"], 1)
                dve.wait_ge(S["k_ss"], u.count(1, 1))
                v.tensor_scalar(var[:, par, REP:REP + 1], var[:, par, REP:REP + 1], 1.0 / D, EPS, ALU.mult, ALU.add
                                ).then_inc(S["k_var"], 1)

            def low_new_v(u):
                if not u.exists():
                    return
                dve.wait_ge(S["vnh_set"], u.count(1, 1))
                v.tensor_tensor(vnl[:, u.k % 4, :], proj_ps[:, D:2 * D], vnh[:, u.k % 4, :].bitcast(F32), ALU.subtract
                                ).then_inc(S["vnl_set"], 1)

            def sum_k(u):
                if not u.exists():
                    return
                dve.wait_ge(S["ksin"], u.count(2, 2))
                dve.wait_ge(S["kcos"], u.count(1, 1))
                v.tensor_tensor(k_cos[:, :], k_cos[:, :], k_sin[:, :], ALU.add).then_inc(S["ksum"], 1)

            def scale_k(u):
                if not u.exists():
                    return
                dve.wait_ge(S["ksum"], u.count(1, 1))
                dve.wait_ge(S["k_pow"], u.count(1, 1))
                v.tensor_scalar(k_cos[:, :], k_cos[:, :], rstd[:, u.k % 2, REP:REP + 1], None, ALU.mult
                                ).then_inc(S["krope"], 1)

            def low_q(u):
                if not u.exists():
                    return
                dve.wait_ge(S["qh"], u.count(1, 1))
                v.tensor_tensor(qTl[:, u.k % 2, :], ring[0][:, :], qTh[:, u.k % 2, :].bitcast(F32), ALU.subtract
                                ).then_inc(S["ql"], 1)

            def low_new_k(u):
                if not u.exists():
                    return
                dve.wait_ge(S["knh"], u.count(1, 1))
                v.tensor_tensor(kTl[:, u.k % 2, L:KEYS], ring[1][:, 0:T], kTh[:, u.k % 2, L:KEYS].bitcast(F32), ALU.subtract
                                ).then_inc(S["knl"], 1)

            def step(u):
                mean_square_q(u + -1)
                invert(u + -2, 2)
                normalise(u + -2, 0)
                invert(u + -2, 3)
                new_wo(u + -2, 0)
                normalise(u + -2, 3)
                mask_max(u + -1, 0)
                new_wo(u + -2, 1)
                mask_max(u + -1, 1)
                low_pt(u + -2, 0)
                low_pt(u + -2, 1)
                cos_q(u)
                cos_k(u)
                low_pt(u + -2, 2)
                invert(u + -1, 0)
                low_new_v(u)
                new_wqkv(u + 1, 0)
                low_pt(u + -2, 3)
                mean_square_k(u)
                low_pt(u + -2, 4)
                sum_k(u)
                new_wqkv(u + 1, 1)
                new_wo(u + -2, 2)
                low_cached_k(u)
                new_wo(u + -2, 3)
                scale_k(u)
                low_o(u + -2)
                mask_max(u + -1, 2)
                low_q(u)
                invert(u + -1, 1)
                low_new_k(u)
                new_wqkv(u + 1, 2)
                mask_max(u + -1, 3)
                add_y(u + -2)
                new_wqkv(u + 1, 3)

            run_steps(dve, step)

            def add3(b):
                dve.wait_ge(S["l2_done"], b + 1)
                v.tensor_tensor(x_sb[:, b, :], x_sb[:, b, :], down_ps[0], ALU.add).then_inc(S["x3_added"], 1)

            def add4(b):
                dve.wait_ge(S["l3_done"], b + 1)
                dve.wait_ge(S["x3_added"], b + 1)
                v.tensor_tensor(x_sb[:, b, :], x_sb[:, b, :], down_ps[1], ALU.add).then_inc(S["x4_added"], 1)

            def low_w3(b):
                dve.wait_ge(S["w3_hi"], b + 1)
                v.tensor_tensor(w3_l[:, b % 2, :, :], w3_raw[:, b % 2, :, :], w3_h[:, b % 2, :, :].bitcast(F32), ALU.subtract
                                ).then_inc(S["w3_lo"], 1)

            def low_x2(b):
                dve.wait_ge(S["x2T_hi"], b + 1)
                v.tensor_tensor(x2T_l[:, b % 2, :], ring[0][:, :], x2T_h[:, b % 2, :].bitcast(F32), ALU.subtract
                                ).then_inc(S["x2T_lo"], 1)

            def low_x3(b):
                dve.wait_ge(S["x3T_hi"], b + 1)
                v.tensor_tensor(x3T_l[:, b % 2, :], ring[1][:, :], x3T_h[:, b % 2, :].bitcast(F32), ALU.subtract
                                ).then_inc(S["x3T_lo"], 1)

            dve.wait_ge(S["y_added"], UNITS)
            dve.wait_ge(S["w2_hi"], 1)
            v.tensor_tensor(w2_l[:, :, :], w2_raw[:, :, :], w2_h[:, :, :].bitcast(F32), ALU.subtract).then_inc(S["w2_lo"], 1)
            low_x2(0)
            low_w3(0)
            for b in range(B):
                add3(b)
                if b + 1 < B:
                    low_x2(b + 1)
                if b:
                    add4(b - 1)
                low_x3(b)
                if b + 1 < B:
                    low_w3(b + 1)
            add4(B - 1)


def kernel(**inputs):
    import numpy as _np
    import concourse.bacc as _bacc
    from concourse import mybir as _mybir
    from concourse.bass_utils import run_bass_kernel_spmd as _run

    g = {k: _np.asarray(v) for k, v in inputs.items()}

    def blocks(w):
        *lead, k, n = w.shape
        return _np.moveaxis(w.reshape(*lead, k // P, P, n), -3, -2)

    def lora_in(a):
        return blocks(a[0].transpose(0, 2, 1))

    whole = (FC - 1) * P
    wgu = _np.stack([blocks(g["L0_cond_W_gate"].T), blocks(g["L0_cond_W_up"].T)], axis=1)
    ad = g["L0_cond_A_down"][0].transpose(0, 2, 1)
    wq = g["L1_cond_Wq"].T.reshape(HID, HK, QW)
    wk = g["L1_cond_Wk"].T.reshape(HID, HK, D)
    wv = g["L1_cond_Wv"].T.reshape(HID, HK, D)
    arrays = {
        "x": g["x"],
        "xT": blocks(g["x"].reshape(B * T, HID).T),
        "pages": g["itok_Bx16_0_63"],
        "ad0": g["itok_B_2_6"],
        "ad3": g["itok_B_3_7"],
        "lens": g["itok_B_207_1644"],
        "code": g["condB_codebook"],
        "inv_freq": _np.float32(1.0) / _np.power(10000.0, _np.arange(0, D, 2) / D).astype(_np.float32),
        "WguT": wgu[..., :whole].reshape(P, 2 * C, FC - 1, P).transpose(2, 0, 1, 3).reshape(FC - 1, P, 2 * C * P),
        "WguTt": wgu[..., whole:].reshape(P, 2 * C, FTAIL),
        "WdT": g["L0_cond_W_down"].T,
        "AguT": _np.stack([lora_in(g["L0_cond_A_gate"]), lora_in(g["L0_cond_A_up"])], axis=2).reshape(-1, P, 2 * C * RANK),
        "BguT": _np.stack([g["L0_cond_B_gate"][0].transpose(0, 2, 1), g["L0_cond_B_up"][0].transpose(0, 2, 1)], axis=2),
        "AdT": blocks(ad[:, :whole]),
        "AdTt": ad[:, whole:],
        "BdT": g["L0_cond_B_down"][0].transpose(0, 2, 1),
        "Wqkv": blocks(_np.concatenate([wq, wk, wv], axis=2).transpose(1, 0, 2)),
        "WoT": g["L1_cond_Wo"].T.reshape(HK, REP, D, HID).transpose(0, 2, 1, 3),
        "qw": g["L1_cond_q_norm_w"],
        "kw": g["L1_cond_k_norm_w"],
        "k_cache": g["L1_cond_k_cache"],
        "v_cache": g["L1_cond_v_cache"],
        "W2T": blocks(g["L2_cond_weight"].T),
        "slT": g["L2_cond_scale_log"][:, :, 0].T,
        "la": g["L2_cond_lora_A"],
        "lbT": g["L2_cond_lora_B"].T,
        "W3T": blocks(g["L3_cond_weight"].transpose(0, 2, 1)),
    }
    arrays = {f"in_{k}": _np.ascontiguousarray(a) for k, a in arrays.items()}
    nc = _bacc.Bacc("TRN2", target_bir_lowering=False, num_devices=1)
    ins = {k[3:]: nc.dram_tensor(k, a.shape, _mybir.dt.from_np(a.dtype), kind="ExternalInput").ap()
           for k, a in arrays.items()}
    out = nc.dram_tensor("out", (B, T, HID), F32, kind="ExternalOutput").ap()
    cond_resid_kernel(nc, ins, out)
    r = _run(nc, [arrays], core_ids=[0])
    return r.results[0]["out"]
```
